# Optimizing a Trainium2 kernel written in Bass

```python
import numpy as np
import jax
import jax.numpy as jnp

def _softmax(x, axis=-1):
    return jax.nn.softmax(x, axis=axis)

def _gelu(x):
    return jax.nn.gelu(x, approximate=True)

def _silu(x):
    return jax.nn.silu(x)

def _sigmoid(x):
    return jax.nn.sigmoid(x)

def _layernorm(x, axis=-1, eps=1e-05):
    m = jnp.mean(x, axis=axis, keepdims=True)
    v = jnp.var(x, axis=axis, keepdims=True)
    return (x - m) / jnp.sqrt(v + eps)

def _scatter_add(tgt, idx, src, axis=0):
    return tgt.at[idx].add(src)

def _segment_sum(src, seg, n):
    return jax.ops.segment_sum(src, seg, n)
kernel_name = 'mk_gps_d2_gnn_r8_571f91'

def setup_inputs(seed: int=0):
    np.random.seed(seed)
    _w = jnp.asarray

    def _rec_inputs():
        import jax
        import jax.numpy as jnp
        _gk = jax.random.key(seed)
        x = -8.776e-05 + 1 * jax.random.normal(jax.random.fold_in(_gk, 1), (6250, 256), jnp.float32)
        _s = jax.random.randint(jax.random.fold_in(_gk, 2), (100000,), 0, 6250, jnp.int32)
        _d = jax.random.randint(jax.random.fold_in(_gk, 3), (100000,), 0, 6250, jnp.int32)
        _loop = jnp.arange(6250, dtype=jnp.int32)
        src = jnp.concatenate([_s, _d, _loop])
        dst = jnp.concatenate([_d, _s, _loop])
        _o = jnp.argsort(dst, stable=True)
        src = src[_o]
        dst = dst[_o]
        return (x, src, dst)
    x, src, dst = _rec_inputs()

    def _L0_gnn_setup():
        import jax, jax.numpy as jnp
        import numpy as np
        N = 2500
        E = 40000
        HID = 256
        HEADS = 8
        HD = HID // HEADS
        key = jax.random.key(seed)
        ks = jax.random.split(key, 12)
        scale = 1.0 / np.sqrt(HID).astype(np.float32)

        def lin_w(k):
            return jax.random.normal(k, (HID, HID), jnp.float32) * scale

        def lin_b(k):
            return jax.random.normal(k, (HID,), jnp.float32) * 0.01
        return {'h': jax.random.normal(ks[0], (N, HID), jnp.float32), 'Wq': lin_w(ks[1]), 'bq': lin_b(ks[2]), 'Wk': lin_w(ks[3]), 'bk': lin_b(ks[4]), 'Wv': lin_w(ks[5]), 'bv': lin_b(ks[6]), 'Wo': lin_w(ks[7]), 'bo': lin_b(ks[8]), 'rows': jax.random.randint(ks[9], (E,), 0, N), 'cols': jax.random.randint(ks[10], (E,), 0, N)}
    _L0_gnn_all = _L0_gnn_setup()
    _L0_gnn_in = {k: v for k, v in _L0_gnn_all.items() if k in ('Wq', 'bq', 'Wk', 'bk', 'Wv', 'bv', 'Wo', 'bo')}
    del _L0_gnn_all

    def _L0_mix_setup():
        import math
        import jax, jax.numpy as jnp
        import numpy as np
        EPS_DIV = 1e-07
        EPS_NORM = 1e-12

        def _l2_normalize(x, axis):
            n = jnp.sqrt(jnp.sum(x * x, axis=axis, keepdims=True))
            return x / jnp.maximum(n, EPS_NORM)
        key = jax.random.key(seed)
        ks = jax.random.split(key, 5)
        b, N, C = (8, 512, 256)
        x = jax.random.normal(ks[0], (b, N, C), dtype=jnp.float32)
        W_qkv = jax.random.normal(ks[1], (C, 3 * C), dtype=jnp.float32) * (1.0 / math.sqrt(C))
        b_qkv = jax.random.normal(ks[2], (3 * C,), dtype=jnp.float32) * 0.02
        W_out = jax.random.normal(ks[3], (C, C), dtype=jnp.float32) * (1.0 / math.sqrt(C))
        b_out = jax.random.normal(ks[4], (C,), dtype=jnp.float32) * 0.02
        return {'x': x, 'W_qkv': W_qkv, 'b_qkv': b_qkv, 'W_out': W_out, 'b_out': b_out}
    _L0_mix_all = _L0_mix_setup()
    _L0_mix_in = {k: v for k, v in _L0_mix_all.items() if k in ('W_qkv', 'b_qkv', 'W_out', 'b_out')}
    del _L0_mix_all

    def _L0_ffn_setup():
        import jax, jax.numpy as jnp
        import numpy as np
        C = 256
        HID = 1024
        E = 8
        TEMP = 1.0
        key = jax.random.key(seed)
        ks = jax.random.split(key, 7)
        x = jax.random.normal(ks[0], (8, 2048, C), dtype=jnp.float32)
        W1 = jax.random.normal(ks[1], (C, HID), dtype=jnp.float32) * 0.02
        b1 = jnp.zeros((HID,), dtype=jnp.float32)
        Wg = jax.random.normal(ks[2], (HID, E), dtype=jnp.float32) * 0.02
        bg = jnp.zeros((E,), dtype=jnp.float32)
        Wd = jax.random.normal(ks[3], (E, HID, C), dtype=jnp.float32) * 0.02
        bd = jnp.zeros((E, C), dtype=jnp.float32)
        return {'x': x, 'W1': W1, 'b1': b1, 'Wg': Wg, 'bg': bg, 'Wd': Wd, 'bd': bd}
    _L0_ffn_all = _L0_ffn_setup()
    _L0_ffn_in = {k: v for k, v in _L0_ffn_all.items() if k in ('W1', 'b1', 'Wg', 'bg', 'Wd', 'bd')}
    del _L0_ffn_all

    def _L1_gnn_setup():
        import jax, jax.numpy as jnp
        import numpy as np
        N_NODES = 6250
        N_EDGES = 100000
        D_IN = 256
        D_OUT = 256
        key = jax.random.key(seed)
        k1, k2, k3, k4, k5, k6 = jax.random.split(key, 6)
        nodes = jax.random.normal(k1, (N_NODES, D_IN), dtype=jnp.float32)
        senders = jax.random.randint(k2, (N_EDGES,), 0, N_NODES, dtype=jnp.int32)
        receivers = jax.random.randint(k3, (N_EDGES,), 0, N_NODES, dtype=jnp.int32)
        W_left = jax.random.normal(k4, (2 * D_IN, D_OUT), dtype=jnp.float32) / np.sqrt(2 * D_IN)
        b_left = jnp.zeros((D_OUT,), dtype=jnp.float32)
        W_right = jax.random.normal(k5, (D_IN, D_OUT), dtype=jnp.float32) / np.sqrt(D_IN)
        return {'nodes': nodes, 'senders': senders, 'receivers': receivers, 'W_left': W_left, 'b_left': b_left, 'W_right': W_right}
    _L1_gnn_all = _L1_gnn_setup()
    _L1_gnn_in = {k: v for k, v in _L1_gnn_all.items() if k in ('W_left', 'b_left', 'W_right')}
    del _L1_gnn_all

    def _L1_mix_setup():
        import jax, jax.numpy as jnp
        import numpy as np
        B, L, D, H = (4, 2048, 256, 8)
        DK = D // H

        def _heads(t):
            b, l, d = t.shape
            return t.reshape(b, l, H, DK).transpose(0, 2, 1, 3)
        key = jax.random.key(seed)
        ks = jax.random.split(key, 9)
        s = 0.02
        return {'x': jax.random.normal(ks[0], (B, L, D), dtype=jnp.float32), 'Wq': jax.random.normal(ks[1], (D, D), dtype=jnp.float32) * s, 'bq': jnp.zeros((D,), dtype=jnp.float32), 'Wk': jax.random.normal(ks[2], (D, D), dtype=jnp.float32) * s, 'bk': jnp.zeros((D,), dtype=jnp.float32), 'Wv': jax.random.normal(ks[3], (D, D), dtype=jnp.float32) * s, 'bv': jnp.zeros((D,), dtype=jnp.float32), 'Wfc': jax.random.normal(ks[4], (D, D), dtype=jnp.float32) * s, 'bfc': jnp.zeros((D,), dtype=jnp.float32)}
    _L1_mix_all = _L1_mix_setup()
    _L1_mix_in = {k: v for k, v in _L1_mix_all.items() if k in ('Wq', 'bq', 'Wk', 'bk', 'Wv', 'bv', 'Wfc', 'bfc')}
    del _L1_mix_all

    def _L1_ffn_setup():
        import jax, jax.numpy as jnp
        import numpy as np
        B, N, D = (16, 512, 256)
        NUM_EXPERTS, TOP_K, HEADS = (4, 2, 4)
        N_EDGES = 131072
        LN_EPS = 1e-05

        def _layernorm(x, g, b):
            mu = x.mean(-1, keepdims=True)
            var = ((x - mu) ** 2).mean(-1, keepdims=True)
            return (x - mu) * jax.lax.rsqrt(var + LN_EPS) * g + b

        def _forward(x, edge_index, W_gat, att_src, att_dst, b_gat, ln_gamma, ln_beta, W1, b1, W2, b2):
            Bc, Nc, Dc = x.shape
            M = Bc * Nc
            x_flat = x.reshape(M, Dc)
            h = (x_flat @ W_gat).reshape(M, HEADS, NUM_EXPERTS)
            loops = jnp.arange(M, dtype=edge_index.dtype)
            src = jnp.concatenate([edge_index[0], loops])
            dst = jnp.concatenate([edge_index[1], loops])
            a_src = (h * att_src).sum(-1)
            a_dst = (h * att_dst).sum(-1)
            e = jax.nn.leaky_relu(a_src[src] + a_dst[dst], negative_slope=0.2)
            e_max = jax.ops.segment_max(e, dst, num_segments=M)
            ee = jnp.exp(e - e_max[dst])
            denom = jax.ops.segment_sum(ee, dst, num_segments=M)
            alpha = ee / (denom[dst] + 1e-16)
            msg = h[src] * alpha[:, :, None]
            agg = jax.ops.segment_sum(msg, dst, num_segments=M).reshape(M, HEADS * NUM_EXPERTS) + b_gat
            scores = _layernorm(agg, ln_gamma, ln_beta).reshape(M, HEADS, NUM_EXPERTS).mean(1)
            scores = scores.reshape(Bc, Nc, NUM_EXPERTS)
            topk_s, topk_i = jax.lax.top_k(scores, TOP_K)
            w = jax.nn.softmax(topk_s, axis=-1)
            out = jnp.zeros_like(x)
            for ei in range(NUM_EXPERTS):
                g = jnp.where(topk_i == ei, w, 0.0).sum(-1)
                hh = jax.nn.gelu(x @ W1[ei] + b1[ei], approximate=False)
                out = out + g[..., None] * (hh @ W2[ei] + b2[ei])
            return out
        key = jax.random.key(seed)
        ks = jax.random.split(key, 8)
        s = 0.05
        return {'x': jax.random.normal(ks[0], (B, N, D), jnp.float32), 'W_gat': jax.random.normal(ks[1], (D, HEADS * NUM_EXPERTS), jnp.float32) * s, 'att_src': jax.random.normal(ks[2], (HEADS, NUM_EXPERTS), jnp.float32) * s, 'att_dst': jax.random.normal(ks[3], (HEADS, NUM_EXPERTS), jnp.float32) * s, 'b_gat': jnp.zeros((HEADS * NUM_EXPERTS,), jnp.float32), 'ln_gamma': jnp.ones((HEADS * NUM_EXPERTS,), jnp.float32), 'ln_beta': jnp.zeros((HEADS * NUM_EXPERTS,), jnp.float32), 'W1': jax.random.normal(ks[4], (NUM_EXPERTS, D, 2 * D), jnp.float32) * s, 'b1': jnp.zeros((NUM_EXPERTS, 2 * D), jnp.float32), 'W2': jax.random.normal(ks[5], (NUM_EXPERTS, 2 * D, D), jnp.float32) * s, 'b2': jnp.zeros((NUM_EXPERTS, D), jnp.float32), 'edge_index': jax.random.randint(ks[6], (2, N_EDGES), 0, B * N, jnp.int32)}
    _L1_ffn_all = _L1_ffn_setup()
    _L1_ffn_in = {k: v for k, v in _L1_ffn_all.items() if k in ('W_gat', 'att_src', 'att_dst', 'b_gat', 'ln_gamma', 'ln_beta', 'W1', 'b1', 'W2', 'b2', 'edge_index')}
    del _L1_ffn_all
    return {'x': x, 'src': src, 'dst': dst, 'L0_gnn_Wq': _L0_gnn_in['Wq'], 'L0_gnn_bq': _L0_gnn_in['bq'], 'L0_gnn_Wk': _L0_gnn_in['Wk'], 'L0_gnn_bk': _L0_gnn_in['bk'], 'L0_gnn_Wv': _L0_gnn_in['Wv'], 'L0_gnn_bv': _L0_gnn_in['bv'], 'L0_gnn_Wo': _L0_gnn_in['Wo'], 'L0_gnn_bo': _L0_gnn_in['bo'], 'L0_mix_W_qkv': _L0_mix_in['W_qkv'], 'L0_mix_b_qkv': _L0_mix_in['b_qkv'], 'L0_mix_W_out': _L0_mix_in['W_out'], 'L0_mix_b_out': _L0_mix_in['b_out'], 'L0_ffn_W1': _L0_ffn_in['W1'], 'L0_ffn_b1': _L0_ffn_in['b1'], 'L0_ffn_Wg': _L0_ffn_in['Wg'], 'L0_ffn_bg': _L0_ffn_in['bg'], 'L0_ffn_Wd': _L0_ffn_in['Wd'], 'L0_ffn_bd': _L0_ffn_in['bd'], 'L1_gnn_W_left': _L1_gnn_in['W_left'], 'L1_gnn_b_left': _L1_gnn_in['b_left'], 'L1_gnn_W_right': _L1_gnn_in['W_right'], 'L1_mix_Wq': _L1_mix_in['Wq'], 'L1_mix_bq': _L1_mix_in['bq'], 'L1_mix_Wk': _L1_mix_in['Wk'], 'L1_mix_bk': _L1_mix_in['bk'], 'L1_mix_Wv': _L1_mix_in['Wv'], 'L1_mix_bv': _L1_mix_in['bv'], 'L1_mix_Wfc': _L1_mix_in['Wfc'], 'L1_mix_bfc': _L1_mix_in['bfc'], 'L1_ffn_W_gat': _L1_ffn_in['W_gat'], 'L1_ffn_att_src': _L1_ffn_in['att_src'], 'L1_ffn_att_dst': _L1_ffn_in['att_dst'], 'L1_ffn_b_gat': _L1_ffn_in['b_gat'], 'L1_ffn_ln_gamma': _L1_ffn_in['ln_gamma'], 'L1_ffn_ln_beta': _L1_ffn_in['ln_beta'], 'L1_ffn_W1': _L1_ffn_in['W1'], 'L1_ffn_b1': _L1_ffn_in['b1'], 'L1_ffn_W2': _L1_ffn_in['W2'], 'L1_ffn_b2': _L1_ffn_in['b2'], 'L1_ffn_edge_index': _L1_ffn_in['edge_index']}

def reference(x, src, dst, L0_gnn_Wq, L0_gnn_bq, L0_gnn_Wk, L0_gnn_bk, L0_gnn_Wv, L0_gnn_bv, L0_gnn_Wo, L0_gnn_bo, L0_mix_W_qkv, L0_mix_b_qkv, L0_mix_W_out, L0_mix_b_out, L0_ffn_W1, L0_ffn_b1, L0_ffn_Wg, L0_ffn_bg, L0_ffn_Wd, L0_ffn_bd, L1_gnn_W_left, L1_gnn_b_left, L1_gnn_W_right, L1_mix_Wq, L1_mix_bq, L1_mix_Wk, L1_mix_bk, L1_mix_Wv, L1_mix_bv, L1_mix_Wfc, L1_mix_bfc, L1_ffn_W_gat, L1_ffn_att_src, L1_ffn_att_dst, L1_ffn_b_gat, L1_ffn_ln_gamma, L1_ffn_ln_beta, L1_ffn_W1, L1_ffn_b1, L1_ffn_W2, L1_ffn_b2, L1_ffn_edge_index):
    import jax
    import jax.numpy as jnp

    def _L0_gnn_ref(h, Wq, bq, Wk, bk, Wv, bv, Wo, bo, rows, cols):
        import jax, jax.numpy as jnp
        import numpy as np
        N = 2500
        E = 40000
        HID = 256
        HEADS = 8
        HD = HID // HEADS
        n = h.shape[0]
        scaling = HD ** (-0.5)
        q = (h @ Wq + bq).reshape(n, HD, HEADS) * scaling
        k = (h @ Wk + bk).reshape(n, HD, HEADS)
        v = (h @ Wv + bv).reshape(n, HD, HEADS)
        s = jnp.einsum('edh,edh->eh', q[rows], k[cols])
        m = jax.ops.segment_max(s, rows, num_segments=n)
        e = jnp.exp(s - m[rows])
        z = jax.ops.segment_sum(e, rows, num_segments=n)
        attn = e / z[rows]
        out = jax.ops.segment_sum(attn[:, None, :] * v[cols], rows, num_segments=n)
        return out.reshape(n, -1) @ Wo + bo

    def _L0_mix_ref(x, W_qkv, b_qkv, W_out, b_out):
        import math
        import jax, jax.numpy as jnp
        import numpy as np
        EPS_DIV = 1e-07
        EPS_NORM = 1e-12

        def _l2_normalize(x, axis):
            n = jnp.sqrt(jnp.sum(x * x, axis=axis, keepdims=True))
            return x / jnp.maximum(n, EPS_NORM)
        b, N, C = x.shape
        qkv = x @ W_qkv + b_qkv
        q, k, v = jnp.split(qkv, 3, axis=2)
        q = q - jnp.mean(q, axis=2, keepdims=True)
        k = k - jnp.mean(k, axis=2, keepdims=True)
        q2 = q * q
        k2 = k * k
        q2s = jnp.sum(q2, axis=2, keepdims=True)
        k2s = jnp.sum(k2, axis=2, keepdims=True)
        k2 = _l2_normalize(k2 / (k2s + EPS_DIV), axis=-2)
        q2 = _l2_normalize(q2 / (q2s + EPS_DIV), axis=-1)
        kv = jnp.einsum('bnc,bnd->bcd', k2, v)
        t2 = jnp.einsum('bnc,bcd->bnd', q2, kv) / math.sqrt(N)
        attn = v + t2
        return attn @ W_out + b_out

    def _L0_ffn_ref(x, W1, b1, Wg, bg, Wd, bd):
        import jax, jax.numpy as jnp
        import numpy as np
        C = 256
        HID = 1024
        E = 8
        TEMP = 1.0
        orig_shape = x.shape
        xf = x.reshape(-1, orig_shape[-1])
        H = jax.nn.gelu(xf @ W1 + b1, approximate=False)
        probs = jax.nn.softmax((H @ Wg + bg) / TEMP, axis=-1)
        assign = jnp.argmax(probs, axis=-1)
        out = jnp.zeros_like(xf)
        for e in range(Wd.shape[0]):
            y = H @ Wd[e] + bd[e]
            sel = (assign == e)[:, None]
            out = out + jnp.where(sel, probs[:, e:e + 1] * y, 0.0)
        return out.reshape(orig_shape)

    def _L1_gnn_ref(nodes, senders, receivers, W_left, b_left, W_right):
        import jax, jax.numpy as jnp
        import numpy as np
        N_NODES = 6250
        N_EDGES = 100000
        D_IN = 256
        D_OUT = 256
        num_nodes = nodes.shape[0]
        seg_sum = jax.ops.segment_sum(nodes[senders], receivers, num_segments=num_nodes)
        counts = jax.ops.segment_sum(jnp.ones_like(receivers, dtype=nodes.dtype), receivers, num_segments=num_nodes)
        h_neigh = seg_sum / jnp.maximum(counts, 1.0)[:, None]
        h = jnp.concatenate((nodes, h_neigh), axis=1)
        out = h @ W_left + b_left
        out = out + nodes @ W_right
        return out

    def _L1_mix_ref(x, Wq, bq, Wk, bk, Wv, bv, Wfc, bfc):
        import jax, jax.numpy as jnp
        import numpy as np
        B, L, D, H = (4, 2048, 256, 8)
        DK = D // H

        def _heads(t):
            b, l, d = t.shape
            return t.reshape(b, l, H, DK).transpose(0, 2, 1, 3)
        q = _heads(x @ Wq.T + bq)
        k = _heads(x @ Wk.T + bk)
        v = _heads(x @ Wv.T + bv)
        seq_len = q.shape[-2]
        p_attn = jnp.einsum('bhnd,bhne->bhde', k, v) / seq_len
        out = jnp.einsum('bhnd,bhde->bhne', q, p_attn)
        out = out.transpose(0, 2, 1, 3).reshape(x.shape[0], seq_len, H * DK)
        return out @ Wfc.T + bfc

    def _L1_ffn_ref(x, W_gat, att_src, att_dst, b_gat, ln_gamma, ln_beta, W1, b1, W2, b2, edge_index):
        import jax, jax.numpy as jnp
        import numpy as np
        B, N, D = (16, 512, 256)
        NUM_EXPERTS, TOP_K, HEADS = (4, 2, 4)
        N_EDGES = 131072
        LN_EPS = 1e-05

        def _layernorm(x, g, b):
            mu = x.mean(-1, keepdims=True)
            var = ((x - mu) ** 2).mean(-1, keepdims=True)
            return (x - mu) * jax.lax.rsqrt(var + LN_EPS) * g + b

        def _forward(x, edge_index, W_gat, att_src, att_dst, b_gat, ln_gamma, ln_beta, W1, b1, W2, b2):
            Bc, Nc, Dc = x.shape
            M = Bc * Nc
            x_flat = x.reshape(M, Dc)
            h = (x_flat @ W_gat).reshape(M, HEADS, NUM_EXPERTS)
            loops = jnp.arange(M, dtype=edge_index.dtype)
            src = jnp.concatenate([edge_index[0], loops])
            dst = jnp.concatenate([edge_index[1], loops])
            a_src = (h * att_src).sum(-1)
            a_dst = (h * att_dst).sum(-1)
            e = jax.nn.leaky_relu(a_src[src] + a_dst[dst], negative_slope=0.2)
            e_max = jax.ops.segment_max(e, dst, num_segments=M)
            ee = jnp.exp(e - e_max[dst])
            denom = jax.ops.segment_sum(ee, dst, num_segments=M)
            alpha = ee / (denom[dst] + 1e-16)
            msg = h[src] * alpha[:, :, None]
            agg = jax.ops.segment_sum(msg, dst, num_segments=M).reshape(M, HEADS * NUM_EXPERTS) + b_gat
            scores = _layernorm(agg, ln_gamma, ln_beta).reshape(M, HEADS, NUM_EXPERTS).mean(1)
            scores = scores.reshape(Bc, Nc, NUM_EXPERTS)
            topk_s, topk_i = jax.lax.top_k(scores, TOP_K)
            w = jax.nn.softmax(topk_s, axis=-1)
            out = jnp.zeros_like(x)
            for ei in range(NUM_EXPERTS):
                g = jnp.where(topk_i == ei, w, 0.0).sum(-1)
                hh = jax.nn.gelu(x @ W1[ei] + b1[ei], approximate=False)
                out = out + g[..., None] * (hh @ W2[ei] + b2[ei])
            return out
        return _forward(x, edge_index, W_gat, att_src, att_dst, b_gat, ln_gamma, ln_beta, W1, b1, W2, b2)
    xn = _layernorm(x, axis=-1)
    x = x + _L0_gnn_ref(xn, L0_gnn_Wq, L0_gnn_bq, L0_gnn_Wk, L0_gnn_bk, L0_gnn_Wv, L0_gnn_bv, L0_gnn_Wo, L0_gnn_bo, src, dst) + _L0_mix_ref(xn[None], L0_mix_W_qkv, L0_mix_b_qkv, L0_mix_W_out, L0_mix_b_out)[0]
    x = x + _L0_ffn_ref(_layernorm(x, axis=-1)[None], L0_ffn_W1, L0_ffn_b1, L0_ffn_Wg, L0_ffn_bg, L0_ffn_Wd, L0_ffn_bd)[0]
    xn = _layernorm(x, axis=-1)
    x = x + _L1_gnn_ref(xn, src, dst, L1_gnn_W_left, L1_gnn_b_left, L1_gnn_W_right) + _L1_mix_ref(xn[None], L1_mix_Wq, L1_mix_bq, L1_mix_Wk, L1_mix_bk, L1_mix_Wv, L1_mix_bv, L1_mix_Wfc, L1_mix_bfc)[0]
    x = x + _L1_ffn_ref(_layernorm(x, axis=-1)[None], L1_ffn_W_gat, L1_ffn_att_src, L1_ffn_att_dst, L1_ffn_b_gat, L1_ffn_ln_gamma, L1_ffn_ln_beta, L1_ffn_W1, L1_ffn_b1, L1_ffn_W2, L1_ffn_b2, L1_ffn_edge_index)[0]
    return x

_drawn_inputs = setup_inputs


def setup_inputs(seed=0):
    import zlib

    import numpy as np

    out = dict(_drawn_inputs(seed))
    spreads = {'L0_ffn_b1': (0.0, 0.652),
     'L0_ffn_bg': (0.0, 0.443),
     'L0_ffn_bd': (0.0, 0.586),
     'L1_gnn_b_left': (0.0, 2.0),
     'L1_mix_bq': (0.0, 0.8),
     'L1_mix_bk': (0.0, 0.8),
     'L1_mix_bv': (0.0, 0.8),
     'L1_mix_bfc': (0.0, 2.0),
     'L1_ffn_b_gat': (0.0, 0.8),
     'L1_ffn_ln_gamma': (1.0, 0.6),
     'L1_ffn_ln_beta': (0.0, 2.0),
     'L1_ffn_b1': (0.0, 0.8),
     'L1_ffn_b2': (0.0, 2.0)}
    factors = {'L0_gnn_bq': 8.0,
     'L0_gnn_bk': 200.0,
     'L0_gnn_bv': 4.895,
     'L0_gnn_bo': 4.398,
     'L0_mix_b_out': 2.943,
     'L0_ffn_W1': 3.375,
     'L0_ffn_Wg': 3.61,
     'L0_ffn_Wd': 3.925,
     'L1_mix_Wq': 7.832,
     'L1_mix_Wk': 8.0,
     'L1_mix_Wv': 8.0,
     'L1_mix_Wfc': 5.874,
     'L1_ffn_att_src': 34.712,
     'L1_ffn_att_dst': 49.24,
     'L1_gnn_W_left': 2.671,
     'L1_ffn_W_gat': 7.085,
     'L1_ffn_W1': 5.112,
     'L1_ffn_W2': 4.631}
    for name, (base, spread) in spreads.items():
        noise = np.random.default_rng([zlib.crc32(name.encode()), seed]).standard_normal(out[name].shape)
        drawn = base * np.exp(spread * noise) if base else spread * noise
        out[name] = jnp.asarray(drawn.astype(out[name].dtype))
    for name, factor in factors.items():
        out[name] = (out[name] * factor).astype(out[name].dtype)
    return out
```

```python
from contextlib import ExitStack

import numpy as np
import concourse.bass as bass
from concourse import mybir

ALU = mybir.AluOpType
ACT = mybir.ActivationFunctionType
F32 = mybir.dt.float32
BF16 = mybir.dt.bfloat16
I32 = mybir.dt.int32
AX = mybir.AxisListType

P = 128
N = 6250
C = 256
NT = 50
NP = NT * P
KC = C // P
LN_EPS = 1e-5
BIG = 1e30

PRIME = 4


def wait_reg(eng, sem, value):
    eng.wait_ge(sem, value)
    if not isinstance(value, int):
        eng.nop(nofuse=True)


def after(eng, sem, t):
    wait_reg(eng, sem, t + 1 + PRIME)


def after_dma(eng, sem, t, per=1):
    wait_reg(eng, sem, (t + 1 + PRIME) * (16 * per))


def loaded(eng, sem, t, s, per=1, slots=2):
    wait_reg(eng, sem, (t - s) * (16 * per // slots) + 16 * per)


class Chain:

    def __init__(self, eng, sem, per):
        self.eng, self.sem, self.per = eng, sem, per

    def start_once(self):
        self.base, self.k = 0, 0

    def start(self, t):
        self.base, self.k = t * self.per, 0

    def __call__(self, ins):
        self.k += 1
        ins.then_inc(self.sem, 1)
        wait_reg(self.eng, self.sem, self.base + self.k)

    def end(self):
        assert self.k == self.per, (self.k, self.per)


def skewed(eng, head, tail, n=NT):
    head(0, 0)
    with eng.Fori(0, n // 2 - 1) as j:
        head(2 * j + 1, 1)
        tail(2 * j, 0)
        head(2 * j + 2, 0)
        tail(2 * j + 1, 1)
    head(n - 1, 1)
    tail(n - 2, 0)
    tail(n - 1, 1)


def ring(eng, body, n=NT, slots=2, first=0):
    with eng.Fori(first // slots, n // slots) as j:
        for s in range(slots):
            body(slots * j + s, s)


def semaphores(nc, c, before="", after=""):
    held = []

    def sem(name):
        held.append(nc.alloc_semaphore(before + name + after))
        return held[-1]

    def clear():
        nc.clear_and_free_semaphores(held)
        nc.all_engine_barrier()
    c.callback(clear)
    return sem


class Core:
    pass


def rows(ap, t):
    return ap[bass.ds(t * P, P), :] if not isinstance(t, int) else ap[t * P:(t + 1) * P, :]


def row_of(ap):
    return ap.rearrange("(a n) -> a n", a=1)


def prime(sp, sems, dma_sems=()):
    for s in sems:
        sp.sem_inc(s, PRIME)
    for s, per in dma_sems:
        sp.sem_inc(s, 16 * PRIME * per)


def constants(nc, k, x):
    with ExitStack() as c:
        zeros = c.enter_context(nc.sbuf_tensor("zeros", [P, C], F32))
        node = c.enter_context(nc.sbuf_tensor("node", [P, NT], I32))
        itmp = c.enter_context(nc.sbuf_tensor("itmp", [P, P], I32))
        ipart = c.enter_context(nc.sbuf_tensor("ipart", [P, 1], I32))
        sem = semaphores(nc, c)
        s_set, s_copied, s_iota, s_mask = (sem(n) for n in ("const_set", "x_copied", "const_iota", "const_mask"))
        block = c.enter_context(nc.Block())

        @block.gpsimd
        def _(pool):
            pool.memset(zeros[:], 0.0).then_inc(s_set, 1)
            pool.memset(k.ident[:], 0.0).then_inc(s_set, 1)
            pool.memset(k.ones[:], 1.0).then_inc(s_set, 1)
            pool.memset(k.neghalf[:], -0.5).then_inc(s_set, 1)
            pool.memset(k.half[:], 0.5).then_inc(s_set, 1)
            pool.memset(k.low[:], 1.0).then_inc(s_set, 1)
            pool.memset(k.upper[:], 1.0).then_inc(s_set, 1)
            pool.wait_ge(s_set, 7)
            pool.affine_select(out=k.ident[:], in_=k.ident[:], compare_op=ALU.not_equal, fill=1.0,
                               base=0, pattern=[[-1, P]], channel_multiplier=1).then_inc(s_set, 1)
            pool.affine_select(out=k.low[:], in_=k.low[:], compare_op=ALU.is_gt, fill=0.0,
                               base=0, pattern=[[-1, P]], channel_multiplier=1).then_inc(s_set, 1)
            pool.affine_select(out=k.upper[:], in_=k.upper[:], compare_op=ALU.is_gt, fill=0.0,
                               base=0, pattern=[[1, P]], channel_multiplier=-1).then_inc(s_set, 1)
            pool.iota(node[:], [[P, NT]], 0, 1).then_inc(s_iota, 1)
            pool.iota(itmp[:], [[1, P]], 0, 0).then_inc(s_iota, 1)
            pool.iota(ipart[:], [[1, 1]], 0, 1).then_inc(s_iota, 1)
            pool.wait_ge(s_set, 10)

        @block.vector
        def _(dve):
            dve.wait_ge(s_iota, 3)
            dve.tensor_scalar(k.valid[:], node[:], float(N), None, ALU.is_lt).then_inc(s_mask, 1)
            dve.tensor_copy(k.nodef[:], node[:]).then_inc(s_mask, 1)
            dve.tensor_copy(k.iota[:], itmp[:]).then_inc(s_mask, 1)
            dve.tensor_copy(k.part[:], ipart[:]).then_inc(s_mask, 1)
            dve.wait_ge(s_mask, 4)

        @block.sync
        def _(sp):
            sp.dma_start(k.XP[0:N, :], x).then_inc(s_copied, 16)
            sp.wait_ge(s_set, 1)
            tail = NP - N
            sp.dma_start(k.XP[N:N + P, :], zeros[:]).then_inc(s_copied, 16)
            sp.dma_start(k.XP[N + P:NP, :], zeros[0:tail - P, :]).then_inc(s_copied, 16)
            sp.wait_ge(s_copied, 48)


def layernorm_dve(dve, link, xt, xn, st, mv, ve, rstd, var_ready, rstd_ready, xn_done, t, wait_xn_free):
    link(dve.bn_stats(st[:], xt))
    link(dve.bn_aggr(mv[:], st[:]))
    dve.tensor_scalar(ve[:], mv[:, 1:2], LN_EPS, None, ALU.add).then_inc(var_ready, 1)
    wait_xn_free()
    after(dve, rstd_ready, t)
    dve.tensor_scalar(xn, xt, mv[:, 0:1], rstd[:, 0:1], ALU.subtract, ALU.mult).then_inc(xn_done, 1)
    after(dve, xn_done, t)


def project_nodes(nc, k, w):
    W3 = 6 * C
    with ExitStack() as c:
        sb = lambda name, shape, dt=F32: c.enter_context(nc.sbuf_tensor(name, shape, dt))
        sem = semaphores(nc, c)
        wcat = sb("wcat", [P, KC, W3])
        bcat = sb("bcat", [P, W3])
        wout = sb("wout", [P, KC, C])
        xt = sb("xt", [P, 2, C])
        xn = sb("xn", [P, C])
        st, mv, ve, rstd = sb("st", [P, 6]), sb("mv", [P, 2]), sb("ve", [P, 1]), sb("rstd", [P, 1])
        xT = sb("xT", [P, KC, P])
        allp = sb("allp", [P, W3])
        mean = sb("mean", [P, 2])
        nmean = sb("nmean", [P, 2])
        sq = sb("sq", [P, 2, C])
        s2 = sb("s2", [P, 2])
        s2e = sb("s2e", [P, 2])
        r2 = sb("r2", [P, 2])
        q4s = sb("q4s", [P, 1])
        q4 = sb("q4", [P, 1])
        qn = sb("qn", [P, 1])
        qr = sb("qr", [P, 1])
        junk = sb("junk", [P, C])
        k2 = sb("k2", [P, C])
        k4 = sb("k4", [P, C])
        q2 = sb("q2", [P, C])
        kvT = sb("kvT", [P, KC, C])
        cn = sb("cn", [P, KC])
        cr = sb("cr", [P, KC])
        psT = c.enter_context(nc.psum_tensor("psT", [P, KC, P], F32))
        psP = c.enter_context(nc.psum_tensor("psP", [P, 3, 512], F32))
        psK = c.enter_context(nc.psum_tensor("psK", [P, KC, C], F32))
        psN = c.enter_context(nc.psum_tensor("psN", [P, 512], F32))
        psM = c.enter_context(nc.psum_tensor("psM", [P, KC, C], F32))
        w_in = sem("w_in")
        x_in = [sem("x_in0"), sem("x_in1")]
        var_ready, rstd_ready, xn_done = sem("var_ready"), sem("rstd_ready"), sem("xn_done")
        xT_ps, xT_sb, proj_done, evac_done = sem("xT_ps"), sem("xT_sb"), sem("proj_done"), sem("evac_done")
        mean_done, sq_done, q4_done, k2_done, k4_done = (sem(n) for n in
                                                         ("mean_done", "sq_done", "q4_done", "k2_done", "k4_done"))
        q2_done, acc_done = sem("q2_done"), sem("acc_done")
        stored_q, stored_kv, stored_m = sem("stored_q"), sem("stored_kv"), sem("stored_m")
        ln_step, mix_step, act_step = sem("ln_step"), sem("mix_step"), sem("act_step")
        kvT_sb, norm_sb, root_done, kvw_ps, fin = (sem(n) for n in
                                                       ("kvT_sb", "norm_sb", "root_done", "kvw_ps", "fin"))
        tiles = [var_ready, rstd_ready, xn_done, xT_ps, xT_sb, proj_done, evac_done, mean_done, sq_done,
                 q4_done, k2_done, k4_done, q2_done, acc_done]
        block = c.enter_context(nc.Block())

        @block.sync
        def _(sp):
            prime(sp, tiles, [(stored_q, 1), (stored_kv, 1), (stored_m, 2)])
            cols = [(w["L0_gnn_Wq"], 0, C), (w["L0_gnn_Wk"], C, C), (w["L0_gnn_Wv"], 2 * C, C),
                    (w["L0_mix_W_qkv"], 3 * C, 3 * C)]
            for src, o, n in cols:
                sp.dma_start(wcat[:, :, o:o + n], src.rearrange("(a p) n -> p a n", p=P)).then_inc(w_in, 16)
            for src, o, n in [(w["L0_gnn_bq"], 0, C), (w["L0_gnn_bk"], C, C), (w["L0_gnn_bv"], 2 * C, C),
                              (w["L0_mix_b_qkv"], 3 * C, 3 * C)]:
                sp.dma_start(bcat[:, o:o + n], src.partition_broadcast(P)).then_inc(w_in, 16)
            sp.dma_start(wout[:], w["L0_mix_W_out"].rearrange("(a p) n -> p a n", p=P)).then_inc(w_in, 16)

            def store(t, s):
                after(sp, evac_done, t)
                sp.dma_start(rows(k.Q, t), allp[:, 0:C]).then_inc(stored_q, 16)
                sp.dma_start(rows(k.KV, t), allp[:, C:3 * C]).then_inc(stored_kv, 16)
                sp.dma_start(rows(k.MV, t)[:, C:2 * C], allp[:, 5 * C:6 * C]).then_inc(stored_m, 16)
                after(sp, q2_done, t)
                sp.dma_start(rows(k.MV, t)[:, 0:C], q2[:]).then_inc(stored_m, 16)
            ring(sp, store)
            after_dma(sp, stored_q, NT - 1)
            after_dma(sp, stored_kv, NT - 1)
            after_dma(sp, stored_m, NT - 1, 2)

        @block.gpsimd
        def _(pool):
            def head(t, s):
                after(pool, xn_done, t - 2)
                pool.dma_start(xt[:, s, :], rows(k.XP, t)).then_inc(x_in[s], 16)
                after(pool, var_ready, t)
                pool.tensor_tensor(rstd[:], ve[:], k.neghalf[:], ALU.pow).then_inc(rstd_ready, 1)

            def tail(t, s):
                after(pool, sq_done, t)
                pool.tensor_tensor(q4[:], q4s[:], k.half[:], ALU.pow).then_inc(q4_done, 1)
            skewed(pool, head, tail)
            pool.wait_ge(norm_sb, 1)
            pool.tensor_tensor(cr[:], cn[:], k.half[:].to_broadcast([P, KC]), ALU.pow).then_inc(root_done, 1)

        @block.vector
        def _(dve):
            ln = Chain(dve, ln_step, 2)
            mix = Chain(dve, mix_step, 6)

            def head(t, s):
                ln.start(t)
                loaded(dve, x_in[s], t, s)
                layernorm_dve(dve, ln, xt[:, s, :], xn[:], st, mv, ve, rstd, var_ready, rstd_ready, xn_done,
                              t, lambda: after(dve, xT_ps, t - 1))
                ln.end()

            def tail(t, s):
                mix.start(t)
                after_dma(dve, stored_q, t - 1)
                after_dma(dve, stored_kv, t - 1)
                after_dma(dve, stored_m, t - 1, 2)
                after(dve, acc_done, t - 1)
                after(dve, proj_done, t)
                dve.tensor_tensor(allp[:], psP[:].rearrange("p a n -> p (a n)"), bcat[:], ALU.add).then_inc(evac_done, 1)
                after(dve, evac_done, t)
                mix(dve.tensor_reduce(mean[:], allp[:, 3 * C:5 * C].rearrange("p (a n) -> p a n", a=2), AX.X, ALU.add))
                dve.tensor_scalar(nmean[:], mean[:], -1.0 / C, None, ALU.mult).then_inc(mean_done, 1)
                after(dve, sq_done, t)
                mix(dve.tensor_scalar(s2e[:], s2[:], 1e-7, None, ALU.add))
                mix(dve.reciprocal(r2[:], s2e[:]))
                dve.tensor_scalar(k2[:], sq[:, 1, :], r2[:, 1:2], k.valid[:, bass.ds(t, 1)], ALU.mult, ALU.mult)\
                    .then_inc(k2_done, 1)
                after(dve, q4_done, t)
                mix(dve.tensor_scalar(qn[:], q4[:], r2[:, 0:1], 1e-12, ALU.mult, ALU.max))
                mix(dve.reciprocal(qr[:], qn[:]))
                mix(dve.tensor_scalar(qn[:], qr[:], r2[:, 0:1], None, ALU.mult))
                dve.tensor_scalar(q2[:], sq[:, 0, :], qn[:, 0:1], None, ALU.mult).then_inc(q2_done, 1)
                after(dve, k2_done, t)
                after(dve, q2_done, t)
                mix.end()
            dve.wait_ge(w_in, 16 * 9)
            skewed(dve, head, tail)
            after(dve, acc_done, NT - 1)
            dve.tensor_copy(kvT[:], psK[:]).then_inc(kvT_sb, 1)
            dve.tensor_copy(cn[:], psN[:, 0:KC]).then_inc(norm_sb, 1)
            dve.wait_ge(kvw_ps, 1)
            dve.wait_ge(root_done, 1)
            dve.tensor_scalar(cn[:], cr[:], 1e-12, float(np.sqrt(N)), ALU.max, ALU.mult).then_inc(fin, 1)
            dve.wait_ge(fin, 1)
            dve.reciprocal(cr[:], cn[:]).then_inc(fin, 1)
            dve.wait_ge(fin, 2)
            for a in range(KC):
                dve.tensor_scalar(k.M1[:, a, :], psM[:, a, :], cr[:, a:a + 1], None, ALU.mult).then_inc(fin, 1)
            dve.wait_ge(fin, 4)

        @block.scalar
        def _(act):
            step = Chain(act, act_step, 2)

            def head(t, s):
                after(act, xT_ps, t)
                after(act, proj_done, t - 1)
                act.activation(xT[:], psT[:], ACT.Copy).then_inc(xT_sb, 1)

            def tail(t, s):
                step.start(t)
                after(act, mean_done, t)
                after(act, q2_done, t - 1)
                step(act.activation(sq[:, 0, :], allp[:, 3 * C:4 * C], ACT.Square, bias=nmean[:, 0:1], accum_out=s2[:, 0:1]))
                step(act.activation(sq[:, 1, :], allp[:, 4 * C:5 * C], ACT.Square, bias=nmean[:, 1:2], accum_out=s2[:, 1:2]))
                act.activation(junk[:], sq[:, 0, :], ACT.Square, accum_out=q4s[:, 0:1]).then_inc(sq_done, 1)
                after(act, k2_done, t)
                after(act, acc_done, t - 1)
                after(act, sq_done, t)
                act.activation(k4[:], k2[:], ACT.Square).then_inc(k4_done, 1)
                step.end()
            skewed(act, head, tail)

        @block.tensor
        def _(pe):
            pe.wait_ge(w_in, 16 * 9)

            def head(t, s):
                after(pe, xn_done, t)
                after(pe, xT_sb, t - 1)
                for a in range(KC):
                    last = pe.transpose(psT[:, a, :], xn[:, a * P:(a + 1) * P], k.ident[:])
                last.then_inc(xT_ps, 1)
                after(pe, xT_sb, t)
                after(pe, evac_done, t - 1)
                for g in range(3):
                    for a in range(KC):
                        last = pe.matmul(psP[:, g, :], xT[:, a, :], wcat[:, a, g * 512:(g + 1) * 512],
                                         start=(a == 0), stop=(a == KC - 1))
                last.then_inc(proj_done, 1)

            def tail(t, s):
                after(pe, k4_done, t)
                after(pe, k2_done, t)
                for a in range(KC):
                    pe.matmul(psK[:, a, :], allp[:, 5 * C + a * P:5 * C + (a + 1) * P], k2[:],
                              start=False, stop=False, skip_group_check=True)
                for a in range(KC):
                    last = pe.matmul(psN[:, a:a + 1], k4[:, a * P:(a + 1) * P], k.ones[:, 0:1],
                                     start=False, stop=False, skip_group_check=True)
                last.then_inc(acc_done, 1)
            pe.matmul(psK[:].rearrange("p a n -> p (a n)"), k.zero1[:], bcat[0:1, 0:512], start=True, stop=True)
            pe.matmul(psN[:, 0:KC], k.zero1[:], bcat[0:1, 0:KC], start=True, stop=True)
            skewed(pe, head, tail)
            pe.wait_ge(kvT_sb, 1)
            for a in range(KC):
                for d in range(KC):
                    last = pe.matmul(psM[:, a, :], kvT[:, d, a * P:(a + 1) * P], wout[:, d, :],
                                     start=(d == 0), stop=(d == KC - 1))
            last.then_inc(kvw_ps, 1)


def mix_output(nc, k, w):
    with ExitStack() as c:
        sb = lambda name, shape, dt=F32: c.enter_context(nc.sbuf_tensor(name, shape, dt))
        sem = semaphores(nc, c)
        wout = sb("a_wout", [P, KC, C])
        bias = sb("a_bias", [P, C])
        bias2 = sb("a_bias2", [P, C])
        mvt = sb("a_mvt", [P, 2, 2 * C])
        xt = sb("a_xt", [P, 2, C])
        mT = sb("a_mT", [P, 4, P])
        xb = sb("a_xb", [P, C])
        xo = sb("a_xo", [P, C])
        psT = c.enter_context(nc.psum_tensor("a_psT", [P, 2, 4, P], F32))
        psO = c.enter_context(nc.psum_tensor("a_psO", [P, 2, 512], F32))
        w_in = sem("a_w_in")
        t_in = [sem("a_t_in0"), sem("a_t_in1")]
        bias_done, ps_T, sb_T, ps_O, xb_done, out_done, stored = (
            sem("a_" + n) for n in ("bias_done", "ps_T", "sb_T", "ps_O", "xb_done", "out_done", "stored"))
        block = c.enter_context(nc.Block())

        @block.sync
        def _(sp):
            prime(sp, [ps_T, sb_T, ps_O, xb_done, out_done], [(stored, 1)])
            sp.dma_start(wout[:], w["L0_mix_W_out"].rearrange("(a p) n -> p a n", p=P)).then_inc(w_in, 16)
            sp.dma_start(bias[:], w["L0_mix_b_out"].partition_broadcast(P)).then_inc(w_in, 16)
            sp.dma_start(bias2[:], w["L0_gnn_bo"].partition_broadcast(P)).then_inc(w_in, 16)

            def load(t, s):
                after(sp, ps_T, t - 2)
                after(sp, xb_done, t - 2)
                sp.dma_start(mvt[:, s, :], rows(k.MV, t)).then_inc(t_in[s], 16)
                sp.dma_start(xt[:, s, :], rows(k.XP, t)).then_inc(t_in[s], 16)
            ring(sp, load)

        @block.tensor
        def _(pe):
            def head(t, s):
                loaded(pe, t_in[s], t, s, per=2)
                after(pe, sb_T, t - 2)
                for a in range(4):
                    last = pe.transpose(psT[:, s, a, :], mvt[:, s, a * P:(a + 1) * P], k.ident[:])
                last.then_inc(ps_T, 1)

            def tail(t, s):
                after(pe, sb_T, t)
                after(pe, out_done, t - 2)
                for a in range(4):
                    rhs = k.M1[:, a, :] if a < KC else wout[:, a - KC, :]
                    last = pe.matmul(psO[:, s, 0:C], mT[:, a, :], rhs, start=(a == 0), stop=(a == 3))
                last.then_inc(ps_O, 1)
            pe.wait_ge(w_in, 48)
            skewed(pe, head, tail)

        @block.scalar
        def _(act):
            def copy(t, s):
                after(act, ps_T, t)
                after(act, ps_O, t - 1)
                act.activation(mT[:], psT[:, s, :, :], ACT.Copy).then_inc(sb_T, 1)

            def store(t, s):
                after(act, out_done, t)
                act.dma_start(rows(k.X1M, t), xo[:]).then_inc(stored, 16)
            skewed(act, copy, store)
            after_dma(act, stored, NT - 1)

        @block.vector
        def _(dve):
            dve.wait_ge(w_in, 48)
            dve.tensor_tensor(bias[:], bias[:], bias2[:], ALU.add).then_inc(bias_done, 1)
            dve.wait_ge(bias_done, 1)

            def body(t, s):
                loaded(dve, t_in[s], t, s, per=2)
                after(dve, out_done, t - 1)
                dve.tensor_tensor(xb[:], xt[:, s, :], bias[:], ALU.add).then_inc(xb_done, 1)
                after(dve, xb_done, t)
                after(dve, ps_O, t)
                after_dma(dve, stored, t - 1)
                dve.tensor_tensor(xo[:], xb[:], psO[:, s, 0:C], ALU.add).then_inc(out_done, 1)
            ring(dve, body)


EA = 206250
BLK = 13
LA = 1612
NBA = LA // BLK
HEADS = 8
DK = C // HEADS


def lane_lists(nc, k, w):
    with ExitStack() as c:
        sb = lambda name, shape, dt=F32: c.enter_context(nc.sbuf_tensor(name, shape, dt))
        sem = semaphores(nc, c)
        lo_i, lo = sb("lo_i", [P, LA], I32), sb("lo", [P, LA])
        hi_i, hi = sb("hi_i", [P, LA], I32), sb("hi", [P, LA])
        dstf = sb("dstf", [P, LA])
        oh_lo = sb("oh_lo", [P, 2, BLK, P], BF16)
        oh_hi = sb("oh_hi", [P, 2, BLK, NT], BF16)
        psC = c.enter_context(nc.psum_tensor("psC", [P, NT], F32))
        set_done, in_done, dve_step, onehots, counted = (sem(n) for n in (
            "l_set_done", "l_in_done", "l_dve_step", "l_onehots", "l_counted"))
        block = c.enter_context(nc.Block())
        full = EA // LA
        rest = EA - full * LA

        @block.sync
        def _(sp):
            prime(sp, [onehots, counted])
            sp.wait_ge(set_done, 2)
            for tile, src in ((k.srci, w["src"]), (k.dsti, w["dst"])):
                sp.dma_start(tile[0:full, :], src[0:full * LA].rearrange("(p i) -> p i", i=LA)).then_inc(in_done, 16)
                sp.dma_start(tile[full:P, 0:rest], row_of(src[full * LA:EA])).then_inc(in_done, 16)

        @block.gpsimd
        def _(pool):
            pool.memset(k.srci[:], 0).then_inc(set_done, 1)
            pool.memset(k.dsti[:], N).then_inc(set_done, 1)

        @block.vector
        def _(dve):
            link = Chain(dve, dve_step, None)
            link.start_once()
            dve.wait_ge(in_done, 64)
            link(dve.tensor_scalar(lo_i[:], k.dsti[:], P - 1, None, ALU.bitwise_and))
            link(dve.tensor_scalar(hi_i[:], k.dsti[:], 7, None, ALU.logical_shift_right))
            link(dve.tensor_copy(lo[:], lo_i[:]))
            link(dve.tensor_copy(hi[:], hi_i[:]))
            link(dve.tensor_copy(dstf[:], k.dsti[:]))
            link(dve.memset(k.same[:, 0:1], 0.0))
            link(dve.tensor_tensor(k.same[:, 1:LA], dstf[:, 1:LA], dstf[:, 0:LA - 1], ALU.is_equal))
            link(dve.tensor_copy(k.first[:], dstf[:, 0:1]))
            link(dve.tensor_copy(k.last[:], dstf[:, LA - 1:LA]))

            def body(b, s):
                after(dve, counted, b - 2)
                dve.tensor_tensor(oh_lo[:, s], k.iota[:].unsqueeze(1).to_broadcast([P, BLK, P]),
                                  lo[:, bass.ds(b * BLK, BLK)].unsqueeze(2).to_broadcast([P, BLK, P]), ALU.is_equal)
                dve.tensor_tensor(oh_hi[:, s], k.iota[:, 0:NT].unsqueeze(1).to_broadcast([P, BLK, NT]),
                                  hi[:, bass.ds(b * BLK, BLK)].unsqueeze(2).to_broadcast([P, BLK, NT]), ALU.is_equal)\
                    .then_inc(onehots, 1)
            ring(dve, body, n=NBA)
            after(dve, counted, NBA - 1)
            link(dve.tensor_copy(k.cnt[:], psC[:]))

        @block.tensor
        def _(pe):
            pe.wait_ge(in_done, 64)
            pe.matmul(psC[:], k.zero1[:], k.ones[0:1, 0:NT], start=True, stop=True)

            def body(b, s):
                after(pe, onehots, b)
                for j in range(BLK):
                    last = pe.matmul(psC[:], oh_lo[:, s, j, :], oh_hi[:, s, j, :],
                                     start=False, stop=False, skip_group_check=True)
                last.then_inc(counted, 1)
            ring(pe, body, n=NBA)


def rank_nodes(nc, k, cnt, nt, length, start, pos_i, inc_i, tag):
    with ExitStack() as c:
        sb = lambda name, shape, dt=F32: c.enter_context(nc.sbuf_tensor(name + tag, shape, dt))
        sem = semaphores(nc, c, after=tag)
        incl, tot, end, pos = sb("incl", [P, nt]), sb("tot", [P, nt]), sb("end", [P, nt]), sb("pos", [P, nt])
        lane, tmp, tmp2 = sb("lane", [P, nt]), sb("tmp", [P, nt]), sb("tmp2", [P, nt])
        starts = sb("starts", [P, P])
        onesr = sb("onesr", [P, nt])
        cmp = sb("cmp", [P, nt, P])
        psA = c.enter_context(nc.psum_tensor("psA" + tag, [P, 512], F32))
        psB = c.enter_context(nc.psum_tensor("psB" + tag, [P, 512], F32))
        summed, step = sem("summed"), sem("rank_step")
        block = c.enter_context(nc.Block())

        @block.tensor
        def _(pe):
            pe.matmul(psA[:, 0:nt], k.ones[:], cnt, start=True, stop=True)
            pe.matmul(psB[:, 0:nt], k.upper[:], cnt, start=True, stop=True).then_inc(summed, 1)

        @block.vector
        def _(dve):
            link = Chain(dve, step, None)
            link.start_once()
            link(dve.memset(onesr[:], 1.0))
            dve.wait_ge(summed, 1)
            link(dve.tensor_copy(tot[:], psA[:, 0:nt]))
            link(dve.tensor_tensor_scan(incl[:], onesr[:], tot[:], 0.0, ALU.mult, ALU.add))
            link(dve.tensor_tensor(tmp[:], incl[:], tot[:], ALU.subtract))
            link(dve.tensor_tensor(start, tmp[:], psB[:, 0:nt], ALU.add))
            link(dve.tensor_tensor(end[:], start, cnt, ALU.add))
            link(dve.tensor_scalar(pos[:], end[:], -1.0, 0.0, ALU.add, ALU.max))
            link(dve.tensor_copy(pos_i, pos[:]))
            link(dve.tensor_scalar(starts[:], k.iota[:], float(length), None, ALU.mult))
            link(dve.tensor_tensor(cmp[:], pos[:].unsqueeze(2).to_broadcast([P, nt, P]),
                                   starts[:].unsqueeze(1).to_broadcast([P, nt, P]), ALU.is_ge))
            link(dve.tensor_reduce(tmp[:], cmp[:], AX.X, ALU.add))
            link(dve.tensor_scalar(lane[:], tmp[:], -1.0, None, ALU.add))
            link(dve.tensor_scalar(tmp[:], lane[:], float(length), None, ALU.mult))
            link(dve.tensor_tensor(tmp2[:], start, tmp[:], ALU.is_lt))
            link(dve.tensor_scalar(tmp[:], lane[:], float(-P), None, ALU.add))
            link(dve.tensor_tensor(lane[:], tmp[:], tmp2[:], ALU.mult))
            link(dve.tensor_scalar(tmp[:], lane[:], float(P), None, ALU.add))
            link(dve.tensor_copy(inc_i, tmp[:]))


def edge_attention(nc, k):
    scale = float(DK) ** -0.5
    D1, S1 = DK + 1, BLK + 1
    with ExitStack() as c:
        sb = lambda name, shape, dt=F32: c.enter_context(nc.sbuf_tensor(name, shape, dt))
        sem = semaphores(nc, c)
        idx = sb("e_idx", [P, 2, 2, BLK], I32)
        q = sb("e_q", [P, 2, BLK, C])
        kv = sb("e_kv", [P, 2, BLK, 2 * C])
        S = sb("e_S", [P, HEADS, S1])
        bias = sb("e_bias", [P, HEADS, S1])
        bias1 = sb("e_bias1", [P, BLK])
        M = sb("e_M", [P, HEADS, S1])
        D = sb("e_D", [P, 2, HEADS, BLK])
        E = sb("e_E", [P, 2, HEADS, BLK])
        CX = sb("e_CX", [P, D1, HEADS, S1])
        PV = sb("e_PV", [P, D1, HEADS, S1])
        A = sb("e_A", [P, D1, HEADS, S1])
        O = sb("e_O", [P, BLK, (D1 + 1) * HEADS])
        idx_in = [sem("idx_in0"), sem("idx_in1")]
        q_in = [sem("q_in0"), sem("q_in1")]
        kv_in = [sem("kv_in0"), sem("kv_in1")]
        set_done, dve_step, d_done, pv_done, a_done, s_done = (sem("e_" + n) for n in (
            "set_done", "dve_step", "d_done", "pv_done", "a_done", "s_done"))
        exp_done, cx_done, o1_done, o_done, stored = (sem("e_" + n) for n in (
            "exp_done", "cx_done", "o1_done", "o_done", "stored"))
        block = c.enter_context(nc.Block())
        src_l, dst_l = k.srci, k.dsti
        pt = k.PT.rearrange("(p i) f -> p i f", i=LA)

        @block.sync
        def _(sp):
            prime(sp, [d_done, pv_done, a_done, s_done, exp_done, cx_done, o_done], [(stored, 1)])

            def fetch(b, s):
                after(sp, pv_done, b - 2)
                sp.dma_start(idx[:, s, 0, :], src_l[:, bass.ds(b * BLK, BLK)]).then_inc(idx_in[s], 16)
                sp.dma_start(idx[:, s, 1, :], dst_l[:, bass.ds(b * BLK, BLK)]).then_inc(idx_in[s], 16)

            def store(b, s):
                after(sp, o_done, b)
                sp.dma_start(pt[:, bass.ds(b * BLK, BLK), :], O[:]).then_inc(stored, 16)
            skewed(sp, fetch, store, n=NBA)
            after_dma(sp, stored, NBA - 1)

        @block.gpsimd
        def _(pool):
            def gather(b, s):
                loaded(pool, idx_in[s], b, s, per=2)
                after(pool, pv_done, b - 2)
                for j in range(BLK):
                    pool.indirect_dma_start(q[:, s, j, :], None, k.Q,
                                            bass.IndirectOffsetOnAxis(ap=idx[:, s, 1, j:j + 1], axis=0)).then_inc(q_in[s], 16)
                    pool.indirect_dma_start(kv[:, s, j, :], None, k.KV,
                                            bass.IndirectOffsetOnAxis(ap=idx[:, s, 0, j:j + 1], axis=0)).then_inc(kv_in[s], 16)
            ring(pool, gather, n=NBA)

        @block.vector
        def _(dve):
            dve.memset(bias[:], -BIG).then_inc(set_done, 1)
            dve.memset(M[:], -BIG).then_inc(set_done, 1)
            dve.memset(CX[:], 0.0).then_inc(set_done, 1)
            dve.memset(A[:], 0.0).then_inc(set_done, 1)
            dve.wait_ge(set_done, 4)
            step = Chain(dve, dve_step, 8)

            def body(b, s):
                step.start(b)
                loaded(dve, q_in[s], b, s, per=BLK)
                loaded(dve, kv_in[s], b, s, per=BLK)
                qs = q[:, s]
                step(dve.tensor_tensor(qs, qs, kv[:, s, :, 0:C], ALU.mult))
                dve.tensor_copy(S[:, :, 0:1], M[:, :, BLK:S1])
                step(dve.tensor_scalar(bias1[:], k.same[:, bass.ds(b * BLK, BLK)], -1.0, BIG, ALU.add, ALU.mult))
                step(dve.tensor_copy(bias[:, :, 1:S1], bias1[:].unsqueeze(1).to_broadcast([P, HEADS, BLK])))
                step(dve.tensor_reduce(S[:, :, 1:S1], qs.rearrange("p j (d h) -> p h j d", h=HEADS), AX.X, ALU.add))
                after(dve, o_done, b - 1)
                step(dve.tensor_tensor_scan(M[:].rearrange("p h j -> p (h j)"), bias[:].rearrange("p h j -> p (h j)"),
                                            S[:].rearrange("p h j -> p (h j)"), -BIG, ALU.add, ALU.max))
                dve.tensor_tensor(D[:, 0], S[:, :, 1:S1], M[:, :, 1:S1], ALU.subtract)
                step(dve.tensor_tensor(D[:, 1], M[:, :, 0:BLK], M[:, :, 1:S1], ALU.subtract))
                dve.tensor_tensor(D[:, 1], D[:, 1], bias[:, :, 1:S1], ALU.add).then_inc(d_done, 1)
                step(dve.tensor_copy(PV[:, :, :, 0], A[:, :, :, BLK]))
                after(dve, exp_done, b)
                step(dve.tensor_copy(PV[:, DK, :, 1:S1], E[:, 0]))
                dve.tensor_tensor(PV[:, 0:DK, :, 1:S1], kv[:, s, :, C:2 * C].rearrange("p j (d h) -> p d h j", h=HEADS),
                                  E[:, 0].unsqueeze(1).to_broadcast([P, DK, HEADS, BLK]), ALU.mult).then_inc(pv_done, 1)
                after(dve, pv_done, b)
                after(dve, cx_done, b)
                dve.tensor_tensor_scan(A[:].rearrange("p d h j -> p (d h j)"), CX[:].rearrange("p d h j -> p (d h j)"),
                                       PV[:].rearrange("p d h j -> p (d h j)"), 0.0, ALU.mult, ALU.add).then_inc(a_done, 1)
                after(dve, a_done, b)
                step.end()
            ring(dve, body, n=NBA)

        @block.scalar
        def _(act):
            act.wait_ge(set_done, 4)

            def body(b, s):
                after(act, d_done, b)
                act.activation(E[:], D[:], ACT.Exp, scale=scale).then_inc(exp_done, 1)
                after(act, exp_done, b)
                act.activation(CX[:, :, :, 1:S1], E[:, 1].unsqueeze(1).to_broadcast([P, D1, HEADS, BLK]), ACT.Copy)\
                    .then_inc(cx_done, 1)
                after(act, a_done, b)
                after_dma(act, stored, b - 1)
                act.activation(O[:, :, 0:D1 * HEADS], A[:, :, :, 1:S1].rearrange("p d h j -> p j (d h)"), ACT.Copy)\
                    .then_inc(o1_done, 1)
                act.activation(O[:, :, D1 * HEADS:], M[:, :, 1:S1].rearrange("p h j -> p j h"), ACT.Copy).then_inc(o_done, 1)
            ring(act, body, n=NBA)


def join_lanes(nc, k, table, length, last_node, first_node, H, D1, scale, incoming, tag):
    W = (D1 + 1) * H if H else D1
    with ExitStack() as c:
        sb = lambda name, shape, dt=F32: c.enter_context(nc.sbuf_tensor(name + tag, shape, dt))
        sem = semaphores(nc, c, after=tag)
        ends, inc, none = sb("j_ends", [P, W]), sb("j_inc", [P, W]), sb("j_none", [1, W])
        diag, mask, mbias = sb("j_diag", [P, P]), sb("j_mask", [P, P]), sb("j_mbias", [P, P])
        X, Wt = sb("j_X", [P, P]), sb("j_Wt", [P, P])
        mx = sb("j_mx", [P, 1])
        ps = c.enter_context(nc.psum_tensor("j_ps" + tag, [P, 512], F32))
        psW = c.enter_context(nc.psum_tensor("j_psW" + tag, [P, 512], F32))
        psV = c.enter_context(nc.psum_tensor("j_psV" + tag, [P, 512], F32))
        ends_in, step, exp_done, spread, turned, joined, stored, pool_set = (sem("j_" + n) for n in (
            "ends_in", "step", "exp_done", "spread", "turned", "joined", "stored", "pool_set"))
        diag_done, wt_done, x_done, wm_done, inc_done = (sem("j_" + n) for n in ("diag_done", "wt_done", "x_done", "wm_done", "inc_done"))
        block = c.enter_context(nc.Block())
        heads = max(H, 1)

        @block.sync
        def _(sp):
            sp.dma_start(ends[:], table.rearrange("(p i) f -> p i f", i=length)[:, length - 1, :]).then_inc(ends_in, 16)
            sp.wait_ge(pool_set, 2 if H else 1)
            sp.dma_start(incoming[P:P + 1, :], none[:]).then_inc(stored, 16)
            sp.wait_ge(inc_done, heads)
            sp.dma_start(incoming[0:P, :], inc[:]).then_inc(stored, 16)
            sp.wait_ge(stored, 32)

        @block.gpsimd
        def _(pool):
            pool.memset(none[:], 0.0).then_inc(pool_set, 1)
            if H:
                pool.wait_ge(pool_set, 1)
                pool.memset(none[:, D1 * H:], -BIG).then_inc(pool_set, 1)

        @block.vector
        def _(dve):
            link = Chain(dve, step, None)
            link.start_once()
            dve.tensor_scalar(diag[:], k.ident[:], last_node, None, ALU.mult).then_inc(diag_done, 1)
            dve.wait_ge(spread, 1)
            link(dve.scalar_tensor_tensor(out=mask[:], in0=ps[:, 0:P], scalar=first_node, in1=k.low[:],
                                          op0=ALU.is_equal, op1=ALU.mult))
            link(dve.tensor_scalar(mbias[:], mask[:], -1.0, BIG, ALU.add, ALU.mult))
            dve.wait_ge(ends_in, 16)
            for h in range(heads):
                if H:
                    m = D1 * H + h
                    dve.tensor_scalar(diag[:], k.ident[:], ends[:, m:m + 1], None, ALU.mult).then_inc(diag_done, 1)
                    dve.wait_ge(spread, h + 2)
                    link(dve.tensor_tensor(X[:], ps[:, 0:P], mbias[:], ALU.add))
                    link(dve.tensor_reduce(mx[:], X[:], AX.X, ALU.max))
                    link(dve.tensor_copy(inc[:, m:m + 1], mx[:]))
                    dve.tensor_scalar(X[:], X[:], mx[:, 0:1], None, ALU.subtract).then_inc(x_done, 1)
                    dve.wait_ge(exp_done, h + 1)
                    dve.tensor_tensor(X[:], X[:], mask[:], ALU.mult).then_inc(wm_done, 1)
                else:
                    dve.tensor_copy(X[:], mask[:]).then_inc(wm_done, 1)
                dve.wait_ge(turned, h + 1)
                dve.tensor_copy(Wt[:], psW[:, 0:P]).then_inc(wt_done, 1)
                dve.wait_ge(joined, h + 1)
                if H:
                    dve.tensor_copy(inc[:, 0:D1 * H].rearrange("p (d h) -> p d h", h=H)[:, :, h], psV[:, 0:D1]).then_inc(inc_done, 1)
                else:
                    dve.tensor_copy(inc[:], psV[:, 0:D1]).then_inc(inc_done, 1)

        @block.scalar
        def _(act):
            if H:
                for h in range(H):
                    act.wait_ge(x_done, h + 1)
                    act.activation(X[:], X[:], ACT.Exp, scale=scale).then_inc(exp_done, 1)

        @block.tensor
        def _(pe):
            pe.wait_ge(diag_done, 1)
            pe.matmul(ps[:, 0:P], k.ones[:], diag[:], start=True, stop=True).then_inc(spread, 1)
            for h in range(heads):
                if H:
                    pe.wait_ge(diag_done, h + 2)
                    pe.matmul(ps[:, 0:P], k.ones[:], diag[:], start=True, stop=True).then_inc(spread, 1)
                pe.wait_ge(wm_done, h + 1)
                pe.transpose(psW[:, 0:P], X[:], k.ident[:]).then_inc(turned, 1)
                pe.wait_ge(wt_done, h + 1)
                if h == 0:
                    pe.wait_ge(ends_in, 16)
                rhs = ends[:, 0:D1 * H].rearrange("p (d h) -> p d h", h=H)[:, :, h] if H else ends[:]
                pe.matmul(psV[:, 0:D1], Wt[:], rhs, start=True, stop=True).then_inc(joined, 1)


def attention_output(nc, k, w):
    scale = float(DK) ** -0.5
    D1 = DK + 1
    W = (D1 + 1) * HEADS
    with ExitStack() as c:
        sb = lambda name, shape, dt=F32: c.enter_context(nc.sbuf_tensor(name, shape, dt))
        sem = semaphores(nc, c)
        wo = sb("b_wo", [P, KC, C])
        idx = sb("b_idx", [P, 2, 2], I32)
        r = sb("b_r", [P, 2, 2, W])
        xm = sb("b_xm", [P, 2, C])
        Mx = sb("b_Mx", [P, HEADS])
        D = sb("b_D", [P, 2, HEADS])
        E = sb("b_E", [P, 2, HEADS])
        T = sb("b_T", [P, 2, D1, HEADS])
        U = sb("b_U", [P, D1, HEADS])
        rz = sb("b_rz", [P, HEADS])
        att = sb("b_att", [P, C])
        aT = sb("b_aT", [P, KC, P])
        xo = sb("b_xo", [P, C])
        psT = c.enter_context(nc.psum_tensor("b_psT", [P, KC, P], F32))
        psO = c.enter_context(nc.psum_tensor("b_psO", [P, 512], F32))
        w_in = sem("b_w_in")
        x_in = [sem("b_x_in0"), sem("b_x_in1")]
        r_in = [sem("b_r_in0"), sem("b_r_in1")]
        idx_done, step, d_done, e_done, att_done, ps_T, sb_T, ps_O, out_done, stored = (
            sem("b_" + n) for n in ("idx_done", "step", "d_done", "e_done", "att_done", "ps_T", "sb_T", "ps_O",
                                    "out_done", "stored"))
        block = c.enter_context(nc.Block())

        @block.sync
        def _(sp):
            prime(sp, [idx_done, d_done, e_done, att_done, ps_T, sb_T, ps_O, out_done], [(stored, 1)])
            sp.dma_start(wo[:], w["L0_gnn_Wo"].rearrange("(a p) n -> p a n", p=P)).then_inc(w_in, 16)

            def load(t, s):
                after(sp, out_done, t - 2)
                sp.dma_start(xm[:, s, :], rows(k.X1M, t)).then_inc(x_in[s], 16)

            def store(t, s):
                after(sp, out_done, t)
                sp.dma_start(rows(k.X1, t), xo[:]).then_inc(stored, 16)
            skewed(sp, load, store)
            after_dma(sp, stored, NT - 1)

        @block.gpsimd
        def _(pool):
            def gather(t, s):
                after(pool, idx_done, t)
                after(pool, att_done, t - 2)
                for g, (tab, width) in enumerate(((k.PT, W), (k.INC, W))):
                    pool.indirect_dma_start(r[:, s, g, :], None, tab,
                                            bass.IndirectOffsetOnAxis(ap=idx[:, s, g:g + 1], axis=0)).then_inc(r_in[s], 16)
            ring(pool, gather)

        @block.vector
        def _(dve):
            ch = Chain(dve, step, 5)

            def index(t, s):
                if not isinstance(t, int) or t >= 2:
                    loaded(dve, r_in[s], t - 2, s, per=2)
                dve.tensor_copy(idx[:, s, 0:1], k.pos_i[:, bass.ds(t, 1)])
                dve.tensor_copy(idx[:, s, 1:2], k.inc_i[:, bass.ds(t, 1)]).then_inc(idx_done, 1)

            def body(t, s):
                ch.start(t)
                loaded(dve, r_in[s], t, s, per=2)
                m = r[:, s, :, D1 * HEADS:]
                ch(dve.tensor_tensor(Mx[:], m[:, 0], m[:, 1], ALU.max))
                dve.tensor_tensor(D[:], m, Mx[:].unsqueeze(1).to_broadcast([P, 2, HEADS]), ALU.subtract).then_inc(d_done, 1)
                after(dve, e_done, t)
                v = r[:, s, :, 0:D1 * HEADS].rearrange("p g (d h) -> p g d h", h=HEADS)
                for g in range(2):
                    ins = dve.tensor_tensor(T[:, g], v[:, g], E[:, g].unsqueeze(1).to_broadcast([P, D1, HEADS]), ALU.mult)
                    ch(ins)
                ch(dve.tensor_tensor(U[:], T[:, 0], T[:, 1], ALU.add))
                ch(dve.reciprocal(rz[:], U[:, DK, :]))
                after(dve, ps_T, t - 1)
                dve.tensor_tensor(att[:].rearrange("p (d h) -> p d h", h=HEADS), U[:, 0:DK],
                                  rz[:].unsqueeze(1).to_broadcast([P, DK, HEADS]), ALU.mult).then_inc(att_done, 1)
                after(dve, ps_O, t)
                loaded(dve, x_in[s], t, s)
                after_dma(dve, stored, t - 1)
                dve.tensor_tensor(xo[:], xm[:, s, :], psO[:, 0:C], ALU.add).then_inc(out_done, 1)
                ch.end()
            index(0, 0)
            index(1, 1)
            body(0, 0)
            index(2, 0)
            body(1, 1)
            index(3, 1)
            with dve.Fori(1, NT // 2 - 1) as j:
                body(2 * j, 0)
                index(2 * j + 2, 0)
                body(2 * j + 1, 1)
                index(2 * j + 3, 1)
            body(NT - 2, 0)
            body(NT - 1, 1)

        @block.scalar
        def _(act):
            def body(t, s):
                after(act, d_done, t)
                act.activation(E[:], D[:], ACT.Exp, scale=scale).then_inc(e_done, 1)
                after(act, ps_T, t)
                after(act, ps_O, t - 1)
                act.activation(aT[:], psT[:], ACT.Copy).then_inc(sb_T, 1)
            ring(act, body)

        @block.tensor
        def _(pe):
            pe.wait_ge(w_in, 16)

            def body(t, s):
                after(pe, att_done, t)
                after(pe, sb_T, t - 1)
                for a in range(KC):
                    last = pe.transpose(psT[:, a, :], att[:, a * P:(a + 1) * P], k.ident[:])
                last.then_inc(ps_T, 1)
                after(pe, sb_T, t)
                after(pe, out_done, t - 1)
                for a in range(KC):
                    last = pe.matmul(psO[:, 0:C], aT[:, a, :], wo[:, a, :], start=(a == 0), stop=(a == KC - 1))
                last.then_inc(ps_O, 1)
            ring(pe, body)


GT = 5
NG = NT // GT
GW = GT * P
HALF = GW // 2


def after_step(eng, sem, g, per, i):
    wait_reg(eng, sem, g * per + i + 1 + PRIME)


def routed_ffn(nc, k, w, second, x_in_dram, x_out_dram):
    EX = 4 if second else 8
    MH = 16 if second else 8
    PH = EX // 2
    tag = "_f1" if second else "_f0"
    with ExitStack() as c:
        sb = lambda name, shape, dt=F32: c.enter_context(nc.sbuf_tensor(name + tag, shape, dt))
        sem = semaphores(nc, c, after=tag)
        w1 = sb("w1", [P, KC, MH * P])
        b1 = sb("b1", [P, MH])
        w2 = sb("w2", [P, MH, C] if second else [P, MH, EX, C])
        b2 = sb("b2", [P, EX, C])
        xg = sb("xg", [P, 2, GT, C])
        xn = sb("xn", [P, GT, C])
        xT = sb("xT", [P, KC, GW])
        H = sb("H", [P, 2, MH, GW])
        st, mv = sb("st", [P, GT, 6]), sb("mv", [P, GT, 2])
        ve, rstd = sb("ve", [P, GT]), sb("rstd", [P, GT])
        gate = sb("gate", [P, 2, GT, EX])
        if not second:
            wg, bg = sb("wg", [P, MH, EX]), sb("bg", [P, EX])
            L, X8, oh, cand = (sb(n, [P, GT, EX]) for n in ("L", "X8", "oh", "cand"))
            mx, sm, pr, mn = (sb(n, [P, GT]) for n in ("mx", "sm", "pr", "mn"))
            im = sb("im", [P, EX])
            psL = c.enter_context(nc.psum_tensor("psL" + tag, [P, GT, EX], F32))
        psT = c.enter_context(nc.psum_tensor("psT" + tag, [P, 2, KC, P], F32))
        psH = c.enter_context(nc.psum_tensor("psH" + tag, [P, 2, 512], F32))
        psY = c.enter_context(nc.psum_tensor("psY" + tag, [P, 2, 2, 512], F32))
        w_in, x_in = sem("w_in"), [sem("x_in0"), sem("x_in1")]
        var_ready, rstd_ready, xn_done, ln_step = sem("var_ready"), sem("rstd_ready"), sem("xn_done"), sem("ln_step")
        tp_done, tc_done, hp_done, h_done = sem("tp_done"), sem("tc_done"), sem("hp_done"), sem("h_done")
        lg_done, lx_done, le_done, gate_done, rt_step = (sem(n) for n in ("lg_done", "lx_done", "le_done", "gate_done", "rt_step"))
        y_done, yc_done, x_done, y_step, stored = (sem(n) for n in ("y_done", "yc_done", "x_done", "y_step", "stored"))
        im_done = sem("im_done")
        block = c.enter_context(nc.Block())
        rounds = [(0, 2), (2, 2), (4, 1)]
        TR, HS, YS = len(rounds), 2 * MH, 2 * GT

        def group(ap, g):
            return ap[bass.ds(g * GW, GW), :].rearrange("(i p) c -> p i c", p=P)

        @block.sync
        def _(sp):
            prime(sp, [var_ready, rstd_ready, xn_done, tp_done, tc_done, hp_done, h_done, lg_done, lx_done, le_done,
                       gate_done, y_done, yc_done, x_done], [(stored, GT)])
            if second:
                for e in range(EX):
                    sp.dma_start(w1[:, :, e * 2 * C:(e + 1) * 2 * C],
                                 w["L1_ffn_W1"][e].rearrange("(a p) n -> p a n", p=P)).then_inc(w_in, 16)
                    sp.dma_start(w2[:, e * 4:(e + 1) * 4, :],
                                 w["L1_ffn_W2"][e].rearrange("(m p) n -> p m n", p=P)).then_inc(w_in, 16)
                    sp.dma_start(b2[:, e, :], w["L1_ffn_b2"][e].partition_broadcast(P)).then_inc(w_in, 16)
                    sp.dma_start(b1[:, e * 4:(e + 1) * 4], w["L1_ffn_b1"][e].rearrange("(m p) -> p m", p=P),
                                 allow_slow_non_contiguous=True).then_inc(w_in, 16)
            else:
                sp.dma_start(w1[:], w["L0_ffn_W1"].rearrange("(a p) n -> p a n", p=P)).then_inc(w_in, 16)
                sp.dma_start(b1[:], w["L0_ffn_b1"].rearrange("(m p) -> p m", p=P),
                                 allow_slow_non_contiguous=True).then_inc(w_in, 16)
                sp.dma_start(wg[:], w["L0_ffn_Wg"].rearrange("(m p) e -> p m e", p=P)).then_inc(w_in, 16)
                sp.dma_start(bg[:], w["L0_ffn_bg"].partition_broadcast(P)).then_inc(w_in, 16)
                for e in range(EX):
                    sp.dma_start(w2[:, :, e, :], w["L0_ffn_Wd"][e].rearrange("(m p) n -> p m n", p=P)).then_inc(w_in, 16)
                    sp.dma_start(b2[:, e, :], w["L0_ffn_bd"][e].partition_broadcast(P)).then_inc(w_in, 16)

            def load(g, s):
                after_dma(sp, stored, g - 2, GT)
                sp.dma_start(xg[:, s], group(x_in_dram, g)).then_inc(x_in[s], 16)

            def store(g, s):
                after(sp, x_done, g)
                for i in range(GT):
                    if second and isinstance(g, int) and (g * GT + i + 1) * P > N:
                        left = N - (g * GT + i) * P
                        if left > 0:
                            sp.dma_start(x_out_dram[N - left:N, :], xg[0:left, s, i, :]).then_inc(stored, 16)
                    else:
                        sp.dma_start(x_out_dram[bass.ds(g * GW + i * P, P), :], xg[:, s, i, :]).then_inc(stored, 16)
            skewed(sp, load, store, n=NG)
            short = (NP - N) // P if second else 0
            sp.wait_ge(stored, 16 * GT * (NG + PRIME) - 16 * short)

        @block.gpsimd
        def _(pool):
            def power(g, s):
                after(pool, var_ready, g)
                pool.tensor_tensor(rstd[:], ve[:], k.neghalf[:].to_broadcast([P, GT]), ALU.pow).then_inc(rstd_ready, 1)
            if not second:
                pool.tensor_scalar(im[:], k.iota[:, 0:EX], float(-EX), None, ALU.add).then_inc(im_done, 1)
            ring(pool, power, n=NG)

        @block.vector
        def _(dve):
            ln = Chain(dve, ln_step, 2)
            rt = Chain(dve, rt_step, 9)
            yc = Chain(dve, y_step, GT * (2 * EX - 2))
            dve.wait_ge(w_in, 16 * (16 if second else 20))
            if not second:
                dve.wait_ge(im_done, 1)

            def bcast(ap):
                return ap.unsqueeze(2).to_broadcast([P, GT, EX])

            def head(g, s):
                ln.start(g)
                loaded(dve, x_in[s], g, s)
                for i in range(GT):
                    last = dve.bn_stats(st[:, i, :], xg[:, s, i, :])
                ln(last)
                for i in range(GT):
                    last = dve.bn_aggr(mv[:, i, :], st[:, i, :])
                ln(last)
                ln.end()
                dve.tensor_scalar(ve[:], mv[:, :, 1], LN_EPS, None, ALU.add).then_inc(var_ready, 1)
                after_step(dve, tp_done, g, TR, -1)
                after(dve, rstd_ready, g)
                for i in range(GT):
                    last = dve.tensor_scalar(xn[:, i, :], xg[:, s, i, :], mv[:, i, 0:1], rstd[:, i:i + 1],
                                             ALU.subtract, ALU.mult)
                last.then_inc(xn_done, 1)
                after(dve, xn_done, g)
                if second:
                    after(dve, x_done, g - 2)
                    dve.tensor_copy(gate[:, s], k.gate[:, bass.ds(g * GT, GT), :]).then_inc(gate_done, 1)
                    after(dve, gate_done, g)
                    return
                rt.start(g)
                after(dve, lg_done, g)
                rt(dve.tensor_tensor(L[:], psL[:], bg[:].unsqueeze(1).to_broadcast([P, GT, EX]), ALU.add))
                rt(dve.tensor_reduce(mx[:], L[:], AX.X, ALU.max))
                dve.tensor_tensor(X8[:], L[:], bcast(mx[:]), ALU.subtract).then_inc(lx_done, 1)
                rt(dve.tensor_tensor(oh[:], L[:], bcast(mx[:]), ALU.is_equal))
                rt(dve.tensor_tensor(cand[:], oh[:], im[:].unsqueeze(1).to_broadcast([P, GT, EX]), ALU.mult))
                rt(dve.tensor_reduce(mn[:], cand[:], AX.X, ALU.min))
                rt(dve.tensor_tensor(oh[:], im[:].unsqueeze(1).to_broadcast([P, GT, EX]), bcast(mn[:]), ALU.is_equal))
                after(dve, le_done, g)
                rt(dve.tensor_reduce(sm[:], X8[:], AX.X, ALU.add))
                rt(dve.reciprocal(pr[:], sm[:]))
                rt(dve.tensor_tensor(gate[:, s], oh[:], bcast(pr[:]), ALU.mult))
                rt.end()

            def tail(g, s):
                yc.start(g)
                for i in range(GT):
                    acc = xg[:, s, i, :]
                    for e in range(EX):
                        yc(dve.scalar_tensor_tensor(out=acc, in0=b2[:, e, :], scalar=gate[:, s, i, e:e + 1], in1=acc,
                                                    op0=ALU.mult, op1=ALU.add))
                    for h in range(2):
                        after_step(dve, y_done, g, YS, 2 * i + h)
                        for e in range(PH):
                            col = 512 * e if second else C * e
                            ins = dve.scalar_tensor_tensor(out=acc, in0=psY[:, h].rearrange("p b n -> p (b n)")[:, col:col + C],
                                                           scalar=gate[:, s, i, h * PH + e:h * PH + e + 1],
                                                           in1=acc, op0=ALU.mult, op1=ALU.add)
                            if e == PH - 1:
                                ins.then_inc(yc_done, 1)
                                after_step(dve, yc_done, g, YS, 2 * i + h)
                            else:
                                yc(ins)
                yc.end()
                dve.engine_nop().then_inc(x_done, 1)

            skewed(dve, head, tail, n=NG)

        @block.scalar
        def _(act):
            act.wait_ge(w_in, 16 * (16 if second else 20))

            def head(g, s):
                for r, (i0, n) in enumerate(rounds):
                    after_step(act, tp_done, g, TR, r)
                    if r == 0:
                        after_step(act, hp_done, g, HS, -1)
                    act.activation(xT[:, :, i0 * P:(i0 + n) * P].rearrange("p a (i n) -> p i a n", n=P), psT[:, 0:n], ACT.Copy)\
                        .then_inc(tc_done, 1)
                after(act, x_done, g - 2)
                for m in range(MH):
                    for h in range(2):
                        after_step(act, hp_done, g, HS, 2 * m + h)
                        act.activation(H[:, s, m, h * HALF:(h + 1) * HALF], psH[:, h, 0:HALF], ACT.Gelu,
                                       bias=b1[:, m:m + 1]).then_inc(h_done, 1)
                if not second:
                    after(act, lx_done, g)
                    act.activation(X8[:], X8[:], ACT.Exp).then_inc(le_done, 1)

            ring(act, head, n=NG)

        @block.tensor
        def _(pe):
            pe.wait_ge(w_in, 16 * (16 if second else 20))

            def head(g, s):
                after(pe, xn_done, g)
                for r, (i0, n) in enumerate(rounds):
                    after_step(pe, tc_done, g, TR, r - 1)
                    for i in range(n):
                        for a in range(KC):
                            last = pe.transpose(psT[:, i, a, :], xn[:, i0 + i, a * P:(a + 1) * P], k.ident[:])
                    last.then_inc(tp_done, 1)
                after_step(pe, tc_done, g, TR, TR - 1)
                for m in range(MH):
                    for h in range(2):
                        after_step(pe, h_done, g, HS, 2 * m + h - 2)
                        for a in range(KC):
                            last = pe.matmul(psH[:, h, 0:HALF], w1[:, a, m * P:(m + 1) * P], xT[:, a, h * HALF:(h + 1) * HALF],
                                             start=(a == 0), stop=(a == KC - 1))
                        last.then_inc(hp_done, 1)
                after_step(pe, h_done, g, HS, HS - 1)
                if not second:
                    after(pe, lx_done, g - 1)
                    for i in range(GT):
                        for m in range(MH):
                            last = pe.matmul(psL[:, i, :], H[:, s, m, i * P:(i + 1) * P], wg[:, m, :],
                                             start=(m == 0), stop=(m == MH - 1))
                    last.then_inc(lg_done, 1)

            def tail(g, s):
                for i in range(GT):
                    for h in range(2):
                        after_step(pe, yc_done, g, YS, 2 * i + h - 2)
                        for b in range(2):
                            if second:
                                e = 2 * h + b
                                for m in range(4):
                                    last = pe.matmul(psY[:, h, b, 0:C], H[:, s, 4 * e + m, i * P:(i + 1) * P],
                                                     w2[:, 4 * e + m, :], start=(m == 0), stop=(m == 3))
                            else:
                                e = 4 * h + 2 * b
                                for m in range(MH):
                                    last = pe.matmul(psY[:, h, b, :], H[:, s, m, i * P:(i + 1) * P],
                                                     w2[:, m, e:e + 2, :].rearrange("p e n -> p (e n)"),
                                                     start=(m == 0), stop=(m == MH - 1))
                        last.then_inc(y_done, 1)
            skewed(pe, head, tail, n=NG)


def normed_nodes(nc, k, w):
    CA = C + 1
    with ExitStack() as c:
        sb = lambda name, shape, dt=F32: c.enter_context(nc.sbuf_tensor("n_" + name, shape, dt))
        sem = semaphores(nc, c, before="n_")
        xt = sb("xt", [P, 2, C])
        xn = sb("xn", [P, CA])
        xm = sb("xm", [P, CA])
        st, mv, ve, rstd = sb("st", [P, 6]), sb("mv", [P, 2]), sb("ve", [P, 1]), sb("rstd", [P, 1])
        psG = [c.enter_context(nc.psum_tensor(f"n_psG{a}", [P, 512], F32)) for a in range(3)]
        x_in = [sem("x_in0"), sem("x_in1")]
        set_done, var_ready, rstd_ready, xn_done, xm_done, acc_done, stored, ln_step, fin = (sem(n) for n in (
            "set_done", "var_ready", "rstd_ready", "xn_done", "xm_done", "acc_done", "stored", "ln_step", "fin"))
        block = c.enter_context(nc.Block())

        @block.sync
        def _(sp):
            prime(sp, [var_ready, rstd_ready, xn_done, xm_done, acc_done], [(stored, 1)])

            def load(t, s):
                after(sp, xn_done, t - 2)
                sp.dma_start(xt[:, s, :], rows(k.X2, t)).then_inc(x_in[s], 16)

            def store(t, s):
                after(sp, xn_done, t)
                sp.dma_start(rows(k.XN2, t), xn[:, 0:C]).then_inc(stored, 16)
            skewed(sp, load, store)
            after_dma(sp, stored, NT - 1)

        @block.gpsimd
        def _(pool):
            def power(t, s):
                after(pool, var_ready, t)
                pool.tensor_tensor(rstd[:], ve[:], k.neghalf[:], ALU.pow).then_inc(rstd_ready, 1)
            ring(pool, power)

        @block.vector
        def _(dve):
            ln = Chain(dve, ln_step, 2)
            dve.memset(xn[:, C:CA], 1.0).then_inc(set_done, 1)
            dve.wait_ge(set_done, 1)

            def free(t):
                after_dma(dve, stored, t - 1)
                after(dve, acc_done, t - 1)

            def body(t, s):
                ln.start(t)
                loaded(dve, x_in[s], t, s)
                layernorm_dve(dve, ln, xt[:, s, :], xn[:, 0:C], st, mv, ve, rstd, var_ready, rstd_ready, xn_done, t,
                              lambda: free(t))
                ln.end()
                dve.tensor_scalar(xm[:], xn[:], k.valid[:, bass.ds(t, 1)], None, ALU.mult).then_inc(xm_done, 1)
                after(dve, xm_done, t)
            ring(dve, body)
            after(dve, acc_done, NT - 1)
            dve.tensor_copy(k.gram[:, 0, :], psG[0][:, 0:CA])
            dve.tensor_copy(k.gram[:, 1, :], psG[1][:, 0:CA])
            dve.tensor_copy(k.gramr[:], psG[2][0:1, 0:CA]).then_inc(fin, 1)
            dve.wait_ge(fin, 1)

        @block.tensor
        def _(pe):
            pe.wait_ge(set_done, 1)
            for a in range(3):
                pe.matmul(psG[a][:, 0:P], k.zero1[:], k.ones[0:1, :], start=True, stop=True)
                pe.matmul(psG[a][:, P:2 * P], k.zero1[:], k.ones[0:1, :], start=True, stop=True)
                pe.matmul(psG[a][:, 2 * P:3 * P], k.zero1[:], k.ones[0:1, :], start=True, stop=True)

            def body(t, s):
                after(pe, xm_done, t)
                for a in range(KC):
                    pe.matmul(psG[a][:, 0:CA], xm[:, a * P:(a + 1) * P], xn[:], start=False, stop=False, skip_group_check=True)
                pe.matmul(psG[2][0:1, 0:CA], xm[:, C:CA], xn[:], start=False, stop=False, skip_group_check=True)\
                    .then_inc(acc_done, 1)
            ring(pe, body)


def fold_second_layer(nc, k, w):
    CA = C + 1
    with ExitStack() as c:
        sb = lambda name, shape, dt=F32: c.enter_context(nc.sbuf_tensor("g_" + name, shape, dt))
        sem = semaphores(nc, c, before="g_")
        raw = {n: sb("raw_" + n, [P, KC, C]) for n in ("Wq", "Wk", "Wv", "Wfc")}
        T = {n: sb("T_" + n, [P, KC, C]) for n in ("Wk", "Wv", "Wfc")}
        brow = sb("brow", [1, 2, C])
        bq = sb("bq", [P, KC])
        bsum = sb("bsum", [1, 2, C])
        wl, wr = sb("wl", [P, KC, C]), sb("wr", [P, KC, C])
        GK, gkr = sb("GK", [P, KC, C]), sb("gkr", [1, C])
        PT, M2 = sb("PT", [P, KC, C]), sb("M2", [P, KC, C])
        br = sb("br", [1, C])
        wg = sb("wg", [P, KC, 16])
        att = sb("att", [P, 2, 16])
        prod = sb("prod", [P, KC, 16])
        gi, pi = sb("gi", [P, C], I32), sb("pi", [P, KC], I32)
        gf, pf = sb("gf", [P, C]), sb("pf", [P, KC])
        ps = [c.enter_context(nc.psum_tensor(f"g_ps{a}", [P, KC, C], F32)) for a in range(3)]
        psr = c.enter_context(nc.psum_tensor("g_psr", [P, 512], F32))
        w_in, iota_done, step, turned, turned_sb, mm, mm_sb = (sem(n) for n in (
            "w_in", "iota_done", "step", "turned", "turned_sb", "mm", "mm_sb"))
        block = c.enter_context(nc.Block())
        n_loads = 4 + 2 + 1 + 2 + 3 + 1 + 2

        @block.sync
        def _(sp):
            for n in raw:
                sp.dma_start(raw[n][:], w["L1_mix_" + n].rearrange("(a p) n -> p a n", p=P)).then_inc(w_in, 16)
            sp.dma_start(brow[:, 0, :], row_of(w["L1_mix_bk"])).then_inc(w_in, 16)
            sp.dma_start(brow[:, 1, :], row_of(w["L1_mix_bv"])).then_inc(w_in, 16)
            sp.dma_start(bq[:], w["L1_mix_bq"].rearrange("(a p) -> p a", p=P),
                         allow_slow_non_contiguous=True).then_inc(w_in, 16)
            sp.dma_start(bsum[:, 0, :], row_of(w["L1_mix_bfc"])).then_inc(w_in, 16)
            sp.dma_start(bsum[:, 1, :], row_of(w["L1_gnn_b_left"])).then_inc(w_in, 16)
            sp.dma_start(wl[:], w["L1_gnn_W_left"][0:C, :].rearrange("(a p) n -> p a n", p=P)).then_inc(w_in, 16)
            sp.dma_start(k.WN[:], w["L1_gnn_W_left"][C:2 * C, :].rearrange("(a p) n -> p a n", p=P)).then_inc(w_in, 16)
            sp.dma_start(wr[:], w["L1_gnn_W_right"].rearrange("(a p) n -> p a n", p=P)).then_inc(w_in, 16)
            sp.dma_start(wg[:], w["L1_ffn_W_gat"].rearrange("(a p) n -> p a n", p=P)).then_inc(w_in, 16)
            for i, n in enumerate(("L1_ffn_att_src", "L1_ffn_att_dst")):
                sp.dma_start(att[:, i, :], w[n].rearrange("h e -> (h e)").partition_broadcast(P)).then_inc(w_in, 16)

        @block.gpsimd
        def _(pool):
            pool.iota(gi[:], [[1, C]], 0, 0).then_inc(iota_done, 1)
            pool.iota(pi[:], [[P, KC]], 0, 1).then_inc(iota_done, 1)

        @block.vector
        def _(dve):
            link = Chain(dve, step, None)
            link.start_once()
            dve.wait_ge(iota_done, 2)
            link(dve.tensor_scalar(gi[:], gi[:], 5, None, ALU.logical_shift_right))
            link(dve.tensor_scalar(pi[:], pi[:], 5, None, ALU.logical_shift_right))
            link(dve.tensor_copy(gf[:], gi[:]))
            link(dve.tensor_copy(pf[:], pi[:]))
            dve.wait_ge(w_in, 16 * n_loads)
            for a in range(KC):
                link(dve.tensor_copy(k.WG[:, a, 0:16].rearrange("p (e h) -> p e h", h=4),
                                     wg[:, a, :].rearrange("p (h e) -> p e h", e=4)))
            for i in range(2):
                link(dve.tensor_tensor(prod[:], wg[:], att[:, i, :].unsqueeze(1).to_broadcast([P, KC, 16]), ALU.mult))
                link(dve.tensor_reduce(k.WG[:, :, 16 + 4 * i:20 + 4 * i], prod[:].rearrange("p a (h e) -> p a h e", e=4), AX.X, ALU.add))
            for i, n in enumerate(T):
                dve.wait_ge(turned, i + 1)
                dve.tensor_copy(T[n][:], ps[i][:]).then_inc(turned_sb, 1)
            dve.wait_ge(mm, 1)
            dve.tensor_copy(GK[:], ps[0][:])
            dve.tensor_copy(gkr[:], psr[0:1, 0:C]).then_inc(mm_sb, 1)
            dve.wait_ge(mm, 2)
            for a in range(KC):
                link(dve.tensor_scalar(PT[:, a, :], gf[:], pf[:, a:a + 1], 1.0 / N, ALU.is_equal, ALU.mult))
            dve.tensor_tensor(PT[:], PT[:], ps[1][:], ALU.mult).then_inc(mm_sb, 1)
            dve.wait_ge(mm, 3)
            dve.tensor_copy(M2[:], ps[2][:]).then_inc(mm_sb, 1)
            link(dve.tensor_tensor(wl[:], wl[:], wr[:], ALU.add))
            link(dve.tensor_tensor(br[:], bsum[:, 0, :], bsum[:, 1, :], ALU.add))
            dve.wait_ge(mm, 4)
            link(dve.tensor_tensor(k.WS[:], wl[:], ps[0][:], ALU.add))
            dve.tensor_tensor(br[:], br[:], psr[0:1, 0:C], ALU.add).then_inc(mm_sb, 1)
            dve.wait_ge(mm, 5)
            link(dve.tensor_copy(k.bias2[:], ps[1][:, 0, :]))

        @block.tensor
        def _(pe):
            pe.wait_ge(w_in, 16 * n_loads)
            for i, n in enumerate(T):
                for a in range(KC):
                    for b in range(KC):
                        last = pe.transpose(ps[i][:, a, b * P:(b + 1) * P], raw[n][:, b, a * P:(a + 1) * P], k.ident[:])
                last.then_inc(turned, 1)
            pe.wait_ge(turned_sb, 3)
            parts = [(k.gram[:, 0, :], T["Wk"][:, 0, :]), (k.gram[:, 1, :], T["Wk"][:, 1, :]), (k.gramr[:], brow[:, 0, :])]
            for o in range(3):
                dst, cols = (ps[0][:, o, :], slice(o * P, (o + 1) * P)) if o < KC else (psr[0:1, 0:C], slice(C, CA))
                for i, (g, wk) in enumerate(parts):
                    last = pe.matmul(dst, g[:, cols], wk, start=(i == 0), stop=(i == 2))
            last.then_inc(mm, 1)
            pe.wait_ge(mm_sb, 1)
            parts = [(T["Wv"][:, 0, :], GK[:, 0, :]), (T["Wv"][:, 1, :], GK[:, 1, :]), (brow[:, 1, :], gkr[:])]
            for a in range(KC):
                for i, (v, gk) in enumerate(parts):
                    last = pe.matmul(ps[1][:, a, :], v[:, a * P:(a + 1) * P], gk, start=(i == 0), stop=(i == 2))
            last.then_inc(mm, 1)
            pe.wait_ge(mm_sb, 2)
            for a in range(KC):
                for b in range(KC):
                    last = pe.matmul(ps[2][:, a, :], PT[:, b, a * P:(a + 1) * P], T["Wfc"][:, b, :], start=(b == 0), stop=(b == KC - 1))
            last.then_inc(mm, 1)
            pe.wait_ge(mm_sb, 3)
            for a in range(KC):
                for b in range(KC):
                    pe.matmul(ps[0][:, a, :], raw["Wq"][:, b, a * P:(a + 1) * P], M2[:, b, :], start=(b == 0), stop=(b == KC - 1))
            for b in range(KC):
                last = pe.matmul(psr[0:1, 0:C], bq[:, b:b + 1], M2[:, b, :], start=(b == 0), stop=(b == KC - 1))
            last.then_inc(mm, 1)
            pe.wait_ge(mm_sb, 4)
            pe.matmul(ps[1][:, 0, :], k.ones[0:1, :], br[:], start=True, stop=True).then_inc(mm, 1)


SLE = 4


def edge_sums(nc, k):
    with ExitStack() as c:
        sb = lambda name, shape, dt=F32: c.enter_context(nc.sbuf_tensor("s_" + name, shape, dt))
        sem = semaphores(nc, c, before="s_")
        idx = sb("idx", [P, SLE, BLK], I32)
        x = sb("x", [P, SLE, BLK, C])
        same = sb("same", [P, BLK])
        carry = sb("carry", [P, C])
        idx_in = [sem(f"idx_in{s}") for s in range(SLE)]
        x_in = [sem(f"x_in{s}") for s in range(SLE)]
        stored = [sem(f"stored{s}") for s in range(SLE)]
        step, sums_done, set_done, carried = sem("step"), sem("sums_done"), sem("set_done"), sem("carried")
        block = c.enter_context(nc.Block())
        ps = k.PS.rearrange("(p i) f -> p i f", i=LA)

        @block.sync
        def _(sp):
            prime(sp, [sums_done, carried])

            def fetch(b, s):
                after(sp, carried, b - SLE)
                sp.dma_start(idx[:, s, :], k.srci[:, bass.ds(b * BLK, BLK)]).then_inc(idx_in[s], 16)
            ring(sp, fetch, n=NBA, slots=SLE)

        @block.scalar
        def _(act):
            def store(b, s):
                after(act, sums_done, b)
                act.dma_start(ps[:, bass.ds(b * BLK, BLK), :], x[:, s]).then_inc(stored[s], 16)
            ring(act, store, n=NBA, slots=SLE)
            for s in range(SLE):
                act.wait_ge(stored[s], 16 * (NBA // SLE))

        @block.gpsimd
        def _(pool):
            def gather(b, s, free=True):
                loaded(pool, idx_in[s], b, s, slots=SLE)
                if free:
                    wait_reg(pool, stored[s], (b - s) * (16 // SLE))
                for j in range(BLK):
                    pool.indirect_dma_start(x[:, s, j, :], None, k.XN2,
                                            bass.IndirectOffsetOnAxis(ap=idx[:, s, j:j + 1], axis=0)).then_inc(x_in[s], 16)
            for s in range(SLE):
                gather(s, s, free=False)
            with pool.Fori(1, NBA // SLE) as i:
                for s in range(SLE):
                    gather(SLE * i + s, s)

        @block.vector
        def _(dve):
            ch = Chain(dve, step, BLK)
            dve.memset(carry[:], 0.0).then_inc(set_done, 1)
            dve.wait_ge(set_done, 1)

            def body(b, s):
                ch.start(b)
                ch(dve.tensor_copy(same[:], k.same[:, bass.ds(b * BLK, BLK)]))
                loaded(dve, x_in[s], b, s, per=BLK, slots=SLE)
                prev = carry[:]
                for j in range(BLK):
                    ins = dve.scalar_tensor_tensor(out=x[:, s, j, :], in0=prev, scalar=same[:, j:j + 1], in1=x[:, s, j, :],
                                                   op0=ALU.mult, op1=ALU.add)
                    prev = x[:, s, j, :]
                    if j < BLK - 1:
                        ch(ins)
                ins.then_inc(sums_done, 1)
                after(dve, sums_done, b)
                dve.tensor_copy(carry[:], prev).then_inc(carried, 1)
                after(dve, carried, b)
                ch.end()
            ring(dve, body, n=NBA, slots=SLE)


def second_layer_nodes(nc, k, w):
    with ExitStack() as c:
        sb = lambda name, shape, dt=F32: c.enter_context(nc.sbuf_tensor("m_" + name, shape, dt))
        sem = semaphores(nc, c, before="m_")
        idx = sb("idx", [P, 2, 2], I32)
        r = sb("r", [P, 2, 2, C])
        xn = sb("xn", [P, 2, C])
        x2 = sb("x2", [P, 2, C])
        rc = sb("rc", [P, NT])
        rsum, hn, xb, x3, x3n = sb("rsum", [P, C]), sb("hn", [P, C]), sb("xb", [P, C]), sb("x3", [P, C]), sb("x3n", [P, C])
        hT, yT = sb("hT", [P, 4, P]), sb("yT", [P, KC, P])
        st, mv, ve, rstd = sb("st", [P, 6]), sb("mv", [P, 2]), sb("ve", [P, 1]), sb("rstd", [P, 1])
        g = sb("g", [P, 24])
        psT = c.enter_context(nc.psum_tensor("m_psT", [P, 4, P], F32))
        psO = c.enter_context(nc.psum_tensor("m_psO", [P, 512], F32))
        psU = c.enter_context(nc.psum_tensor("m_psU", [P, KC, P], F32))
        psG = c.enter_context(nc.psum_tensor("m_psG", [P, 512], F32))
        x_in = [sem("x_in0"), sem("x_in1")]
        r_in = [sem("r_in0"), sem("r_in1")]
        names = ("idx_done", "hn_done", "xb_done", "ps_T", "sb_T", "ps_O", "x3_done", "var_ready", "rstd_ready", "xn_done",
                 "ps_U", "sb_U", "ps_G", "g_done")
        (idx_done, hn_done, xb_done, ps_T, sb_T, ps_O, x3_done, var_ready, rstd_ready, xn_done,
         ps_U, sb_U, ps_G, g_done) = tiles = [sem(n) for n in names]
        stored_x, stored_g, ln_step, step = sem("stored_x"), sem("stored_g"), sem("ln_step"), sem("step")
        rc_done = sem("rc_done")
        block = c.enter_context(nc.Block())

        @block.sync
        def _(sp):
            prime(sp, tiles, [(stored_x, 1), (stored_g, 1)])

            def load(t, s):
                after(sp, ps_T, t - 2)
                after(sp, xb_done, t - 2)
                sp.dma_start(xn[:, s, :], rows(k.XN2, t)).then_inc(x_in[s], 16)
                sp.dma_start(x2[:, s, :], rows(k.X2, t)).then_inc(x_in[s], 16)

            def store(t, s):
                after(sp, x3_done, t)
                sp.dma_start(rows(k.X3, t), x3[:]).then_inc(stored_x, 16)
                after(sp, g_done, t)
                sp.dma_start(rows(k.G, t), g[:]).then_inc(stored_g, 16)
            skewed(sp, load, store)
            after_dma(sp, stored_x, NT - 1)
            after_dma(sp, stored_g, NT - 1)

        @block.gpsimd
        def _(pool):
            def gather(t, s):
                after(pool, idx_done, t)
                after(pool, hn_done, t - 2)
                for i, tab in enumerate((k.PS, k.INS)):
                    pool.indirect_dma_start(r[:, s, i, :], None, tab,
                                            bass.IndirectOffsetOnAxis(ap=idx[:, s, i:i + 1], axis=0)).then_inc(r_in[s], 16)

            def power(t, s):
                after(pool, var_ready, t)
                pool.tensor_tensor(rstd[:], ve[:], k.neghalf[:], ALU.pow).then_inc(rstd_ready, 1)
            skewed(pool, gather, power)

        @block.vector
        def _(dve):
            ln = Chain(dve, ln_step, 2)
            ch = Chain(dve, step, 1)
            dve.tensor_scalar(rc[:], k.cnt[:], 1.0, None, ALU.max).then_inc(rc_done, 1)
            dve.wait_ge(rc_done, 1)
            dve.reciprocal(rc[:], rc[:]).then_inc(rc_done, 1)
            dve.wait_ge(rc_done, 2)

            def index(t, s):
                if not isinstance(t, int) or t >= 2:
                    loaded(dve, r_in[s], t - 2, s, per=2)
                dve.tensor_copy(idx[:, s, 0:1], k.pos_i[:, bass.ds(t, 1)])
                dve.tensor_copy(idx[:, s, 1:2], k.inc_i[:, bass.ds(t, 1)]).then_inc(idx_done, 1)

            def body(t, s):
                ch.start(t)
                ln.start(t)
                loaded(dve, r_in[s], t, s, per=2)
                ch(dve.tensor_tensor(rsum[:], r[:, s, 0, :], r[:, s, 1, :], ALU.add))
                after(dve, ps_T, t - 1)
                dve.tensor_scalar(hn[:], rsum[:], rc[:, bass.ds(t, 1)], None, ALU.mult).then_inc(hn_done, 1)
                loaded(dve, x_in[s], t, s, per=2)
                dve.tensor_tensor(xb[:], x2[:, s, :], k.bias2[:], ALU.add).then_inc(xb_done, 1)
                after(dve, xb_done, t)
                after(dve, ps_O, t)
                after_dma(dve, stored_x, t - 1)
                dve.tensor_tensor(x3[:], xb[:], psO[:, 0:C], ALU.add).then_inc(x3_done, 1)
                after(dve, x3_done, t)
                layernorm_dve(dve, ln, x3[:], x3n[:], st, mv, ve, rstd, var_ready, rstd_ready, xn_done, t,
                              lambda: after(dve, ps_U, t - 1))
                after(dve, ps_G, t)
                after_dma(dve, stored_g, t - 1)
                dve.tensor_copy(g[:], psG[:, 0:24]).then_inc(g_done, 1)
                ln.end()
                ch.end()
            index(0, 0)
            index(1, 1)
            body(0, 0)
            index(2, 0)
            body(1, 1)
            index(3, 1)
            with dve.Fori(1, NT // 2 - 1) as j:
                body(2 * j, 0)
                index(2 * j + 2, 0)
                body(2 * j + 1, 1)
                index(2 * j + 3, 1)
            body(NT - 2, 0)
            body(NT - 1, 1)

        @block.scalar
        def _(act):
            def body(t, s):
                after(act, ps_T, t)
                after(act, ps_O, t - 1)
                act.activation(hT[:], psT[:], ACT.Copy).then_inc(sb_T, 1)
                after(act, ps_U, t)
                after(act, ps_G, t - 1)
                act.activation(yT[:], psU[:], ACT.Copy).then_inc(sb_U, 1)
            ring(act, body)

        @block.tensor
        def _(pe):
            def body(t, s):
                loaded(pe, x_in[s], t, s, per=2)
                after(pe, sb_T, t - 1)
                for a in range(KC):
                    pe.transpose(psT[:, a, :], xn[:, s, a * P:(a + 1) * P], k.ident[:])
                after(pe, hn_done, t)
                for a in range(KC):
                    last = pe.transpose(psT[:, KC + a, :], hn[:, a * P:(a + 1) * P], k.ident[:])
                last.then_inc(ps_T, 1)
                after(pe, sb_T, t)
                after(pe, x3_done, t - 1)
                for a in range(4):
                    rhs = k.WS[:, a, :] if a < KC else k.WN[:, a - KC, :]
                    last = pe.matmul(psO[:, 0:C], hT[:, a, :], rhs, start=(a == 0), stop=(a == 3))
                last.then_inc(ps_O, 1)
                after(pe, xn_done, t)
                after(pe, sb_U, t - 1)
                for a in range(KC):
                    last = pe.transpose(psU[:, a, :], x3n[:, a * P:(a + 1) * P], k.ident[:])
                last.then_inc(ps_U, 1)
                after(pe, sb_U, t)
                after(pe, g_done, t - 1)
                for a in range(KC):
                    last = pe.matmul(psG[:, 0:24], yT[:, a, :], k.WG[:, a, :], start=(a == 0), stop=(a == KC - 1))
                last.then_inc(ps_G, 1)
            ring(pe, body)


EG = 131072
TG = EG // P
HG = 64
LG = EG // P + HG
HE = 4
SB = 8


def gat_count(nc, k, w):
    HB = 16
    with ExitStack() as c:
        sb = lambda name, shape, dt=F32: c.enter_context(nc.sbuf_tensor("c_" + name, shape, dt))
        sem = semaphores(nc, c, before="c_")
        nat_i, nat = sb("nat_i", [P, 2, TG], I32), sb("nat", [P, 2, TG])
        tmp_i = sb("tmp_i", [P, TG], I32)
        oh_lo, oh_hi = sb("oh_lo", [P, 2, HB, P], BF16), sb("oh_hi", [P, 2, HB, HG], BF16)
        psT = [c.enter_context(nc.psum_tensor(f"c_psT{i}", [P, TG], F32)) for i in range(2)]
        psC = c.enter_context(nc.psum_tensor("c_psC", [P, HG], F32))
        nat_in, step, nat_done, turned, ready, onehots, counted = (sem(n) for n in (
            "nat_in", "step", "nat_done", "turned", "ready", "onehots", "counted"))
        block = c.enter_context(nc.Block())

        @block.sync
        def _(sp):
            prime(sp, [onehots, counted])
            for i in range(2):
                sp.dma_start(nat_i[:, i, :].rearrange("i (b p) -> i b p", p=P),
                             w["L1_ffn_edge_index"][i].rearrange("(b i p) -> i b p", i=P, p=P)).then_inc(nat_in, 16)

        @block.tensor
        def _(pe):
            pe.wait_ge(nat_done, 2)
            for i in range(2):
                for b in range(TG // P):
                    last = pe.transpose(psT[i][:, b * P:(b + 1) * P], nat[:, i, b * P:(b + 1) * P], k.ident[:])
            last.then_inc(turned, 1)
            pe.matmul(psC[:], k.zero1[:], k.ones[0:1, 0:HG], start=True, stop=True)

            def body(b, s):
                after(pe, onehots, b)
                for j in range(HB):
                    last = pe.matmul(psC[:], oh_lo[:, s, j, :], oh_hi[:, s, j, :], start=False, stop=False,
                                     skip_group_check=True)
                last.then_inc(counted, 1)
            ring(pe, body, n=TG // HB)

        @block.vector
        def _(dve):
            link = Chain(dve, step, None)
            link.start_once()
            dve.wait_ge(nat_in, 32)
            dve.tensor_scalar(nat[:, 0, :], nat_i[:, 0, :], float(N - 1), None, ALU.min).then_inc(nat_done, 1)
            dve.tensor_copy(nat[:, 1, :], nat_i[:, 1, :]).then_inc(nat_done, 1)
            dve.wait_ge(turned, 1)
            for i in range(2):
                link(dve.tensor_copy(k.pair[:, :, i], psT[i][:]))
            link(dve.tensor_scalar(tmp_i[:], k.pair[:, :, 1], P - 1, None, ALU.bitwise_and))
            link(dve.tensor_copy(k.lo[:], tmp_i[:]))
            link(dve.tensor_scalar(tmp_i[:], k.pair[:, :, 1], 7, None, ALU.logical_shift_right))
            link(dve.tensor_copy(k.hi[:], tmp_i[:]))
            link(dve.tensor_copy(k.dcol[:], k.pair[:, :, 1]))

            def body(b, s):
                after(dve, counted, b - 2)
                dve.tensor_tensor(oh_lo[:, s], k.iota[:].unsqueeze(1).to_broadcast([P, HB, P]),
                                  k.lo[:, bass.ds(b * HB, HB)].unsqueeze(2).to_broadcast([P, HB, P]), ALU.is_equal)
                dve.tensor_tensor(oh_hi[:, s], k.iota[:, 0:HG].unsqueeze(1).to_broadcast([P, HB, HG]),
                                  k.hi[:, bass.ds(b * HB, HB)].unsqueeze(2).to_broadcast([P, HB, HG]), ALU.is_equal)\
                    .then_inc(onehots, 1)
            ring(dve, body, n=TG // HB)
            after(dve, counted, TG // HB - 1)
            link(dve.tensor_scalar(k.cnt2[:], psC[:], 1.0, None, ALU.add))


def gat_sort(nc, k, w):
    with ExitStack() as c:
        sb = lambda name, shape, dt=F32: c.enter_context(nc.sbuf_tensor("o_" + name, shape, dt))
        sem = semaphores(nc, c, before="o_")
        db = sb("db", [P, 2, SB * P], I32)
        dlo, dbf = sb("dlo", [P, SB * P], I32), sb("dbf", [P, 2, SB * P])
        ahead = sb("ahead", [P, SB * P])
        oht = sb("oht", [P, 2, SB, P])
        oh_lo, oh_hi = sb("oh_lo", [P, 2, SB, P], BF16), sb("oh_hi", [P, 2, SB, HG], BF16)
        dc = sb("dc", [P, SB])
        rank, prior = sb("rank", [P, 2, SB]), sb("prior", [P, SB])
        eq, sel = sb("eq", [P, SB, SB * P]), sb("sel", [P, SB, HG])
        base = sb("base", [P, HG])
        loops = sb("loops", [P, HG, 2], I32)
        nodes_i, nodes_f = sb("nodes_i", [P, HG], I32), sb("nodes_f", [P, HG])
        C_sb = sb("C_sb", [P, HG])
        pos, pay = sb("pos", [P, 2, SB], I32), sb("pay", [P, 2, SB, 2], I32)
        psC = c.enter_context(nc.psum_tensor("o_psC", [P, 512], F32))
        psR = c.enter_context(nc.psum_tensor("o_psR", [P, 2, SB, HG], F32))
        db_in = [sem("db_in0"), sem("db_in1")]
        scattered = [sem("scattered0"), sem("scattered1")]
        (setup, iota_done, hots_done, rank_step, rank_done, sel_step, sel_done, pos_done, ring_free, dbf_done, counted, c_sb,
         r_done, base_done, init_done) = (sem(n) for n in (
             "setup", "iota_done", "hots_done", "rank_step", "rank_done", "sel_step", "sel_done", "pos_done",
             "ring_free", "dbf_done", "counted", "c_sb", "r_done", "base_done", "init_done"))
        block = c.enter_context(nc.Block())
        nb = TG // SB
        nbl = HG // SB

        @block.sync
        def _(sp):
            prime(sp, [hots_done, rank_done, sel_done, pos_done, ring_free, dbf_done, counted, c_sb, r_done])

            def load(b, s):
                after(sp, hots_done, b - 2)
                after(sp, dbf_done, b - 2)
                sp.dma_start(db[:, s, :], w["L1_ffn_edge_index"][1, bass.ds(b * SB * P, SB * P)].partition_broadcast(P))\
                    .then_inc(db_in[s], 16)

            def relay(b, s):
                loaded(sp, scattered[s], b, s, per=SB)
                sp.sem_inc(ring_free, 1)
            load(0, 0)
            load(1, 1)
            with sp.Fori(0, nb // 2 - 1) as j:
                load(2 * j + 2, 0)
                relay(2 * j, 0)
                load(2 * j + 3, 1)
                relay(2 * j + 1, 1)
            for b in range(nb - 2, nb + nbl):
                relay(b, b % 2)

        @block.gpsimd
        def _(pool):
            pool.iota(nodes_i[:], [[P, HG]], 0, 1).then_inc(iota_done, 1)

            def scatter(b, s):
                after(pool, pos_done, b)
                for j in range(SB):
                    pool.indirect_dma_start(k.SD, bass.IndirectOffsetOnAxis(ap=pos[:, s, j:j + 1], axis=0),
                                            pay[:, s, j, :], None).then_inc(scattered[s], 16)
            ring(pool, scatter, n=nb + nbl)

        @block.vector
        def _(dve):
            link = Chain(dve, setup, None)
            link.start_once()
            dve.tensor_scalar(base[:], k.start2[:], 1.0, None, ALU.add).then_inc(base_done, 1)
            dve.wait_ge(iota_done, 1)
            link(dve.tensor_copy(loops[:, :, 1], nodes_i[:]))
            link(dve.tensor_scalar(nodes_f[:], nodes_i[:], float(N - 1), None, ALU.min))
            link(dve.tensor_copy(loops[:, :, 0], nodes_f[:]))
            link(dve.tensor_copy(k.start2_i[:], k.start2[:]))
            link(dve.memset(ahead[:, 0:(SB - 1) * P], 1.0))
            link(dve.tensor_copy(ahead[:, (SB - 1) * P:], k.low[:]))
            rk = Chain(dve, rank_step, 2)
            sl = Chain(dve, sel_step, 3)

            def head(b, s):
                rk.start(b)
                loaded(dve, db_in[s], b, s)
                after(dve, rank_done, b - 1)
                rk(dve.tensor_copy(dc[:], k.dcol[:, bass.ds(b * SB, SB)]))
                rk(dve.tensor_scalar(dlo[:], db[:, s, :], P - 1, None, ALU.bitwise_and))
                after(dve, sel_done, b - 2)
                after(dve, counted, b - 2)
                dve.tensor_scalar(oht[:, s].rearrange("p j e -> p (j e)"), dlo[:], k.part[:, 0:1], None, ALU.is_equal)
                dve.tensor_tensor(oh_lo[:, s], k.iota[:].unsqueeze(1).to_broadcast([P, SB, P]),
                                  k.lo[:, bass.ds(b * SB, SB)].unsqueeze(2).to_broadcast([P, SB, P]), ALU.is_equal)
                dve.tensor_tensor(oh_hi[:, s], k.iota[:, 0:HG].unsqueeze(1).to_broadcast([P, SB, HG]),
                                  k.hi[:, bass.ds(b * SB, SB)].unsqueeze(2).to_broadcast([P, SB, HG]), ALU.is_equal)\
                    .then_inc(hots_done, 1)
                after(dve, dbf_done, b)
                for j in range(SB):
                    n = (j + 1) * P
                    last = dve.scalar_tensor_tensor(out=eq[:, j, 0:n], in0=dbf[:, s, 0:n], scalar=dc[:, j:j + 1],
                                                    in1=ahead[:, SB * P - n:], op0=ALU.is_equal, op1=ALU.mult,
                                                    accum_out=rank[:, s, j:j + 1])
                last.then_inc(rank_done, 1)
                rk.end()

            def tail(b, s):
                sl.start(b)
                after(dve, r_done, b)
                sl(dve.tensor_tensor(sel[:], oh_hi[:, s], psR[:, s], ALU.mult))
                sl(dve.tensor_reduce(prior[:], sel[:], AX.X, ALU.add))
                after(dve, rank_done, b)
                dve.sem_inc(sel_done, 1)
                after(dve, ring_free, b - 2)
                dve.tensor_copy(pay[:, s], k.pair[:, bass.ds(b * SB, SB), :])
                sl(dve.tensor_tensor(pos[:, s, :], prior[:], rank[:, s, :], ALU.add))
                dve.sem_inc(pos_done, 1)
                sl.end()
            skewed(dve, head, tail, n=nb)

            def self_loops(b, s):
                sl.start(b)
                after(dve, ring_free, b - 2)
                sl(dve.memset(sel[:, 0, 0:1], 0.0))
                sl(dve.tensor_copy(pay[:, s], loops[:, bass.ds((b - nb) * SB, SB), :]))
                sl(dve.tensor_copy(pos[:, s, :], k.start2_i[:, bass.ds((b - nb) * SB, SB)]))
                dve.sem_inc(pos_done, 1)
                sl.end()
            ring(dve, self_loops, n=nb + nbl, first=nb)

        @block.scalar
        def _(act):
            act.wait_ge(init_done, 1)

            def convert(b, s):
                loaded(act, db_in[s], b, s)
                after(act, rank_done, b - 2)
                act.activation(dbf[:, s, :], db[:, s, :], ACT.Copy).then_inc(dbf_done, 1)

            def free_rows(b, s):
                after(act, counted, b - 1)
                act.activation(C_sb[:], psC[:, 0:HG], ACT.Copy).then_inc(c_sb, 1)
            skewed(act, convert, free_rows, n=nb)

        @block.tensor
        def _(pe):
            pe.wait_ge(base_done, 1)
            pe.matmul(psC[:, 0:HG], k.ident[:], base[:], start=True, stop=True).then_inc(init_done, 1)

            def body(b, s):
                after(pe, hots_done, b)
                after(pe, c_sb, b)
                after(pe, sel_done, b - 2)
                for j in range(SB):
                    last = pe.matmul(psR[:, s, j, :], oht[:, s, j, :], C_sb[:], start=True, stop=True)
                last.then_inc(r_done, 1)
                for j in range(SB):
                    last = pe.matmul(psC[:, 0:HG], oh_lo[:, s, j, :], oh_hi[:, s, j, :], start=False, stop=False,
                                     skip_group_check=True)
                last.then_inc(counted, 1)
            ring(pe, body, n=nb)


def gat_edges(nc, k):
    GB = 16
    R = 24
    with ExitStack() as c:
        sb = lambda name, shape, dt=F32: c.enter_context(nc.sbuf_tensor("t_" + name, shape, dt))
        sem = semaphores(nc, c, before="t_")
        sd = sb("sd", [P, LG, 2], I32)
        g = sb("g", [P, LG, R])
        z = sb("z", [P, LG * HE])
        e = sb("e", [P, HE, LG])
        same, bias = sb("same", [P, LG]), sb("bias", [P, LG])
        gn = sb("gn", [P, NT, R])
        gr = sb("gr", [P, 2, GB, R])
        idx = sb("idx", [P, 2, GB], I32)
        first_f, first_i, g0 = sb("first_f", [P, 1]), sb("first_i", [P, 1], I32), sb("g0", [P, R])
        sd_in, gn_in, zeroed, zero_st, placed, z_in, first_done, g0_in, moved, idx_done, step, e_done, x_done, p_done, stored = (
            sem(n) for n in ("sd_in", "gn_in", "zeroed", "zero_st", "placed", "z_in", "first_done", "g0_in", "moved",
                             "idx_done", "step", "e_done", "x_done", "p_done", "stored"))
        g_in = [sem("g_in0"), sem("g_in1")]
        block = c.enter_context(nc.Block())
        nb = LG // GB
        pz = z[:].rearrange("p (h i) -> p h i", h=HE)

        @block.sync
        def _(sp):
            prime(sp, [moved, idx_done])
            sp.dma_start(sd[:], k.SD.rearrange("(p i) f -> p i f", i=LG)).then_inc(sd_in, 16)
            sp.dma_start(gn[:], k.G.rearrange("(t p) f -> p t f", p=P)).then_inc(gn_in, 16)
            sp.wait_ge(zeroed, 1)
            sp.dma_start(k.ZD.rearrange("(p i) f -> p (i f)", i=LG), z[:]).then_inc(zero_st, 16)
            sp.wait_ge(zero_st, 16)
            sp.wait_ge(placed, 16 * NT)
            sp.dma_start(z[:], k.ZD.rearrange("(p i) f -> p (i f)", i=LG)).then_inc(z_in, 16)
            sp.wait_ge(p_done, 1)
            sp.dma_start(k.PG.rearrange("(p i) f -> p i f", i=LG), g[:]).then_inc(stored, 16)
            sp.wait_ge(stored, 16)

        @block.gpsimd
        def _(pool):
            pool.memset(z[:], 0.0).then_inc(zeroed, 1)
            pool.wait_ge(gn_in, 16)
            pool.wait_ge(zero_st, 16)
            for t in range(NT):
                pool.indirect_dma_start(k.ZD, bass.IndirectOffsetOnAxis(ap=k.start2_i[:, t:t + 1], axis=0),
                                        gn[:, t, 20:24], None).then_inc(placed, 16)
            pool.wait_ge(first_done, 1)
            pool.indirect_dma_start(g0[:], None, k.G, bass.IndirectOffsetOnAxis(ap=first_i[:], axis=0)).then_inc(g0_in, 16)

            def gather(b, s):
                after(pool, idx_done, b)
                after(pool, moved, b - 2)
                for j in range(GB):
                    pool.indirect_dma_start(gr[:, s, j, :], None, k.G,
                                            bass.IndirectOffsetOnAxis(ap=idx[:, s, j:j + 1], axis=0)).then_inc(g_in[s], 16)
            ring(pool, gather, n=nb)

        @block.vector
        def _(dve):
            link = Chain(dve, step, None)
            link.start_once()
            dve.wait_ge(sd_in, 16)
            link(dve.tensor_copy(bias[:], sd[:, :, 1]))
            link(dve.tensor_copy(k.first2[:], bias[:, 0:1]))
            link(dve.tensor_copy(k.last2[:], bias[:, LG - 1:LG]))
            link(dve.memset(same[:, 0:1], 0.0))
            link(dve.tensor_tensor(same[:, 1:LG], bias[:, 1:LG], bias[:, 0:LG - 1], ALU.is_equal))
            link(dve.tensor_scalar(bias[:], same[:], -1.0, BIG, ALU.add, ALU.mult))
            link(dve.tensor_scalar(first_f[:], k.first2[:], float(NP - 1), None, ALU.min))
            dve.tensor_copy(first_i[:], first_f[:]).then_inc(first_done, 1)

            def index(b, s):
                dve.tensor_copy(idx[:, s, :], sd[:, bass.ds(b * GB, GB), 0]).then_inc(idx_done, 1)

            def move(b, s):
                loaded(dve, g_in[s], b, s, per=GB)
                dve.tensor_copy(g[:, bass.ds(b * GB, GB), :], gr[:, s]).then_inc(moved, 1)
            index(0, 0)
            index(1, 1)
            with dve.Fori(0, nb // 2 - 1) as j:
                move(2 * j, 0)
                index(2 * j + 2, 0)
                move(2 * j + 1, 1)
                index(2 * j + 3, 1)
            move(nb - 2, 0)
            move(nb - 1, 1)
            after(dve, moved, nb - 1)
            dve.wait_ge(z_in, 16)
            dve.wait_ge(g0_in, 16)
            zi = z[:].rearrange("p (i h) -> p i h", h=HE)
            link(dve.tensor_copy(zi[:, 0, :], g0[:, 20:24]))
            for h in range(HE):
                link(dve.tensor_tensor_scan(e[:, h, :], same[:], zi[:, :, h], 0.0, ALU.mult, ALU.add))
            link(dve.tensor_tensor(e[:], e[:], g[:, :, 16:20].rearrange("p i h -> p h i"), ALU.add))
            link(dve.scalar_tensor_tensor(out=e[:], in0=e[:], scalar=0.2, in1=e[:], op0=ALU.mult, op1=ALU.max))
            for h in range(HE):
                link(dve.tensor_tensor_scan(g[:, :, 20 + h], bias[:], e[:, h, :], -BIG, ALU.add, ALU.max))
            M = g[:, :, 20:24].rearrange("p i h -> p h i")
            link(dve.tensor_tensor(pz, e[:], M, ALU.subtract))
            link(dve.memset(e[:, :, 0:1], -BIG))
            link(dve.tensor_tensor(e[:, :, 1:LG], M[:, :, 0:LG - 1], M[:, :, 1:LG], ALU.subtract))
            dve.tensor_tensor(e[:, :, 1:LG], e[:, :, 1:LG], bias[:, 1:LG].unsqueeze(1).to_broadcast([P, HE, LG - 1]), ALU.add)\
                .then_inc(e_done, 1)
            dve.wait_ge(x_done, 2)
            for x in range(HE):
                cols = g[:, :, x * HE:(x + 1) * HE].rearrange("p i h -> p h i")
                link(dve.tensor_tensor(cols, cols, pz, ALU.mult))
            for h in range(HE):
                for col in [x * HE + h for x in range(HE)]:
                    link(dve.tensor_tensor_scan(g[:, :, col], e[:, h, :], g[:, :, col], 0.0, ALU.mult, ALU.add))
                last = dve.tensor_tensor_scan(g[:, :, 16 + h], e[:, h, :], pz[:, h, :], 0.0, ALU.mult, ALU.add)
                if h < HE - 1:
                    link(last)
            last.then_inc(p_done, 1)

        @block.scalar
        def _(act):
            act.wait_ge(e_done, 1)
            act.activation(pz, pz, ACT.Exp).then_inc(x_done, 1)
            act.activation(e[:], e[:], ACT.Exp).then_inc(x_done, 1)


def gat_gates(nc, k, w):
    R = 24
    with ExitStack() as c:
        sb = lambda name, shape, dt=F32: c.enter_context(nc.sbuf_tensor("h_" + name, shape, dt))
        sem = semaphores(nc, c, before="h_")
        r = sb("r", [P, 2, NT, R])
        Mx = sb("Mx", [P, NT, HE])
        D = sb("D", [P, 2, NT, HE])
        T = sb("T", [P, 2, NT, 5 * HE])
        rz = sb("rz", [P, NT, HE])
        A, B = sb("A", [P, NT, 16]), sb("B", [P, NT, 16])
        vec, vecp = sb("vec", [P, 3, 16]), sb("vecp", [P, 3, 16])
        mean, var, rstd = sb("mean", [P, NT]), sb("var", [P, NT]), sb("rstd", [P, NT])
        s4, oh1, oh2, cand = sb("s4", [P, NT, HE]), sb("oh1", [P, NT, HE]), sb("oh2", [P, NT, HE]), sb("cand", [P, NT, HE])
        m1, m2, mn, ex, w1, w2 = (sb(n, [P, NT]) for n in ("m1", "m2", "mn", "ex", "w1", "w2"))
        im = sb("im", [P, HE])
        v_in, r_in, step, d_done, d_exp, var_done, rstd_done, x_done, x_exp = (sem(n) for n in (
            "v_in", "r_in", "step", "d_done", "d_exp", "var_done", "rstd_done", "x_done", "x_exp"))
        block = c.enter_context(nc.Block())

        @block.sync
        def _(sp):
            for i, n in enumerate(("L1_ffn_b_gat", "L1_ffn_ln_gamma", "L1_ffn_ln_beta")):
                sp.dma_start(vec[:, i, :], w[n].partition_broadcast(P)).then_inc(v_in, 16)

        @block.gpsimd
        def _(pool):
            for t in range(NT):
                for i, (tab, ix) in enumerate(((k.PG, k.pos2_i), (k.ING, k.inc2_i))):
                    pool.indirect_dma_start(r[:, i, t, :], None, tab,
                                            bass.IndirectOffsetOnAxis(ap=ix[:, t:t + 1], axis=0)).then_inc(r_in, 16)
            pool.wait_ge(var_done, 1)
            pool.tensor_tensor(rstd[:], var[:], k.neghalf[:].to_broadcast([P, NT]), ALU.pow).then_inc(rstd_done, 1)

        @block.scalar
        def _(act):
            act.wait_ge(d_done, 1)
            act.activation(D[:], D[:], ACT.Exp).then_inc(d_exp, 1)
            act.wait_ge(x_done, 1)
            act.activation(ex[:], ex[:], ACT.Exp).then_inc(x_exp, 1)

        @block.vector
        def _(dve):
            link = Chain(dve, step, None)
            link.start_once()
            dve.wait_ge(v_in, 48)
            link(dve.tensor_copy(vecp[:].rearrange("p v (e h) -> p v e h", h=HE), vec[:].rearrange("p v (h e) -> p v e h", e=HE)))
            link(dve.tensor_scalar(im[:], k.iota[:, 0:HE], float(-HE), None, ALU.add))
            dve.wait_ge(r_in, 16 * 2 * NT)
            m = r[:, :, :, 20:24]
            link(dve.tensor_tensor(Mx[:], m[:, 0], m[:, 1], ALU.max))
            link(dve.tensor_tensor(D[:, 0], m[:, 0], Mx[:], ALU.subtract))
            dve.tensor_tensor(D[:, 1], m[:, 1], Mx[:], ALU.subtract).then_inc(d_done, 1)
            dve.wait_ge(d_exp, 1)
            for i in range(2):
                link(dve.tensor_tensor(T[:, i].rearrange("p t (d h) -> p t d h", h=HE),
                                       r[:, i, :, 0:20].rearrange("p t (d h) -> p t d h", h=HE),
                                       D[:, i].unsqueeze(2).to_broadcast([P, NT, 5, HE]), ALU.mult))
            link(dve.tensor_tensor(T[:, 0], T[:, 0], T[:, 1], ALU.add))
            link(dve.tensor_scalar(rz[:], T[:, 0, :, 16:20], 1e-16, None, ALU.add))
            link(dve.reciprocal(rz[:], rz[:]))
            link(dve.tensor_tensor(A[:].rearrange("p t (e h) -> p t e h", h=HE),
                                   T[:, 0, :, 0:16].rearrange("p t (e h) -> p t e h", h=HE),
                                   rz[:].unsqueeze(2).to_broadcast([P, NT, HE, HE]), ALU.mult))

            def vector(i):
                return vecp[:, i, :].unsqueeze(1).to_broadcast([P, NT, 16])

            def over(ap, n):
                return ap.unsqueeze(2).to_broadcast([P, NT, n])
            link(dve.tensor_tensor(A[:], A[:], vector(0), ALU.add))
            link(dve.tensor_reduce(mean[:], A[:], AX.X, ALU.add))
            link(dve.tensor_scalar(mean[:], mean[:], 1.0 / 16, None, ALU.mult))
            link(dve.tensor_tensor(A[:], A[:], over(mean[:], 16), ALU.subtract))
            link(dve.tensor_tensor(B[:], A[:], A[:], ALU.mult))
            link(dve.tensor_reduce(var[:], B[:], AX.X, ALU.add))
            dve.tensor_scalar(var[:], var[:], 1.0 / 16, LN_EPS, ALU.mult, ALU.add).then_inc(var_done, 1)
            dve.wait_ge(rstd_done, 1)
            link(dve.tensor_tensor(A[:], A[:], over(rstd[:], 16), ALU.mult))
            link(dve.tensor_tensor(A[:], A[:], vector(1), ALU.mult))
            link(dve.tensor_tensor(A[:], A[:], vector(2), ALU.add))
            link(dve.tensor_reduce(s4[:], A[:].rearrange("p t (e h) -> p t e h", h=HE), AX.X, ALU.add))
            link(dve.tensor_scalar(s4[:], s4[:], 1.0 / HE, None, ALU.mult))

            def best(mx, oh):
                imb = im[:].unsqueeze(1).to_broadcast([P, NT, HE])
                link(dve.tensor_reduce(mx[:], s4[:], AX.X, ALU.max))
                link(dve.tensor_tensor(cand[:], s4[:], over(mx[:], HE), ALU.is_equal))
                link(dve.tensor_tensor(cand[:], cand[:], imb, ALU.mult))
                link(dve.tensor_reduce(mn[:], cand[:], AX.X, ALU.min))
                link(dve.tensor_tensor(oh[:], imb, over(mn[:], HE), ALU.is_equal))
            best(m1, oh1)
            link(dve.scalar_tensor_tensor(out=s4[:], in0=oh1[:], scalar=-BIG, in1=s4[:], op0=ALU.mult, op1=ALU.add))
            best(m2, oh2)
            dve.tensor_tensor(ex[:], m2[:], m1[:], ALU.subtract).then_inc(x_done, 1)
            dve.wait_ge(x_exp, 1)
            link(dve.tensor_scalar(w1[:], ex[:], 1.0, None, ALU.add))
            link(dve.reciprocal(w1[:], w1[:]))
            link(dve.tensor_tensor(w2[:], ex[:], w1[:], ALU.mult))
            link(dve.tensor_tensor(oh1[:], oh1[:], over(w1[:], HE), ALU.mult))
            link(dve.tensor_tensor(oh2[:], oh2[:], over(w2[:], HE), ALU.mult))
            link(dve.tensor_tensor(k.gate[:], oh1[:], oh2[:], ALU.add))


def program(nc, w, out, scratch):
    k = Core()
    with ExitStack() as c:
        sb = lambda name, shape, dt=F32: c.enter_context(nc.sbuf_tensor(name, shape, dt))
        k.ident, k.ones = sb("ident", [P, P]), sb("ones", [P, P])
        k.low, k.upper = sb("low", [P, P]), sb("upper", [P, P])
        k.neghalf, k.half = sb("neghalf", [P, 1]), sb("half", [P, 1])
        k.valid, k.nodef = sb("valid", [P, NT]), sb("nodef", [P, NT])
        k.iota, k.part = sb("iota", [P, P]), sb("part", [P, 1])
        k.zero1 = k.low[0:1, :]
        k.M1 = sb("M1", [P, KC, C])
        k.XP = scratch("XP", [NP, C])
        k.Q, k.KV, k.MV = scratch("Q", [NP, C]), scratch("KV", [NP, 2 * C]), scratch("MV", [NP, 2 * C])
        k.X1M, k.X1 = scratch("X1M", [NP, C]), scratch("X1", [NP, C])
        WA = (DK + 2) * HEADS
        k.PT, k.INC = scratch("PT", [P * LA, WA]), scratch("INC", [P + 1, WA])
        k.first, k.last = sb("first", [P, 1]), sb("last", [P, 1])
        k.cnt, k.start = sb("cnt", [P, NT]), sb("start", [P, NT])
        k.pos_i, k.inc_i = sb("pos_i", [P, NT], I32), sb("inc_i", [P, NT], I32)
        k.X2, k.XN2, k.X3 = scratch("X2", [NP, C]), scratch("XN2", [NP, C]), scratch("X3", [NP, C])
        k.PS, k.INS = scratch("PS", [P * LA, C]), scratch("INS", [P + 1, C])
        k.G = scratch("G", [NP, 24])
        k.gram, k.gramr = sb("gram", [P, KC, C + 1]), sb("gramr", [1, C + 1])
        k.WS, k.WN, k.WG = sb("WS", [P, KC, C]), sb("WN", [P, KC, C]), sb("WG", [P, KC, 24])
        k.bias2 = sb("bias2", [P, C])
        k.cnt2, k.start2 = sb("cnt2", [P, HG]), sb("start2", [P, HG])
        k.start2_i, k.pos2_i, k.inc2_i = (sb(n, [P, HG], I32) for n in ("start2_i", "pos2_i", "inc2_i"))
        k.first2, k.last2 = sb("first2", [P, 1]), sb("last2", [P, 1])
        k.gate = sb("kgate", [P, NT, HE])
        k.SD, k.ZD = scratch("SD", [P * LG, 2], I32), scratch("ZD", [P * LG, HE])
        k.PG, k.ING = scratch("PG", [P * LG, 24]), scratch("ING", [P + 1, 24])
        constants(nc, k, w["x"])
        with ExitStack() as ca:
            lane = lambda name, dt: ca.enter_context(nc.sbuf_tensor(name, [P, LA], dt))
            k.srci, k.dsti, k.same = lane("srci", I32), lane("dsti", I32), lane("same", F32)
            project_nodes(nc, k, w)
            mix_output(nc, k, w)
            lane_lists(nc, k, w)
            rank_nodes(nc, k, k.cnt[:], NT, LA, k.start[:], k.pos_i[:], k.inc_i[:], "_a")
            edge_attention(nc, k)
            join_lanes(nc, k, k.PT, LA, k.last[:, 0:1], k.first[:, 0:1], HEADS, DK + 1, float(DK) ** -0.5, k.INC, "_a")
            attention_output(nc, k, w)
            routed_ffn(nc, k, w, False, k.X1, k.X2)
            normed_nodes(nc, k, w)
            fold_second_layer(nc, k, w)
            edge_sums(nc, k)
            join_lanes(nc, k, k.PS, LA, k.last[:, 0:1], k.first[:, 0:1], 0, C, 1.0, k.INS, "_s")
            second_layer_nodes(nc, k, w)
        with ExitStack() as cg:
            k.pair = cg.enter_context(nc.sbuf_tensor("pair", [P, TG, 2], I32))
            k.lo, k.hi, k.dcol = (cg.enter_context(nc.sbuf_tensor(n, [P, TG], F32)) for n in ("glo", "ghi", "dcol"))
            gat_count(nc, k, w)
            rank_nodes(nc, k, k.cnt2[:], HG, LG, k.start2[:], k.pos2_i[:], k.inc2_i[:], "_g")
            gat_sort(nc, k, w)
        gat_edges(nc, k)
        join_lanes(nc, k, k.PG, LG, k.last2[:, 0:1], k.first2[:, 0:1], HE, 5, 1.0, k.ING, "_g")
        gat_gates(nc, k, w)
        routed_ffn(nc, k, w, True, k.X3, out)


_OUTS = [((N, C), "float32")]


def kernel(**inputs):
    import numpy as _np
    import concourse.bacc as _bacc
    from concourse import mybir as _mybir
    from concourse.bass_utils import run_bass_kernel_spmd as _run

    nc = _bacc.Bacc("TRN2", target_bir_lowering=False, num_devices=1)
    arrays, args = {}, {}
    for name in inputs:
        a = _np.ascontiguousarray(inputs[name])
        arrays[f"in_{name}_dram"] = a
        args[name] = nc.dram_tensor(f"in_{name}_dram", a.shape, _mybir.dt.from_np(a.dtype), kind="ExternalInput").ap()
    out = nc.dram_tensor("out_0_dram", (N, C), _mybir.dt.float32, kind="ExternalOutput").ap()

    def scratch(name, shape, dt=_mybir.dt.float32):
        return nc.dram_tensor(name, shape, dt, kind="Internal").ap()

    program(nc, args, out, scratch)
    r = _run(nc, [arrays], core_ids=[0])
    return r.results[0]["out_0_dram"]
```

```python
from contextlib import ExitStack

import numpy as np
import concourse.bass as bass
from concourse import mybir

ALU = mybir.AluOpType
ACT = mybir.ActivationFunctionType
F32 = mybir.dt.float32
BF16 = mybir.dt.bfloat16
I32 = mybir.dt.int32
AX = mybir.AxisListType

P = 128
N = 6250
C = 256
NT = 50
NP = NT * P
KC = C // P
LN_EPS = 1e-5
BIG = 1e30

PRIME = 4


def wait_reg(eng, sem, value):
    eng.wait_ge(sem, value)
    if not isinstance(value, int):
        eng.nop(nofuse=True)


def after(eng, sem, t):
    wait_reg(eng, sem, t + 1 + PRIME)


def after_dma(eng, sem, t, per=1):
    wait_reg(eng, sem, (t + 1 + PRIME) * (16 * per))


def loaded(eng, sem, t, s, per=1, slots=2):
    wait_reg(eng, sem, (t - s) * (16 * per // slots) + 16 * per)


class Chain:

    def __init__(self, eng, sem, per):
        self.eng, self.sem, self.per = eng, sem, per

    def start_once(self):
        self.base, self.k = 0, 0

    def start(self, t):
        self.base, self.k = t * self.per, 0

    def __call__(self, ins):
        self.k += 1
        ins.then_inc(self.sem, 1)
        wait_reg(self.eng, self.sem, self.base + self.k)

    def end(self):
        assert self.k == self.per, (self.k, self.per)


def skewed(eng, head, tail, n=NT):
    head(0, 0)
    with eng.Fori(0, n // 2 - 1) as j:
        head(2 * j + 1, 1)
        tail(2 * j, 0)
        head(2 * j + 2, 0)
        tail(2 * j + 1, 1)
    head(n - 1, 1)
    tail(n - 2, 0)
    tail(n - 1, 1)


def two_ahead(eng, head, tail, n=NT):
    head(0, 0)
    head(1, 1)
    with eng.Fori(0, n // 2 - 1) as j:
        head(2 * j + 2, 0)
        tail(2 * j, 0)
        head(2 * j + 3, 1)
        tail(2 * j + 1, 1)
    tail(n - 2, 0)
    tail(n - 1, 1)


def ring(eng, body, n=NT, slots=2, first=0):
    with eng.Fori(first // slots, n // slots) as j:
        for s in range(slots):
            body(slots * j + s, s)


def semaphores(nc, c, before="", after=""):
    held = []

    def sem(name):
        held.append(nc.alloc_semaphore(before + name + after))
        return held[-1]

    def clear():
        nc.clear_and_free_semaphores(held)
        nc.all_engine_barrier()
    c.callback(clear)
    return sem


class Core:
    pass


def rows(ap, t):
    return ap[bass.ds(t * P, P), :] if not isinstance(t, int) else ap[t * P:(t + 1) * P, :]


def row_of(ap):
    return ap.rearrange("(a n) -> a n", a=1)


def prime(sp, sems, dma_sems=()):
    for s in sems:
        sp.sem_inc(s, PRIME)
    for s, per in dma_sems:
        sp.sem_inc(s, 16 * PRIME * per)


def constants(nc, k, x):
    with ExitStack() as c:
        zeros = c.enter_context(nc.sbuf_tensor("zeros", [P, C], F32))
        node = c.enter_context(nc.sbuf_tensor("node", [P, NT], I32))
        itmp = c.enter_context(nc.sbuf_tensor("itmp", [P, P], I32))
        ipart = c.enter_context(nc.sbuf_tensor("ipart", [P, 1], I32))
        sem = semaphores(nc, c)
        s_set, s_copied, s_iota, s_mask = (sem(n) for n in ("const_set", "x_copied", "const_iota", "const_mask"))
        block = c.enter_context(nc.Block())

        @block.gpsimd
        def _(pool):
            pool.memset(zeros[:], 0.0).then_inc(s_set, 1)
            pool.memset(k.ident[:], 0.0).then_inc(s_set, 1)
            pool.memset(k.ones[:], 1.0).then_inc(s_set, 1)
            pool.memset(k.neghalf[:], -0.5).then_inc(s_set, 1)
            pool.memset(k.half[:], 0.5).then_inc(s_set, 1)
            pool.memset(k.low[:], 1.0).then_inc(s_set, 1)
            pool.memset(k.upper[:], 1.0).then_inc(s_set, 1)
            pool.wait_ge(s_set, 7)
            pool.affine_select(out=k.ident[:], in_=k.ident[:], compare_op=ALU.not_equal, fill=1.0,
                               base=0, pattern=[[-1, P]], channel_multiplier=1).then_inc(s_set, 1)
            pool.affine_select(out=k.low[:], in_=k.low[:], compare_op=ALU.is_gt, fill=0.0,
                               base=0, pattern=[[-1, P]], channel_multiplier=1).then_inc(s_set, 1)
            pool.affine_select(out=k.upper[:], in_=k.upper[:], compare_op=ALU.is_gt, fill=0.0,
                               base=0, pattern=[[1, P]], channel_multiplier=-1).then_inc(s_set, 1)
            pool.iota(node[:], [[P, NT]], 0, 1).then_inc(s_iota, 1)
            pool.iota(itmp[:], [[1, P]], 0, 0).then_inc(s_iota, 1)
            pool.iota(ipart[:], [[1, 1]], 0, 1).then_inc(s_iota, 1)
            pool.wait_ge(s_set, 10)

        @block.vector
        def _(dve):
            dve.wait_ge(s_iota, 3)
            dve.tensor_scalar(k.valid[:], node[:], float(N), None, ALU.is_lt).then_inc(s_mask, 1)
            dve.tensor_copy(k.nodef[:], node[:]).then_inc(s_mask, 1)
            dve.tensor_copy(k.iota[:], itmp[:]).then_inc(s_mask, 1)
            dve.tensor_copy(k.part[:], ipart[:]).then_inc(s_mask, 1)
            dve.wait_ge(s_mask, 4)

        @block.sync
        def _(sp):
            sp.dma_start(k.XP[0:N, :], x).then_inc(s_copied, 16)
            sp.wait_ge(s_set, 1)
            tail = NP - N
            sp.dma_start(k.XP[N:N + P, :], zeros[:]).then_inc(s_copied, 16)
            sp.dma_start(k.XP[N + P:NP, :], zeros[0:tail - P, :]).then_inc(s_copied, 16)
            sp.wait_ge(s_copied, 48)


def layernorm_dve(dve, link, xt, xn, st, mv, ve, rstd, var_ready, rstd_ready, xn_done, t, wait_xn_free):
    link(dve.bn_stats(st[:], xt))
    link(dve.bn_aggr(mv[:], st[:]))
    dve.tensor_scalar(ve[:], mv[:, 1:2], LN_EPS, None, ALU.add).then_inc(var_ready, 1)
    wait_xn_free()
    after(dve, rstd_ready, t)
    dve.tensor_scalar(xn, xt, mv[:, 0:1], rstd[:, 0:1], ALU.subtract, ALU.mult).then_inc(xn_done, 1)
    after(dve, xn_done, t)


def project_nodes(nc, k, w):
    W3 = 6 * C
    with ExitStack() as c:
        sb = lambda name, shape, dt=F32: c.enter_context(nc.sbuf_tensor(name, shape, dt))
        sem = semaphores(nc, c)
        wcat = sb("wcat", [P, KC, W3])
        bcat = sb("bcat", [P, W3])
        wout = sb("wout", [P, KC, C])
        xt = sb("xt", [P, 2, C])
        xn = sb("xn", [P, C])
        st, mv, ve, rstd = sb("st", [P, 6]), sb("mv", [P, 2]), sb("ve", [P, 1]), sb("rstd", [P, 1])
        xT = sb("xT", [P, KC, P])
        allp = sb("allp", [P, W3])
        mean = sb("mean", [P, 2])
        nmean = sb("nmean", [P, 2])
        sq = sb("sq", [P, 2, C])
        s2 = sb("s2", [P, 2])
        s2e = sb("s2e", [P, 2])
        r2 = sb("r2", [P, 2])
        q4s = sb("q4s", [P, 1])
        q4 = sb("q4", [P, 1])
        qn = sb("qn", [P, 1])
        qr = sb("qr", [P, 1])
        junk = sb("junk", [P, C])
        k2 = sb("k2", [P, C])
        k4 = sb("k4", [P, C])
        q2 = sb("q2", [P, C])
        kvT = sb("kvT", [P, KC, C])
        cn = sb("cn", [P, KC])
        cr = sb("cr", [P, KC])
        psT = c.enter_context(nc.psum_tensor("psT", [P, KC, P], F32))
        psP = c.enter_context(nc.psum_tensor("psP", [P, 3, 512], F32))
        psK = c.enter_context(nc.psum_tensor("psK", [P, KC, C], F32))
        psN = c.enter_context(nc.psum_tensor("psN", [P, 512], F32))
        psM = c.enter_context(nc.psum_tensor("psM", [P, KC, C], F32))
        w_in = sem("w_in")
        x_in = [sem("x_in0"), sem("x_in1")]
        var_ready, rstd_ready, xn_done = sem("var_ready"), sem("rstd_ready"), sem("xn_done")
        xT_ps, xT_sb, proj_done, evac_done = sem("xT_ps"), sem("xT_sb"), sem("proj_done"), sem("evac_done")
        mean_done, sq_done, q4_done, k2_done, k4_done = (sem(n) for n in
                                                         ("mean_done", "sq_done", "q4_done", "k2_done", "k4_done"))
        q2_done, acc_done = sem("q2_done"), sem("acc_done")
        stored_q, stored_kv, stored_m = sem("stored_q"), sem("stored_kv"), sem("stored_m")
        ln_step, mix_step, act_step = sem("ln_step"), sem("mix_step"), sem("act_step")
        kvT_sb, norm_sb, root_done, kvw_ps, fin = (sem(n) for n in
                                                       ("kvT_sb", "norm_sb", "root_done", "kvw_ps", "fin"))
        tiles = [var_ready, rstd_ready, xn_done, xT_ps, xT_sb, proj_done, evac_done, mean_done, sq_done,
                 q4_done, k2_done, k4_done, q2_done, acc_done]
        block = c.enter_context(nc.Block())

        @block.sync
        def _(sp):
            prime(sp, tiles, [(stored_q, 1), (stored_kv, 1), (stored_m, 2)])
            cols = [(w["L0_gnn_Wq"], 0, C), (w["L0_gnn_Wk"], C, C), (w["L0_gnn_Wv"], 2 * C, C),
                    (w["L0_mix_W_qkv"], 3 * C, 3 * C)]
            for src, o, n in cols:
                sp.dma_start(wcat[:, :, o:o + n], src.rearrange("(a p) n -> p a n", p=P)).then_inc(w_in, 16)
            for src, o, n in [(w["L0_gnn_bq"], 0, C), (w["L0_gnn_bk"], C, C), (w["L0_gnn_bv"], 2 * C, C),
                              (w["L0_mix_b_qkv"], 3 * C, 3 * C)]:
                sp.dma_start(bcat[:, o:o + n], src.partition_broadcast(P)).then_inc(w_in, 16)
            sp.dma_start(wout[:], w["L0_mix_W_out"].rearrange("(a p) n -> p a n", p=P)).then_inc(w_in, 16)

            def store(t, s):
                after(sp, evac_done, t)
                sp.dma_start(rows(k.Q, t), allp[:, 0:C]).then_inc(stored_q, 16)
                sp.dma_start(rows(k.KV, t), allp[:, C:3 * C]).then_inc(stored_kv, 16)
                sp.dma_start(rows(k.MV, t)[:, C:2 * C], allp[:, 5 * C:6 * C]).then_inc(stored_m, 16)
                after(sp, q2_done, t)
                sp.dma_start(rows(k.MV, t)[:, 0:C], q2[:]).then_inc(stored_m, 16)
            ring(sp, store)
            after_dma(sp, stored_q, NT - 1)
            after_dma(sp, stored_kv, NT - 1)
            after_dma(sp, stored_m, NT - 1, 2)

        @block.gpsimd
        def _(pool):
            def head(t, s):
                after(pool, xn_done, t - 2)
                pool.dma_start(xt[:, s, :], rows(k.XP, t)).then_inc(x_in[s], 16)
                after(pool, var_ready, t)
                pool.tensor_tensor(rstd[:], ve[:], k.neghalf[:], ALU.pow).then_inc(rstd_ready, 1)

            def tail(t, s):
                after(pool, sq_done, t)
                pool.tensor_tensor(q4[:], q4s[:], k.half[:], ALU.pow).then_inc(q4_done, 1)
            skewed(pool, head, tail)
            pool.wait_ge(norm_sb, 1)
            pool.tensor_tensor(cr[:], cn[:], k.half[:].to_broadcast([P, KC]), ALU.pow).then_inc(root_done, 1)

        @block.vector
        def _(dve):
            ln = Chain(dve, ln_step, 2)
            mix = Chain(dve, mix_step, 6)

            def head(t, s):
                ln.start(t)
                loaded(dve, x_in[s], t, s)
                layernorm_dve(dve, ln, xt[:, s, :], xn[:], st, mv, ve, rstd, var_ready, rstd_ready, xn_done,
                              t, lambda: after(dve, xT_ps, t - 1))
                ln.end()

            def tail(t, s):
                mix.start(t)
                after_dma(dve, stored_q, t - 1)
                after_dma(dve, stored_kv, t - 1)
                after_dma(dve, stored_m, t - 1, 2)
                after(dve, acc_done, t - 1)
                after(dve, proj_done, t)
                dve.tensor_tensor(allp[:], psP[:].rearrange("p a n -> p (a n)"), bcat[:], ALU.add).then_inc(evac_done, 1)
                after(dve, evac_done, t)
                mix(dve.tensor_reduce(mean[:], allp[:, 3 * C:5 * C].rearrange("p (a n) -> p a n", a=2), AX.X, ALU.add))
                dve.tensor_scalar(nmean[:], mean[:], -1.0 / C, None, ALU.mult).then_inc(mean_done, 1)
                after(dve, sq_done, t)
                mix(dve.tensor_scalar(s2e[:], s2[:], 1e-7, None, ALU.add))
                mix(dve.reciprocal(r2[:], s2e[:]))
                dve.tensor_scalar(k2[:], sq[:, 1, :], r2[:, 1:2], k.valid[:, bass.ds(t, 1)], ALU.mult, ALU.mult)\
                    .then_inc(k2_done, 1)
                after(dve, q4_done, t)
                mix(dve.tensor_scalar(qn[:], q4[:], r2[:, 0:1], 1e-12, ALU.mult, ALU.max))
                mix(dve.reciprocal(qr[:], qn[:]))
                mix(dve.tensor_scalar(qn[:], qr[:], r2[:, 0:1], None, ALU.mult))
                dve.tensor_scalar(q2[:], sq[:, 0, :], qn[:, 0:1], None, ALU.mult).then_inc(q2_done, 1)
                after(dve, k2_done, t)
                after(dve, q2_done, t)
                mix.end()
            dve.wait_ge(w_in, 16 * 9)
            skewed(dve, head, tail)
            after(dve, acc_done, NT - 1)
            dve.tensor_copy(kvT[:], psK[:]).then_inc(kvT_sb, 1)
            dve.tensor_copy(cn[:], psN[:, 0:KC]).then_inc(norm_sb, 1)
            dve.wait_ge(kvw_ps, 1)
            dve.wait_ge(root_done, 1)
            dve.tensor_scalar(cn[:], cr[:], 1e-12, float(np.sqrt(N)), ALU.max, ALU.mult).then_inc(fin, 1)
            dve.wait_ge(fin, 1)
            dve.reciprocal(cr[:], cn[:]).then_inc(fin, 1)
            dve.wait_ge(fin, 2)
            for a in range(KC):
                dve.tensor_scalar(k.M1[:, a, :], psM[:, a, :], cr[:, a:a + 1], None, ALU.mult).then_inc(fin, 1)
            dve.wait_ge(fin, 4)

        @block.scalar
        def _(act):
            step = Chain(act, act_step, 2)

            def head(t, s):
                after(act, xT_ps, t)
                after(act, proj_done, t - 1)
                act.activation(xT[:], psT[:], ACT.Copy).then_inc(xT_sb, 1)

            def tail(t, s):
                step.start(t)
                after(act, mean_done, t)
                after(act, q2_done, t - 1)
                step(act.activation(sq[:, 0, :], allp[:, 3 * C:4 * C], ACT.Square, bias=nmean[:, 0:1], accum_out=s2[:, 0:1]))
                step(act.activation(sq[:, 1, :], allp[:, 4 * C:5 * C], ACT.Square, bias=nmean[:, 1:2], accum_out=s2[:, 1:2]))
                act.activation(junk[:], sq[:, 0, :], ACT.Square, accum_out=q4s[:, 0:1]).then_inc(sq_done, 1)
                after(act, k2_done, t)
                after(act, acc_done, t - 1)
                after(act, sq_done, t)
                act.activation(k4[:], k2[:], ACT.Square).then_inc(k4_done, 1)
                step.end()
            skewed(act, head, tail)

        @block.tensor
        def _(pe):
            pe.wait_ge(w_in, 16 * 9)

            def head(t, s):
                after(pe, xn_done, t)
                after(pe, xT_sb, t - 1)
                for a in range(KC):
                    last = pe.transpose(psT[:, a, :], xn[:, a * P:(a + 1) * P], k.ident[:])
                last.then_inc(xT_ps, 1)
                after(pe, xT_sb, t)
                after(pe, evac_done, t - 1)
                for g in range(3):
                    for a in range(KC):
                        last = pe.matmul(psP[:, g, :], xT[:, a, :], wcat[:, a, g * 512:(g + 1) * 512],
                                         start=(a == 0), stop=(a == KC - 1))
                last.then_inc(proj_done, 1)

            def tail(t, s):
                after(pe, k4_done, t)
                after(pe, k2_done, t)
                for a in range(KC):
                    pe.matmul(psK[:, a, :], allp[:, 5 * C + a * P:5 * C + (a + 1) * P], k2[:],
                              start=False, stop=False, skip_group_check=True)
                for a in range(KC):
                    last = pe.matmul(psN[:, a:a + 1], k4[:, a * P:(a + 1) * P], k.ones[:, 0:1],
                                     start=False, stop=False, skip_group_check=True)
                last.then_inc(acc_done, 1)
            pe.matmul(psK[:].rearrange("p a n -> p (a n)"), k.zero1[:], bcat[0:1, 0:512], start=True, stop=True)
            pe.matmul(psN[:, 0:KC], k.zero1[:], bcat[0:1, 0:KC], start=True, stop=True)
            skewed(pe, head, tail)
            pe.wait_ge(kvT_sb, 1)
            for a in range(KC):
                for d in range(KC):
                    last = pe.matmul(psM[:, a, :], kvT[:, d, a * P:(a + 1) * P], wout[:, d, :],
                                     start=(d == 0), stop=(d == KC - 1))
            last.then_inc(kvw_ps, 1)


def mix_output(nc, k, w):
    with ExitStack() as c:
        sb = lambda name, shape, dt=F32: c.enter_context(nc.sbuf_tensor(name, shape, dt))
        sem = semaphores(nc, c)
        wout = sb("a_wout", [P, KC, C])
        bias = sb("a_bias", [P, C])
        bias2 = sb("a_bias2", [P, C])
        mvt = sb("a_mvt", [P, 2, 2 * C])
        xt = sb("a_xt", [P, 2, C])
        mT = sb("a_mT", [P, 4, P])
        xb = sb("a_xb", [P, C])
        xo = sb("a_xo", [P, C])
        psT = c.enter_context(nc.psum_tensor("a_psT", [P, 2, 4, P], F32))
        psO = c.enter_context(nc.psum_tensor("a_psO", [P, 2, 512], F32))
        w_in = sem("a_w_in")
        t_in = [sem("a_t_in0"), sem("a_t_in1")]
        bias_done, ps_T, sb_T, ps_O, xb_done, out_done, stored = (
            sem("a_" + n) for n in ("bias_done", "ps_T", "sb_T", "ps_O", "xb_done", "out_done", "stored"))
        block = c.enter_context(nc.Block())

        @block.sync
        def _(sp):
            prime(sp, [ps_T, sb_T, ps_O, xb_done, out_done], [(stored, 1)])
            sp.dma_start(wout[:], w["L0_mix_W_out"].rearrange("(a p) n -> p a n", p=P)).then_inc(w_in, 16)
            sp.dma_start(bias[:], w["L0_mix_b_out"].partition_broadcast(P)).then_inc(w_in, 16)
            sp.dma_start(bias2[:], w["L0_gnn_bo"].partition_broadcast(P)).then_inc(w_in, 16)

            def load(t, s):
                after(sp, ps_T, t - 2)
                after(sp, xb_done, t - 2)
                sp.dma_start(mvt[:, s, :], rows(k.MV, t)).then_inc(t_in[s], 16)
                sp.dma_start(xt[:, s, :], rows(k.XP, t)).then_inc(t_in[s], 16)
            ring(sp, load)

        @block.tensor
        def _(pe):
            def head(t, s):
                loaded(pe, t_in[s], t, s, per=2)
                after(pe, sb_T, t - 2)
                for a in range(4):
                    last = pe.transpose(psT[:, s, a, :], mvt[:, s, a * P:(a + 1) * P], k.ident[:])
                last.then_inc(ps_T, 1)

            def tail(t, s):
                after(pe, sb_T, t)
                after(pe, out_done, t - 2)
                for a in range(4):
                    rhs = k.M1[:, a, :] if a < KC else wout[:, a - KC, :]
                    last = pe.matmul(psO[:, s, 0:C], mT[:, a, :], rhs, start=(a == 0), stop=(a == 3))
                last.then_inc(ps_O, 1)
            pe.wait_ge(w_in, 48)
            skewed(pe, head, tail)

        @block.scalar
        def _(act):
            def copy(t, s):
                after(act, ps_T, t)
                after(act, ps_O, t - 1)
                act.activation(mT[:], psT[:, s, :, :], ACT.Copy).then_inc(sb_T, 1)

            def store(t, s):
                after(act, out_done, t)
                act.dma_start(rows(k.X1M, t), xo[:]).then_inc(stored, 16)
            skewed(act, copy, store)
            after_dma(act, stored, NT - 1)

        @block.vector
        def _(dve):
            dve.wait_ge(w_in, 48)
            dve.tensor_tensor(bias[:], bias[:], bias2[:], ALU.add).then_inc(bias_done, 1)
            dve.wait_ge(bias_done, 1)

            def body(t, s):
                loaded(dve, t_in[s], t, s, per=2)
                after(dve, out_done, t - 1)
                dve.tensor_tensor(xb[:], xt[:, s, :], bias[:], ALU.add).then_inc(xb_done, 1)
                after(dve, xb_done, t)
                after(dve, ps_O, t)
                after_dma(dve, stored, t - 1)
                dve.tensor_tensor(xo[:], xb[:], psO[:, s, 0:C], ALU.add).then_inc(out_done, 1)
            ring(dve, body)


EA = 206250
BLK = 13
LA = 1612
NBA = LA // BLK
HEADS = 8
DK = C // HEADS


def lane_lists(nc, k, w):
    with ExitStack() as c:
        sb = lambda name, shape, dt=F32: c.enter_context(nc.sbuf_tensor(name, shape, dt))
        sem = semaphores(nc, c)
        lo_i, lo = sb("lo_i", [P, LA], I32), sb("lo", [P, LA])
        hi_i, hi = sb("hi_i", [P, LA], I32), sb("hi", [P, LA])
        dstf = sb("dstf", [P, LA])
        oh_lo = sb("oh_lo", [P, 2, BLK, P], BF16)
        oh_hi = sb("oh_hi", [P, 2, BLK, NT], BF16)
        psC = c.enter_context(nc.psum_tensor("psC", [P, NT], F32))
        set_done, in_done, dve_step, onehots, counted, same_done, kept = (sem(n) for n in (
            "l_set_done", "l_in_done", "l_dve_step", "l_onehots", "l_counted", "l_same_done", "l_kept"))
        block = c.enter_context(nc.Block())
        full = EA // LA
        rest = EA - full * LA

        @block.sync
        def _(sp):
            prime(sp, [onehots, counted])
            sp.wait_ge(set_done, 2)
            for tile, src in ((k.srci, w["src"]), (k.dsti, w["dst"])):
                sp.dma_start(tile[0:full, :], src[0:full * LA].rearrange("(p i) -> p i", i=LA)).then_inc(in_done, 16)
                sp.dma_start(tile[full:P, 0:rest], row_of(src[full * LA:EA])).then_inc(in_done, 16)
            sp.wait_ge(in_done, 64)
            sp.wait_ge(same_done, 1)
            sp.dma_start(k.SRCL, k.srci[:]).then_inc(kept, 16)
            sp.dma_start(k.SAMEL, k.same[:]).then_inc(kept, 16)
            sp.wait_ge(kept, 32)

        @block.gpsimd
        def _(pool):
            pool.memset(k.srci[:], 0).then_inc(set_done, 1)
            pool.memset(k.dsti[:], N).then_inc(set_done, 1)

        @block.vector
        def _(dve):
            link = Chain(dve, dve_step, None)
            link.start_once()
            dve.wait_ge(in_done, 64)
            link(dve.tensor_scalar(lo_i[:], k.dsti[:], P - 1, None, ALU.bitwise_and))
            link(dve.tensor_scalar(hi_i[:], k.dsti[:], 7, None, ALU.logical_shift_right))
            link(dve.tensor_copy(lo[:], lo_i[:]))
            link(dve.tensor_copy(hi[:], hi_i[:]))
            link(dve.tensor_copy(dstf[:], k.dsti[:]))
            link(dve.memset(k.same[:, 0:1], 0.0))
            dve.tensor_tensor(k.same[:, 1:LA], dstf[:, 1:LA], dstf[:, 0:LA - 1], ALU.is_equal).then_inc(same_done, 1)
            link(dve.tensor_copy(k.first[:], dstf[:, 0:1]))
            link(dve.tensor_copy(k.last[:], dstf[:, LA - 1:LA]))

            def body(b, s):
                after(dve, counted, b - 2)
                dve.tensor_tensor(oh_lo[:, s], k.iota[:].unsqueeze(1).to_broadcast([P, BLK, P]),
                                  lo[:, bass.ds(b * BLK, BLK)].unsqueeze(2).to_broadcast([P, BLK, P]), ALU.is_equal)
                dve.tensor_tensor(oh_hi[:, s], k.iota[:, 0:NT].unsqueeze(1).to_broadcast([P, BLK, NT]),
                                  hi[:, bass.ds(b * BLK, BLK)].unsqueeze(2).to_broadcast([P, BLK, NT]), ALU.is_equal)\
                    .then_inc(onehots, 1)
            ring(dve, body, n=NBA)
            after(dve, counted, NBA - 1)
            link(dve.tensor_copy(k.cnt[:], psC[:]))

        @block.tensor
        def _(pe):
            pe.wait_ge(in_done, 64)
            pe.matmul(psC[:], k.zero1[:], k.ones[0:1, 0:NT], start=True, stop=True)

            def body(b, s):
                after(pe, onehots, b)
                for j in range(BLK):
                    last = pe.matmul(psC[:], oh_lo[:, s, j, :], oh_hi[:, s, j, :],
                                     start=False, stop=False, skip_group_check=True)
                last.then_inc(counted, 1)
            ring(pe, body, n=NBA)


def rank_nodes(nc, k, cnt, nt, length, start, pos_i, inc_i, tag):
    with ExitStack() as c:
        sb = lambda name, shape, dt=F32: c.enter_context(nc.sbuf_tensor(name + tag, shape, dt))
        sem = semaphores(nc, c, after=tag)
        incl, tot, end, pos = sb("incl", [P, nt]), sb("tot", [P, nt]), sb("end", [P, nt]), sb("pos", [P, nt])
        lane, tmp, tmp2 = sb("lane", [P, nt]), sb("tmp", [P, nt]), sb("tmp2", [P, nt])
        starts = sb("starts", [P, P])
        onesr = sb("onesr", [P, nt])
        cmp = sb("cmp", [P, nt, P])
        psA = c.enter_context(nc.psum_tensor("psA" + tag, [P, 512], F32))
        psB = c.enter_context(nc.psum_tensor("psB" + tag, [P, 512], F32))
        summed, step = sem("summed"), sem("rank_step")
        block = c.enter_context(nc.Block())

        @block.tensor
        def _(pe):
            pe.matmul(psA[:, 0:nt], k.ones[:], cnt, start=True, stop=True)
            pe.matmul(psB[:, 0:nt], k.upper[:], cnt, start=True, stop=True).then_inc(summed, 1)

        @block.vector
        def _(dve):
            link = Chain(dve, step, None)
            link.start_once()
            link(dve.memset(onesr[:], 1.0))
            dve.wait_ge(summed, 1)
            link(dve.tensor_copy(tot[:], psA[:, 0:nt]))
            link(dve.tensor_tensor_scan(incl[:], onesr[:], tot[:], 0.0, ALU.mult, ALU.add))
            link(dve.tensor_tensor(tmp[:], incl[:], tot[:], ALU.subtract))
            link(dve.tensor_tensor(start, tmp[:], psB[:, 0:nt], ALU.add))
            link(dve.tensor_tensor(end[:], start, cnt, ALU.add))
            link(dve.tensor_scalar(pos[:], end[:], -1.0, 0.0, ALU.add, ALU.max))
            link(dve.tensor_copy(pos_i, pos[:]))
            link(dve.tensor_scalar(starts[:], k.iota[:], float(length), None, ALU.mult))
            link(dve.tensor_tensor(cmp[:], pos[:].unsqueeze(2).to_broadcast([P, nt, P]),
                                   starts[:].unsqueeze(1).to_broadcast([P, nt, P]), ALU.is_ge))
            link(dve.tensor_reduce(tmp[:], cmp[:], AX.X, ALU.add))
            link(dve.tensor_scalar(lane[:], tmp[:], -1.0, None, ALU.add))
            link(dve.tensor_scalar(tmp[:], lane[:], float(length), None, ALU.mult))
            link(dve.tensor_tensor(tmp2[:], start, tmp[:], ALU.is_lt))
            link(dve.tensor_scalar(tmp[:], lane[:], float(-P), None, ALU.add))
            link(dve.tensor_tensor(lane[:], tmp[:], tmp2[:], ALU.mult))
            link(dve.tensor_scalar(tmp[:], lane[:], float(P), None, ALU.add))
            link(dve.tensor_copy(inc_i, tmp[:]))


def edge_attention(nc, k):
    scale = float(DK) ** -0.5
    D1, S1 = DK + 1, BLK + 1
    with ExitStack() as c:
        sb = lambda name, shape, dt=F32: c.enter_context(nc.sbuf_tensor(name, shape, dt))
        sem = semaphores(nc, c)
        idx = sb("e_idx", [P, 2, 2, BLK], I32)
        q = sb("e_q", [P, 2, BLK, C])
        kv = sb("e_kv", [P, 2, BLK, 2 * C])
        S = sb("e_S", [P, HEADS, S1])
        bias = sb("e_bias", [P, HEADS, S1])
        bias1 = sb("e_bias1", [P, BLK])
        M = sb("e_M", [P, HEADS, S1])
        D = sb("e_D", [P, 2, HEADS, BLK])
        E = sb("e_E", [P, 2, HEADS, BLK])
        CX = sb("e_CX", [P, D1, HEADS, S1])
        PV = sb("e_PV", [P, D1, HEADS, S1])
        A = sb("e_A", [P, D1, HEADS, S1])
        O = sb("e_O", [P, BLK, (D1 + 1) * HEADS])
        idx_in = [sem("idx_in0"), sem("idx_in1")]
        q_in = [sem("q_in0"), sem("q_in1")]
        kv_in = [sem("kv_in0"), sem("kv_in1")]
        set_done, dve_step, d_done, pv_done, a_done, s_done = (sem("e_" + n) for n in (
            "set_done", "dve_step", "d_done", "pv_done", "a_done", "s_done"))
        exp_done, cx_done, o1_done, o_done, stored = (sem("e_" + n) for n in (
            "exp_done", "cx_done", "o1_done", "o_done", "stored"))
        block = c.enter_context(nc.Block())
        src_l, dst_l = k.srci, k.dsti
        pt = k.PT.rearrange("(p i) f -> p i f", i=LA)

        @block.sync
        def _(sp):
            prime(sp, [d_done, pv_done, a_done, s_done, exp_done, cx_done, o_done], [(stored, 1)])

            def fetch(b, s):
                after(sp, pv_done, b - 2)
                sp.dma_start(idx[:, s, 0, :], src_l[:, bass.ds(b * BLK, BLK)]).then_inc(idx_in[s], 16)
                sp.dma_start(idx[:, s, 1, :], dst_l[:, bass.ds(b * BLK, BLK)]).then_inc(idx_in[s], 16)

            def store(b, s):
                after(sp, o_done, b)
                sp.dma_start(pt[:, bass.ds(b * BLK, BLK), :], O[:]).then_inc(stored, 16)
            two_ahead(sp, fetch, store, n=NBA)
            after_dma(sp, stored, NBA - 1)

        @block.gpsimd
        def _(pool):
            def gather(b, s):
                loaded(pool, idx_in[s], b, s, per=2)
                after(pool, pv_done, b - 2)
                for j in range(BLK):
                    pool.indirect_dma_start(q[:, s, j, :], None, k.Q,
                                            bass.IndirectOffsetOnAxis(ap=idx[:, s, 1, j:j + 1], axis=0)).then_inc(q_in[s], 16)
                    pool.indirect_dma_start(kv[:, s, j, :], None, k.KV,
                                            bass.IndirectOffsetOnAxis(ap=idx[:, s, 0, j:j + 1], axis=0)).then_inc(kv_in[s], 16)
            ring(pool, gather, n=NBA)

        @block.vector
        def _(dve):
            dve.memset(bias[:], -BIG).then_inc(set_done, 1)
            dve.memset(M[:], -BIG).then_inc(set_done, 1)
            dve.memset(CX[:], 0.0).then_inc(set_done, 1)
            dve.memset(A[:], 0.0).then_inc(set_done, 1)
            dve.wait_ge(set_done, 4)
            step = Chain(dve, dve_step, 8)

            def body(b, s):
                step.start(b)
                loaded(dve, q_in[s], b, s, per=BLK)
                loaded(dve, kv_in[s], b, s, per=BLK)
                qs = q[:, s]
                step(dve.tensor_tensor(qs, qs, kv[:, s, :, 0:C], ALU.mult))
                dve.tensor_copy(S[:, :, 0:1], M[:, :, BLK:S1])
                step(dve.tensor_scalar(bias1[:], k.same[:, bass.ds(b * BLK, BLK)], -1.0, BIG, ALU.add, ALU.mult))
                step(dve.tensor_copy(bias[:, :, 1:S1], bias1[:].unsqueeze(1).to_broadcast([P, HEADS, BLK])))
                step(dve.tensor_reduce(S[:, :, 1:S1], qs.rearrange("p j (d h) -> p h j d", h=HEADS), AX.X, ALU.add))
                after(dve, o_done, b - 1)
                step(dve.tensor_tensor_scan(M[:].rearrange("p h j -> p (h j)"), bias[:].rearrange("p h j -> p (h j)"),
                                            S[:].rearrange("p h j -> p (h j)"), -BIG, ALU.add, ALU.max))
                dve.tensor_tensor(D[:, 0], S[:, :, 1:S1], M[:, :, 1:S1], ALU.subtract)
                step(dve.tensor_tensor(D[:, 1], M[:, :, 0:BLK], M[:, :, 1:S1], ALU.subtract))
                dve.tensor_tensor(D[:, 1], D[:, 1], bias[:, :, 1:S1], ALU.add).then_inc(d_done, 1)
                step(dve.tensor_copy(PV[:, :, :, 0], A[:, :, :, BLK]))
                after(dve, exp_done, b)
                step(dve.tensor_copy(PV[:, DK, :, 1:S1], E[:, 0]))
                dve.tensor_tensor(PV[:, 0:DK, :, 1:S1], kv[:, s, :, C:2 * C].rearrange("p j (d h) -> p d h j", h=HEADS),
                                  E[:, 0].unsqueeze(1).to_broadcast([P, DK, HEADS, BLK]), ALU.mult).then_inc(pv_done, 1)
                after(dve, pv_done, b)
                after(dve, cx_done, b)
                dve.tensor_tensor_scan(A[:].rearrange("p d h j -> p (d h j)"), CX[:].rearrange("p d h j -> p (d h j)"),
                                       PV[:].rearrange("p d h j -> p (d h j)"), 0.0, ALU.mult, ALU.add).then_inc(a_done, 1)
                after(dve, a_done, b)
                step.end()
            ring(dve, body, n=NBA)

        @block.scalar
        def _(act):
            act.wait_ge(set_done, 4)

            def body(b, s):
                after(act, d_done, b)
                act.activation(E[:], D[:], ACT.Exp, scale=scale).then_inc(exp_done, 1)
                after(act, exp_done, b)
                act.activation(CX[:, :, :, 1:S1], E[:, 1].unsqueeze(1).to_broadcast([P, D1, HEADS, BLK]), ACT.Copy)\
                    .then_inc(cx_done, 1)
                after(act, a_done, b)
                after_dma(act, stored, b - 1)
                act.activation(O[:, :, 0:D1 * HEADS], A[:, :, :, 1:S1].rearrange("p d h j -> p j (d h)"), ACT.Copy)\
                    .then_inc(o1_done, 1)
                act.activation(O[:, :, D1 * HEADS:], M[:, :, 1:S1].rearrange("p h j -> p j h"), ACT.Copy).then_inc(o_done, 1)
            ring(act, body, n=NBA)


def join_lanes(nc, k, table, length, last_node, first_node, H, D1, scale, incoming, tag):
    W = (D1 + 1) * H if H else D1
    with ExitStack() as c:
        sb = lambda name, shape, dt=F32: c.enter_context(nc.sbuf_tensor(name + tag, shape, dt))
        sem = semaphores(nc, c, after=tag)
        ends, inc, none = sb("j_ends", [P, W]), sb("j_inc", [P, W]), sb("j_none", [1, W])
        diag, mask, mbias = sb("j_diag", [P, P]), sb("j_mask", [P, P]), sb("j_mbias", [P, P])
        X, Wt = sb("j_X", [P, P]), sb("j_Wt", [P, P])
        mx = sb("j_mx", [P, 1])
        ps = c.enter_context(nc.psum_tensor("j_ps" + tag, [P, 512], F32))
        psW = c.enter_context(nc.psum_tensor("j_psW" + tag, [P, 512], F32))
        psV = c.enter_context(nc.psum_tensor("j_psV" + tag, [P, 512], F32))
        ends_in, step, exp_done, spread, turned, joined, stored, pool_set = (sem("j_" + n) for n in (
            "ends_in", "step", "exp_done", "spread", "turned", "joined", "stored", "pool_set"))
        diag_done, wt_done, x_done, wm_done, inc_done = (sem("j_" + n) for n in ("diag_done", "wt_done", "x_done", "wm_done", "inc_done"))
        block = c.enter_context(nc.Block())
        heads = max(H, 1)

        @block.sync
        def _(sp):
            sp.dma_start(ends[:], table.rearrange("(p i) f -> p i f", i=length)[:, length - 1, :]).then_inc(ends_in, 16)
            sp.wait_ge(pool_set, 2 if H else 1)
            sp.dma_start(incoming[P:P + 1, :], none[:]).then_inc(stored, 16)
            sp.wait_ge(inc_done, heads)
            sp.dma_start(incoming[0:P, :], inc[:]).then_inc(stored, 16)
            sp.wait_ge(stored, 32)

        @block.gpsimd
        def _(pool):
            pool.memset(none[:], 0.0).then_inc(pool_set, 1)
            if H:
                pool.wait_ge(pool_set, 1)
                pool.memset(none[:, D1 * H:], -BIG).then_inc(pool_set, 1)

        @block.vector
        def _(dve):
            link = Chain(dve, step, None)
            link.start_once()
            dve.tensor_scalar(diag[:], k.ident[:], last_node, None, ALU.mult).then_inc(diag_done, 1)
            dve.wait_ge(spread, 1)
            link(dve.scalar_tensor_tensor(out=mask[:], in0=ps[:, 0:P], scalar=first_node, in1=k.low[:],
                                          op0=ALU.is_equal, op1=ALU.mult))
            link(dve.tensor_scalar(mbias[:], mask[:], -1.0, BIG, ALU.add, ALU.mult))
            dve.wait_ge(ends_in, 16)
            for h in range(heads):
                if H:
                    m = D1 * H + h
                    dve.tensor_scalar(diag[:], k.ident[:], ends[:, m:m + 1], None, ALU.mult).then_inc(diag_done, 1)
                    dve.wait_ge(spread, h + 2)
                    link(dve.tensor_tensor(X[:], ps[:, 0:P], mbias[:], ALU.add))
                    link(dve.tensor_reduce(mx[:], X[:], AX.X, ALU.max))
                    link(dve.tensor_copy(inc[:, m:m + 1], mx[:]))
                    dve.tensor_scalar(X[:], X[:], mx[:, 0:1], None, ALU.subtract).then_inc(x_done, 1)
                    dve.wait_ge(exp_done, h + 1)
                    dve.tensor_tensor(X[:], X[:], mask[:], ALU.mult).then_inc(wm_done, 1)
                else:
                    dve.tensor_copy(X[:], mask[:]).then_inc(wm_done, 1)
                dve.wait_ge(turned, h + 1)
                dve.tensor_copy(Wt[:], psW[:, 0:P]).then_inc(wt_done, 1)
                dve.wait_ge(joined, h + 1)
                if H:
                    dve.tensor_copy(inc[:, 0:D1 * H].rearrange("p (d h) -> p d h", h=H)[:, :, h], psV[:, 0:D1]).then_inc(inc_done, 1)
                else:
                    dve.tensor_copy(inc[:], psV[:, 0:D1]).then_inc(inc_done, 1)

        @block.scalar
        def _(act):
            if H:
                for h in range(H):
                    act.wait_ge(x_done, h + 1)
                    act.activation(X[:], X[:], ACT.Exp, scale=scale).then_inc(exp_done, 1)

        @block.tensor
        def _(pe):
            pe.wait_ge(diag_done, 1)
            pe.matmul(ps[:, 0:P], k.ones[:], diag[:], start=True, stop=True).then_inc(spread, 1)
            for h in range(heads):
                if H:
                    pe.wait_ge(diag_done, h + 2)
                    pe.matmul(ps[:, 0:P], k.ones[:], diag[:], start=True, stop=True).then_inc(spread, 1)
                pe.wait_ge(wm_done, h + 1)
                pe.transpose(psW[:, 0:P], X[:], k.ident[:]).then_inc(turned, 1)
                pe.wait_ge(wt_done, h + 1)
                if h == 0:
                    pe.wait_ge(ends_in, 16)
                rhs = ends[:, 0:D1 * H].rearrange("p (d h) -> p d h", h=H)[:, :, h] if H else ends[:]
                pe.matmul(psV[:, 0:D1], Wt[:], rhs, start=True, stop=True).then_inc(joined, 1)


def attention_output(nc, k, w):
    scale = float(DK) ** -0.5
    D1 = DK + 1
    W = (D1 + 1) * HEADS
    with ExitStack() as c:
        sb = lambda name, shape, dt=F32: c.enter_context(nc.sbuf_tensor(name, shape, dt))
        sem = semaphores(nc, c)
        wo = sb("b_wo", [P, KC, C])
        idx = sb("b_idx", [P, 2, 2], I32)
        r = sb("b_r", [P, 2, 2, W])
        xm = sb("b_xm", [P, 2, C])
        Mx = sb("b_Mx", [P, HEADS])
        D = sb("b_D", [P, 2, HEADS])
        E = sb("b_E", [P, 2, HEADS])
        T = sb("b_T", [P, 2, D1, HEADS])
        U = sb("b_U", [P, D1, HEADS])
        rz = sb("b_rz", [P, HEADS])
        att = sb("b_att", [P, C])
        aT = sb("b_aT", [P, KC, P])
        xo = sb("b_xo", [P, C])
        psT = c.enter_context(nc.psum_tensor("b_psT", [P, KC, P], F32))
        psO = c.enter_context(nc.psum_tensor("b_psO", [P, 512], F32))
        w_in = sem("b_w_in")
        x_in = [sem("b_x_in0"), sem("b_x_in1")]
        r_in = [sem("b_r_in0"), sem("b_r_in1")]
        idx_done, step, d_done, e_done, att_done, ps_T, sb_T, ps_O, out_done, stored = (
            sem("b_" + n) for n in ("idx_done", "step", "d_done", "e_done", "att_done", "ps_T", "sb_T", "ps_O",
                                    "out_done", "stored"))
        block = c.enter_context(nc.Block())

        @block.sync
        def _(sp):
            prime(sp, [idx_done, d_done, e_done, att_done, ps_T, sb_T, ps_O, out_done], [(stored, 1)])
            sp.dma_start(wo[:], w["L0_gnn_Wo"].rearrange("(a p) n -> p a n", p=P)).then_inc(w_in, 16)

            def load(t, s):
                after(sp, out_done, t - 2)
                sp.dma_start(xm[:, s, :], rows(k.X1M, t)).then_inc(x_in[s], 16)

            def store(t, s):
                after(sp, out_done, t)
                sp.dma_start(rows(k.X1, t), xo[:]).then_inc(stored, 16)
            two_ahead(sp, load, store)
            after_dma(sp, stored, NT - 1)

        @block.gpsimd
        def _(pool):
            def gather(t, s):
                after(pool, idx_done, t)
                after(pool, att_done, t - 2)
                for g, (tab, width) in enumerate(((k.PT, W), (k.INC, W))):
                    pool.indirect_dma_start(r[:, s, g, :], None, tab,
                                            bass.IndirectOffsetOnAxis(ap=idx[:, s, g:g + 1], axis=0)).then_inc(r_in[s], 16)
            ring(pool, gather)

        @block.vector
        def _(dve):
            ch = Chain(dve, step, 5)

            def index(t, s):
                if not isinstance(t, int) or t >= 2:
                    loaded(dve, r_in[s], t - 2, s, per=2)
                dve.tensor_copy(idx[:, s, 0:1], k.pos_i[:, bass.ds(t, 1)])
                dve.tensor_copy(idx[:, s, 1:2], k.inc_i[:, bass.ds(t, 1)]).then_inc(idx_done, 1)

            def body(t, s):
                ch.start(t)
                loaded(dve, r_in[s], t, s, per=2)
                m = r[:, s, :, D1 * HEADS:]
                ch(dve.tensor_tensor(Mx[:], m[:, 0], m[:, 1], ALU.max))
                dve.tensor_tensor(D[:], m, Mx[:].unsqueeze(1).to_broadcast([P, 2, HEADS]), ALU.subtract).then_inc(d_done, 1)
                after(dve, e_done, t)
                v = r[:, s, :, 0:D1 * HEADS].rearrange("p g (d h) -> p g d h", h=HEADS)
                for g in range(2):
                    ins = dve.tensor_tensor(T[:, g], v[:, g], E[:, g].unsqueeze(1).to_broadcast([P, D1, HEADS]), ALU.mult)
                    ch(ins)
                ch(dve.tensor_tensor(U[:], T[:, 0], T[:, 1], ALU.add))
                ch(dve.reciprocal(rz[:], U[:, DK, :]))
                after(dve, ps_T, t - 1)
                dve.tensor_tensor(att[:].rearrange("p (d h) -> p d h", h=HEADS), U[:, 0:DK],
                                  rz[:].unsqueeze(1).to_broadcast([P, DK, HEADS]), ALU.mult).then_inc(att_done, 1)
                after(dve, ps_O, t)
                loaded(dve, x_in[s], t, s)
                after_dma(dve, stored, t - 1)
                dve.tensor_tensor(xo[:], xm[:, s, :], psO[:, 0:C], ALU.add).then_inc(out_done, 1)
                ch.end()
            index(0, 0)
            index(1, 1)
            body(0, 0)
            index(2, 0)
            body(1, 1)
            index(3, 1)
            with dve.Fori(1, NT // 2 - 1) as j:
                body(2 * j, 0)
                index(2 * j + 2, 0)
                body(2 * j + 1, 1)
                index(2 * j + 3, 1)
            body(NT - 2, 0)
            body(NT - 1, 1)

        @block.scalar
        def _(act):
            def body(t, s):
                after(act, d_done, t)
                act.activation(E[:], D[:], ACT.Exp, scale=scale).then_inc(e_done, 1)
                after(act, ps_T, t)
                after(act, ps_O, t - 1)
                act.activation(aT[:], psT[:], ACT.Copy).then_inc(sb_T, 1)
            ring(act, body)

        @block.tensor
        def _(pe):
            pe.wait_ge(w_in, 16)

            def body(t, s):
                after(pe, att_done, t)
                after(pe, sb_T, t - 1)
                for a in range(KC):
                    last = pe.transpose(psT[:, a, :], att[:, a * P:(a + 1) * P], k.ident[:])
                last.then_inc(ps_T, 1)
                after(pe, sb_T, t)
                after(pe, out_done, t - 1)
                for a in range(KC):
                    last = pe.matmul(psO[:, 0:C], aT[:, a, :], wo[:, a, :], start=(a == 0), stop=(a == KC - 1))
                last.then_inc(ps_O, 1)
            ring(pe, body)


EG = 131072
TG = EG // P
HG = 64
LG = EG // P + HG
HE = 4
SB = 8


def gat_count(nc, k, w):
    HB = 16
    with ExitStack() as c:
        sb = lambda name, shape, dt=F32: c.enter_context(nc.sbuf_tensor("c_" + name, shape, dt))
        sem = semaphores(nc, c, before="c_")
        nat_i, nat = sb("nat_i", [P, 2, TG], I32), sb("nat", [P, 2, TG])
        tmp_i = sb("tmp_i", [P, TG], I32)
        oh_lo, oh_hi = sb("oh_lo", [P, 2, HB, P], BF16), sb("oh_hi", [P, 2, HB, HG], BF16)
        psT = [c.enter_context(nc.psum_tensor(f"c_psT{i}", [P, TG], F32)) for i in range(2)]
        psC = c.enter_context(nc.psum_tensor("c_psC", [P, HG], F32))
        nat_in, step, nat_done, turned, ready, onehots, counted = (sem(n) for n in (
            "nat_in", "step", "nat_done", "turned", "ready", "onehots", "counted"))
        block = c.enter_context(nc.Block())

        @block.sync
        def _(sp):
            prime(sp, [onehots, counted])
            for i in range(2):
                sp.dma_start(nat_i[:, i, :].rearrange("i (b p) -> i b p", p=P),
                             w["L1_ffn_edge_index"][i].rearrange("(b i p) -> i b p", i=P, p=P)).then_inc(nat_in, 16)

        @block.tensor
        def _(pe):
            pe.wait_ge(nat_done, 2)
            for i in range(2):
                for b in range(TG // P):
                    last = pe.transpose(psT[i][:, b * P:(b + 1) * P], nat[:, i, b * P:(b + 1) * P], k.ident[:])
            last.then_inc(turned, 1)
            pe.matmul(psC[:], k.zero1[:], k.ones[0:1, 0:HG], start=True, stop=True)

            def body(b, s):
                after(pe, onehots, b)
                for j in range(HB):
                    last = pe.matmul(psC[:], oh_lo[:, s, j, :], oh_hi[:, s, j, :], start=False, stop=False,
                                     skip_group_check=True)
                last.then_inc(counted, 1)
            ring(pe, body, n=TG // HB)

        @block.vector
        def _(dve):
            link = Chain(dve, step, None)
            link.start_once()
            dve.wait_ge(nat_in, 32)
            dve.tensor_scalar(nat[:, 0, :], nat_i[:, 0, :], float(N - 1), None, ALU.min).then_inc(nat_done, 1)
            dve.tensor_copy(nat[:, 1, :], nat_i[:, 1, :]).then_inc(nat_done, 1)
            dve.wait_ge(turned, 1)
            for i in range(2):
                link(dve.tensor_copy(k.pair[:, :, i], psT[i][:]))
            link(dve.tensor_scalar(tmp_i[:], k.pair[:, :, 1], P - 1, None, ALU.bitwise_and))
            link(dve.tensor_copy(k.lo[:], tmp_i[:]))
            link(dve.tensor_scalar(tmp_i[:], k.pair[:, :, 1], 7, None, ALU.logical_shift_right))
            link(dve.tensor_copy(k.hi[:], tmp_i[:]))
            link(dve.tensor_copy(k.dcol[:], k.pair[:, :, 1]))

            def body(b, s):
                after(dve, counted, b - 2)
                dve.tensor_tensor(oh_lo[:, s], k.iota[:].unsqueeze(1).to_broadcast([P, HB, P]),
                                  k.lo[:, bass.ds(b * HB, HB)].unsqueeze(2).to_broadcast([P, HB, P]), ALU.is_equal)
                dve.tensor_tensor(oh_hi[:, s], k.iota[:, 0:HG].unsqueeze(1).to_broadcast([P, HB, HG]),
                                  k.hi[:, bass.ds(b * HB, HB)].unsqueeze(2).to_broadcast([P, HB, HG]), ALU.is_equal)\
                    .then_inc(onehots, 1)
            ring(dve, body, n=TG // HB)
            after(dve, counted, TG // HB - 1)
            link(dve.tensor_scalar(k.cnt2[:], psC[:], 1.0, None, ALU.add))


class GatSort:

    blocks = TG // SB

    def __init__(self, nc, k, w, c, sem, psC, psR):
        self.k, self.w, self.psC, self.psR = k, w, psC, psR
        sb = lambda name, shape, dt=F32: c.enter_context(nc.sbuf_tensor("o_" + name, shape, dt))
        self.db = sb("db", [P, 2, SB * P], I32)
        self.dlo, self.dbf = sb("dlo", [P, SB * P], I32), sb("dbf", [P, 2, SB * P])
        self.ahead = sb("ahead", [P, SB * P], BF16)
        self.oht = sb("oht", [P, 2, SB, P])
        self.oh_lo, self.oh_hi = sb("oh_lo", [P, 2, SB, P], BF16), sb("oh_hi", [P, 2, SB, HG], BF16)
        self.dc = sb("dc", [P, SB])
        self.rank, self.prior = sb("rank", [P, 2, SB]), sb("prior", [P, SB])
        self.eq, self.sel = sb("eq", [P, SB - 1, SB * P // 2], BF16), sb("sel", [P, SB, HG])
        self.base = sb("base", [P, HG])
        self.loops = sb("loops", [P, HG, 2], I32)
        self.nodes_i, self.nodes_f = sb("nodes_i", [P, HG], I32), sb("nodes_f", [P, HG])
        self.C_sb = sb("C_sb", [P, HG])
        self.pos, self.pay = sb("pos", [P, 2, SB], I32), sb("pay", [P, 2, SB, 2], I32)
        self.blank = sb("blank", [P, 2, 2], I32)
        self.db_in = [sem("db_in0"), sem("db_in1")]
        self.scattered = [sem("scattered0"), sem("scattered1")]
        self.setup, self.iota_done, self.loops_done, self.placed = (
            sem(n) for n in ("setup", "iota_done", "loops_done", "placed"))
        self.base_done, self.init_done = sem("base_done"), sem("init_done")
        self.dbf_done, self.hots_done, self.r_done = sem("dbf_done"), sem("hots_done"), sem("r_done")
        self.counted, self.c_sb = sem("counted"), sem("c_sb")
        self.rank_step, self.rank_done = sem("rank_step"), sem("rank_done")
        self.sel_step, self.sel_done, self.pos_done = sem("sel_step"), sem("sel_done"), sem("pos_done")

    def primed(self):
        return [self.hots_done, self.rank_done, self.sel_done, self.pos_done, self.dbf_done, self.counted, self.c_sb,
                self.r_done]

    def pool_start(self, pool):
        k = self.k
        pool.iota(self.nodes_i[:], [[P, HG]], 0, 1).then_inc(self.iota_done, 1)
        pool.memset(self.blank[:], 0).then_inc(self.iota_done, 1)
        pool.wait_ge(self.iota_done, 2)
        for s in range(2):
            pool.dma_start(self.blank[:, s, 1:2], self.blank[:, s, 0:1]).then_inc(self.scattered[s], 16 * SB)
        pool.wait_ge(self.loops_done, 1)
        for t in range(HG):
            pool.indirect_dma_start(k.SD, bass.IndirectOffsetOnAxis(ap=k.start2_i[:, t:t + 1], axis=0),
                                    self.loops[:, t, :], None).then_inc(self.placed, 16)
        pool.wait_ge(self.placed, 16 * HG)

    def pool_step(self, pool, b, s):
        after(pool, self.pos_done, b)
        for j in range(SB):
            pool.indirect_dma_start(self.k.SD, bass.IndirectOffsetOnAxis(ap=self.pos[:, s, j:j + 1], axis=0),
                                    self.pay[:, s, j, :], None).then_inc(self.scattered[s], 16)

    def pool_end(self, pool):
        for s in range(2):
            pool.wait_ge(self.scattered[s], 16 * SB * (self.blocks // 2 + 1))

    def dve_start(self, dve):
        k = self.k
        link = Chain(dve, self.setup, None)
        link.start_once()
        dve.tensor_scalar(self.base[:], k.start2[:], 1.0, None, ALU.add).then_inc(self.base_done, 1)
        dve.wait_ge(self.iota_done, 2)
        link(dve.tensor_copy(self.loops[:, :, 1], self.nodes_i[:]))
        link(dve.tensor_scalar(self.nodes_f[:], self.nodes_i[:], float(N - 1), None, ALU.min))
        link(dve.tensor_copy(k.start2_i[:], k.start2[:]))
        dve.tensor_copy(self.loops[:, :, 0], self.nodes_f[:]).then_inc(self.loops_done, 1)
        link(dve.memset(self.ahead[:, 0:(SB - 1) * P], 1.0))
        link(dve.tensor_copy(self.ahead[:, (SB - 1) * P:], k.low[:]))
        self.rk = Chain(dve, self.rank_step, 3)
        self.sl = Chain(dve, self.sel_step, 3)
        self.prepare(dve, 0, 0)

    def prepare(self, dve, b, s):
        k, rk = self.k, self.rk
        rk.start(b)
        loaded(dve, self.db_in[s], b, s)
        after(dve, self.rank_done, b - 1)
        rk(dve.tensor_copy(self.dc[:], k.dcol[:, bass.ds(b * SB, SB)]))
        rk(dve.tensor_scalar(self.dlo[:], self.db[:, s, :], P - 1, None, ALU.bitwise_and))
        after(dve, self.sel_done, b - 2)
        after(dve, self.counted, b - 2)
        dve.tensor_scalar(self.oht[:, s].rearrange("p j e -> p (j e)"), self.dlo[:], k.part[:, 0:1], None, ALU.is_equal)
        dve.tensor_tensor(self.oh_lo[:, s], k.iota[:].unsqueeze(1).to_broadcast([P, SB, P]),
                          k.lo[:, bass.ds(b * SB, SB)].unsqueeze(2).to_broadcast([P, SB, P]), ALU.is_equal)
        dve.tensor_tensor(self.oh_hi[:, s], k.iota[:, 0:HG].unsqueeze(1).to_broadcast([P, SB, HG]),
                          k.hi[:, bass.ds(b * SB, SB)].unsqueeze(2).to_broadcast([P, SB, HG]), ALU.is_equal)\
            .then_inc(self.hots_done, 1)
        after(dve, self.dbf_done, b)
        for j in range(SB):
            n = (j + 1) * P
            last = dve.scalar_tensor_tensor(out=self.scrap(j), in0=self.dbf[:, s, 0:n], scalar=self.dc[:, j:j + 1],
                                            in1=self.ahead[:, SB * P - n:], op0=ALU.is_equal, op1=ALU.mult,
                                            accum_out=self.rank[:, s, j:j + 1])
            if j == SB - 2:
                rk(last)
        last.then_inc(self.rank_done, 1)
        rk.end()

    def scrap(self, j):
        n = (j + 1) * P
        flat = self.eq[:].rearrange("p j n -> p (j n)")
        o = P * sum(i + 1 for i in range(j)) if j < SB - 1 else 0
        return flat[:, o:o + n]

    def dve_step(self, dve, b, s):
        k, sl = self.k, self.sl
        if not isinstance(b, int) or b + 1 < self.blocks:
            self.prepare(dve, b + 1, 1 - s)
        sl.start(b)
        after(dve, self.r_done, b)
        sl(dve.tensor_tensor(self.sel[:], self.oh_hi[:, s], self.psR, ALU.mult))
        sl(dve.tensor_reduce(self.prior[:], self.sel[:], AX.X, ALU.add))
        after(dve, self.rank_done, b)
        dve.sem_inc(self.sel_done, 1)
        wait_reg(dve, self.scattered[s], (b - s) * (8 * SB) + 16 * SB)
        dve.tensor_copy(self.pay[:, s], k.pair[:, bass.ds(b * SB, SB), :])
        sl(dve.tensor_tensor(self.pos[:, s, :], self.prior[:], self.rank[:, s, :], ALU.add))
        dve.sem_inc(self.pos_done, 1)
        sl.end()

    def fetch(self, act, b, s):
        after(act, self.hots_done, b - 2)
        after(act, self.dbf_done, b - 2)
        act.dma_start(self.db[:, s, :],
                      self.w["L1_ffn_edge_index"][1, bass.ds(b * SB * P, SB * P)].partition_broadcast(P))\
            .then_inc(self.db_in[s], 16)

    def convert(self, act, b, s):
        loaded(act, self.db_in[s], b, s)
        after(act, self.rank_done, b - 2)
        act.activation(self.dbf[:, s, :], self.db[:, s, :], ACT.Copy).then_inc(self.dbf_done, 1)

    def act_start(self, act):
        self.fetch(act, 0, 0)
        self.fetch(act, 1, 1)
        self.convert(act, 0, 0)
        act.wait_ge(self.init_done, 1)

    def act_step(self, act, b, s):
        after(act, self.counted, b - 1)
        act.activation(self.C_sb[:], self.psC, ACT.Copy).then_inc(self.c_sb, 1)
        if not isinstance(b, int) or b + 1 < self.blocks:
            self.convert(act, b + 1, 1 - s)
        if not isinstance(b, int) or b + 2 < self.blocks:
            self.fetch(act, b + 2, s)

    def pe_start(self, pe):
        pe.wait_ge(self.base_done, 1)
        pe.matmul(self.psC, self.k.ident[:], self.base[:], start=True, stop=True).then_inc(self.init_done, 1)

    def pe_step(self, pe, b, s):
        after(pe, self.hots_done, b)
        after(pe, self.c_sb, b)
        after(pe, self.sel_done, b - 1)
        for j in range(SB):
            last = pe.matmul(self.psR[:, j, :], self.oht[:, s, j, :], self.C_sb[:], start=True, stop=True)
        last.then_inc(self.r_done, 1)
        pe.matmul(self.psC, self.k.ident[:], self.C_sb[:], start=True, stop=False, skip_group_check=True)
        for j in range(SB):
            last = pe.matmul(self.psC, self.oh_lo[:, s, j, :], self.oh_hi[:, s, j, :], start=False, stop=j == SB - 1,
                             skip_group_check=True)
        last.then_inc(self.counted, 1)



GT = 5
NG = NT // GT
GW = GT * P
HALF = GW // 2


def after_step(eng, sem, g, per, i):
    wait_reg(eng, sem, g * per + i + 1 + PRIME)


def routed_ffn(nc, k, w, second, x_in_dram, x_out_dram):
    EX = 4 if second else 8
    MH = 16 if second else 8
    PH = EX // 2
    tag = "_f1" if second else "_f0"
    with ExitStack() as c:
        sb = lambda name, shape, dt=F32: c.enter_context(nc.sbuf_tensor(name + tag, shape, dt))
        sem = semaphores(nc, c, after=tag)
        w1 = sb("w1", [P, KC, MH * P])
        b1 = sb("b1", [P, MH])
        w2 = sb("w2", [P, MH, C] if second else [P, MH, EX, C])
        b2 = sb("b2", [P, EX, C])
        xg = sb("xg", [P, 2, GT, C])
        xn = sb("xn", [P, GT, C])
        xT = sb("xT", [P, KC, GW])
        H = sb("H", [P, MH, GW])
        st, mv = sb("st", [P, GT, 6]), sb("mv", [P, GT, 2])
        ve, rstd = sb("ve", [P, GT]), sb("rstd", [P, GT])
        gate = sb("gate", [P, 2, GT, EX])
        if not second:
            wg, bg = sb("wg", [P, MH, EX]), sb("bg", [P, EX])
            L, X8, oh, cand = (sb(n, [P, GT, EX]) for n in ("L", "X8", "oh", "cand"))
            mx, sm, pr, mn = (sb(n, [P, GT]) for n in ("mx", "sm", "pr", "mn"))
            im = sb("im", [P, EX])
        psT = c.enter_context(nc.psum_tensor("psT" + tag, [P, 2, KC, P], F32))
        psH = c.enter_context(nc.psum_tensor("psH" + tag, [P, 2, 512], F32))
        psL = psH[:, 1, HALF:HALF + GT * EX].rearrange("p (i e) -> p i e", e=EX)
        psY = c.enter_context(nc.psum_tensor("psY" + tag, [P, 2, 2, 512], F32))
        w_in, x_in = sem("w_in"), [sem("x_in0"), sem("x_in1")]
        var_ready, rstd_ready, xn_done, ln_step = sem("var_ready"), sem("rstd_ready"), sem("xn_done"), sem("ln_step")
        tp_done, tc_done, hp_done, h_done = sem("tp_done"), sem("tc_done"), sem("hp_done"), sem("h_done")
        lg_done, lx_done, le_done, gate_done, rt_step = (sem(n) for n in ("lg_done", "lx_done", "le_done", "gate_done", "rt_step"))
        y_done, yc_done, x_done, y_step, stored = (sem(n) for n in ("y_done", "yc_done", "x_done", "y_step", "stored"))
        im_done = sem("im_done")
        sort = None
        if not second:
            psR = c.enter_context(nc.psum_tensor("psR" + tag, [P, SB, HG], F32))
            sort = GatSort(nc, k, w, c, sem, psH[:, 0, HALF:HALF + HG], psR[:])
        block = c.enter_context(nc.Block())
        rounds = [(0, 2), (2, 2), (4, 1)]
        TR, HS, YS = len(rounds), 2 * MH, 2 * GT

        def group(ap, g):
            return ap[bass.ds(g * GW, GW), :].rearrange("(i p) c -> p i c", p=P)

        @block.sync
        def _(sp):
            prime(sp, [var_ready, rstd_ready, xn_done, tp_done, tc_done, hp_done, h_done, lg_done, lx_done, le_done,
                       gate_done, y_done, yc_done, x_done] + (sort.primed() if sort else []), [(stored, GT)])
            if second:
                for e in range(EX):
                    sp.dma_start(w1[:, :, e * 2 * C:(e + 1) * 2 * C],
                                 w["L1_ffn_W1"][e].rearrange("(a p) n -> p a n", p=P)).then_inc(w_in, 16)
                    sp.dma_start(w2[:, e * 4:(e + 1) * 4, :],
                                 w["L1_ffn_W2"][e].rearrange("(m p) n -> p m n", p=P)).then_inc(w_in, 16)
                    sp.dma_start(b2[:, e, :], w["L1_ffn_b2"][e].partition_broadcast(P)).then_inc(w_in, 16)
                    sp.dma_start(b1[:, e * 4:(e + 1) * 4], w["L1_ffn_b1"][e].rearrange("(m p) -> p m", p=P),
                                 allow_slow_non_contiguous=True).then_inc(w_in, 16)
            else:
                sp.dma_start(w1[:], w["L0_ffn_W1"].rearrange("(a p) n -> p a n", p=P)).then_inc(w_in, 16)
                sp.dma_start(b1[:], w["L0_ffn_b1"].rearrange("(m p) -> p m", p=P),
                                 allow_slow_non_contiguous=True).then_inc(w_in, 16)
                sp.dma_start(wg[:], w["L0_ffn_Wg"].rearrange("(m p) e -> p m e", p=P)).then_inc(w_in, 16)
                sp.dma_start(bg[:], w["L0_ffn_bg"].partition_broadcast(P)).then_inc(w_in, 16)
                for e in range(EX):
                    sp.dma_start(w2[:, :, e, :], w["L0_ffn_Wd"][e].rearrange("(m p) n -> p m n", p=P)).then_inc(w_in, 16)
                    sp.dma_start(b2[:, e, :], w["L0_ffn_bd"][e].partition_broadcast(P)).then_inc(w_in, 16)

            def load(g, s):
                after_dma(sp, stored, g - 2, GT)
                sp.dma_start(xg[:, s], group(x_in_dram, g)).then_inc(x_in[s], 16)

            def store(g, s):
                after(sp, x_done, g)
                for i in range(GT):
                    if second and isinstance(g, int) and (g * GT + i + 1) * P > N:
                        left = N - (g * GT + i) * P
                        if left > 0:
                            sp.dma_start(x_out_dram[N - left:N, :], xg[0:left, s, i, :]).then_inc(stored, 16)
                    else:
                        sp.dma_start(x_out_dram[bass.ds(g * GW + i * P, P), :], xg[:, s, i, :]).then_inc(stored, 16)
            skewed(sp, load, store, n=NG)
            short = (NP - N) // P if second else 0
            sp.wait_ge(stored, 16 * GT * (NG + PRIME) - 16 * short)

        BG = 2 + YS if sort else 0
        breaks = (MH // 4, 3 * MH // 4)
        NEXT = 6
        rest = range(NG * BG, GatSort.blocks) if sort else ()

        def slot(g, n):
            return g * BG + n, n % 2

        def groups(body):
            def run(eng):
                with eng.Fori(0, NG // 2 - 1) as j:
                    body(2 * j, 0, True)
                    body(2 * j + 1, 1, True)
                body(NG - 2, 0, True)
                body(NG - 1, 1, False)
            return run

        @block.gpsimd
        def _(pool):
            def power(g):
                after(pool, var_ready, g)
                pool.tensor_tensor(rstd[:], ve[:], k.neghalf[:].to_broadcast([P, GT]), ALU.pow).then_inc(rstd_ready, 1)

            def body(g, s, more):
                for n in range(BG):
                    if n == 2 + NEXT and more:
                        power(g + 1)
                    sort.pool_step(pool, *slot(g, n))
                if not sort and more:
                    power(g + 1)
            if not second:
                pool.tensor_scalar(im[:], k.iota[:, 0:EX], float(-EX), None, ALU.add).then_inc(im_done, 1)
            power(0)
            if sort:
                sort.pool_start(pool)
            groups(body)(pool)
            for b in rest:
                sort.pool_step(pool, b, b % 2)
            if sort:
                sort.pool_end(pool)

        @block.vector
        def _(dve):
            ln = Chain(dve, ln_step, 2)
            rt = Chain(dve, rt_step, 9)
            yc = Chain(dve, y_step, GT * (2 * EX - 2))
            dve.wait_ge(w_in, 16 * (16 if second else 20))
            if not second:
                dve.wait_ge(im_done, 1)

            def bcast(ap):
                return ap.unsqueeze(2).to_broadcast([P, GT, EX])

            def norm(g, s):
                ln.start(g)
                loaded(dve, x_in[s], g, s)
                for i in range(GT):
                    last = dve.bn_stats(st[:, i, :], xg[:, s, i, :])
                ln(last)
                for i in range(GT):
                    last = dve.bn_aggr(mv[:, i, :], st[:, i, :])
                ln(last)
                ln.end()
                dve.tensor_scalar(ve[:], mv[:, :, 1], LN_EPS, None, ALU.add).then_inc(var_ready, 1)
                after_step(dve, tp_done, g, TR, -1)
                after(dve, rstd_ready, g)
                for i in range(GT):
                    last = dve.tensor_scalar(xn[:, i, :], xg[:, s, i, :], mv[:, i, 0:1], rstd[:, i:i + 1],
                                             ALU.subtract, ALU.mult)
                last.then_inc(xn_done, 1)
                after(dve, xn_done, g)

            def route(g, s):
                if second:
                    dve.tensor_copy(gate[:, s], k.gate[:, bass.ds(g * GT, GT), :]).then_inc(gate_done, 1)
                    after(dve, gate_done, g)
                    return
                rt.start(g)
                after(dve, lg_done, g)
                rt(dve.tensor_tensor(L[:], psL, bg[:].unsqueeze(1).to_broadcast([P, GT, EX]), ALU.add))
                rt(dve.tensor_reduce(mx[:], L[:], AX.X, ALU.max))
                dve.tensor_tensor(X8[:], L[:], bcast(mx[:]), ALU.subtract).then_inc(lx_done, 1)
                rt(dve.tensor_tensor(oh[:], L[:], bcast(mx[:]), ALU.is_equal))
                rt(dve.tensor_tensor(cand[:], oh[:], im[:].unsqueeze(1).to_broadcast([P, GT, EX]), ALU.mult))
                rt(dve.tensor_reduce(mn[:], cand[:], AX.X, ALU.min))
                rt(dve.tensor_tensor(oh[:], im[:].unsqueeze(1).to_broadcast([P, GT, EX]), bcast(mn[:]), ALU.is_equal))
                after(dve, le_done, g)
                rt(dve.tensor_reduce(sm[:], X8[:], AX.X, ALU.add))
                rt(dve.reciprocal(pr[:], sm[:]))
                rt(dve.tensor_tensor(gate[:, s], oh[:], bcast(pr[:]), ALU.mult))
                rt.end()

            def body(g, s, more):
                if sort:
                    for n in range(2):
                        sort.dve_step(dve, *slot(g, n))
                route(g, s)
                yc.start(g)
                for i in range(GT):
                    acc = xg[:, s, i, :]
                    for e in range(EX):
                        yc(dve.scalar_tensor_tensor(out=acc, in0=b2[:, e, :], scalar=gate[:, s, i, e:e + 1], in1=acc,
                                                    op0=ALU.mult, op1=ALU.add))
                    for h in range(2):
                        after_step(dve, y_done, g, YS, 2 * i + h)
                        for e in range(PH):
                            col = 512 * e if second else C * e
                            ins = dve.scalar_tensor_tensor(out=acc, in0=psY[:, h].rearrange("p b n -> p (b n)")[:, col:col + C],
                                                           scalar=gate[:, s, i, h * PH + e:h * PH + e + 1],
                                                           in1=acc, op0=ALU.mult, op1=ALU.add)
                            if e == PH - 1:
                                ins.then_inc(yc_done, 1)
                                after_step(dve, yc_done, g, YS, 2 * i + h)
                            else:
                                yc(ins)
                        if 2 * i + h == NEXT and more:
                            norm(g + 1, 1 - s)
                        if sort:
                            sort.dve_step(dve, *slot(g, 2 + 2 * i + h))
                yc.end()
                dve.engine_nop().then_inc(x_done, 1)
            norm(0, 0)
            if sort:
                sort.dve_start(dve)
            groups(body)(dve)
            for b in rest:
                sort.dve_step(dve, b, b % 2)

        @block.scalar
        def _(act):
            act.wait_ge(w_in, 16 * (16 if second else 20))

            def body(g, s, more):
                for r, (i0, n) in enumerate(rounds):
                    after_step(act, tp_done, g, TR, r)
                    if r == 0:
                        after_step(act, hp_done, g, HS, -1)
                    act.activation(xT[:, :, i0 * P:(i0 + n) * P].rearrange("p a (i n) -> p i a n", n=P), psT[:, 0:n], ACT.Copy)\
                        .then_inc(tc_done, 1)
                for m in range(MH):
                    if sort and m in breaks:
                        sort.act_step(act, *slot(g, breaks.index(m)))
                    for h in range(2):
                        after_step(act, hp_done, g, HS, 2 * m + h)
                        act.activation(H[:, m, h * HALF:(h + 1) * HALF], psH[:, h, 0:HALF], ACT.Gelu,
                                       bias=b1[:, m:m + 1]).then_inc(h_done, 1)
                if not second:
                    after(act, lx_done, g)
                    act.activation(X8[:], X8[:], ACT.Exp).then_inc(le_done, 1)
                for n in range(2, BG):
                    sort.act_step(act, *slot(g, n))
            if sort:
                sort.act_start(act)
            groups(body)(act)
            for b in rest:
                sort.act_step(act, b, b % 2)

        @block.tensor
        def _(pe):
            pe.wait_ge(w_in, 16 * (16 if second else 20))

            def body(g, s, more):
                after(pe, xn_done, g)
                for r, (i0, n) in enumerate(rounds):
                    after_step(pe, tc_done, g, TR, r - 1)
                    for i in range(n):
                        for a in range(KC):
                            last = pe.transpose(psT[:, i, a, :], xn[:, i0 + i, a * P:(a + 1) * P], k.ident[:])
                    last.then_inc(tp_done, 1)
                after_step(pe, tc_done, g, TR, TR - 1)
                for m in range(MH):
                    if sort and m in breaks:
                        sort.pe_step(pe, *slot(g, breaks.index(m)))
                    for h in range(2):
                        after_step(pe, h_done, g, HS, 2 * m + h - 2)
                        for a in range(KC):
                            last = pe.matmul(psH[:, h, 0:HALF], w1[:, a, m * P:(m + 1) * P], xT[:, a, h * HALF:(h + 1) * HALF],
                                             start=(a == 0), stop=(a == KC - 1))
                        last.then_inc(hp_done, 1)
                after_step(pe, h_done, g, HS, HS - 1)
                if not second:
                    after(pe, lx_done, g - 1)
                    for i in range(GT):
                        for m in range(MH):
                            last = pe.matmul(psL[:, i, :], H[:, m, i * P:(i + 1) * P], wg[:, m, :],
                                             start=(m == 0), stop=(m == MH - 1))
                    last.then_inc(lg_done, 1)
                for i in range(GT):
                    for h in range(2):
                        after_step(pe, yc_done, g, YS, 2 * i + h - 2)
                        for b in range(2):
                            if second:
                                e = 2 * h + b
                                for m in range(4):
                                    last = pe.matmul(psY[:, h, b, 0:C], H[:, 4 * e + m, i * P:(i + 1) * P],
                                                     w2[:, 4 * e + m, :], start=(m == 0), stop=(m == 3))
                            else:
                                e = 4 * h + 2 * b
                                for m in range(MH):
                                    last = pe.matmul(psY[:, h, b, :], H[:, m, i * P:(i + 1) * P],
                                                     w2[:, m, e:e + 2, :].rearrange("p e n -> p (e n)"),
                                                     start=(m == 0), stop=(m == MH - 1))
                        last.then_inc(y_done, 1)
                        if sort:
                            sort.pe_step(pe, *slot(g, 2 + 2 * i + h))
            if sort:
                sort.pe_start(pe)
            groups(body)(pe)
            for b in rest:
                sort.pe_step(pe, b, b % 2)


def normed_nodes(nc, k, w):
    CA = C + 1
    with ExitStack() as c:
        sb = lambda name, shape, dt=F32: c.enter_context(nc.sbuf_tensor("n_" + name, shape, dt))
        sem = semaphores(nc, c, before="n_")
        xt = sb("xt", [P, 2, C])
        xn = sb("xn", [P, CA])
        xm = sb("xm", [P, CA])
        st, mv, ve, rstd = sb("st", [P, 6]), sb("mv", [P, 2]), sb("ve", [P, 1]), sb("rstd", [P, 1])
        psG = [c.enter_context(nc.psum_tensor(f"n_psG{a}", [P, 512], F32)) for a in range(3)]
        x_in = [sem("x_in0"), sem("x_in1")]
        set_done, var_ready, rstd_ready, xn_done, xm_done, acc_done, stored, ln_step, fin = (sem(n) for n in (
            "set_done", "var_ready", "rstd_ready", "xn_done", "xm_done", "acc_done", "stored", "ln_step", "fin"))
        block = c.enter_context(nc.Block())

        @block.sync
        def _(sp):
            prime(sp, [var_ready, rstd_ready, xn_done, xm_done, acc_done], [(stored, 1)])

            def load(t, s):
                after(sp, xn_done, t - 2)
                sp.dma_start(xt[:, s, :], rows(k.X2, t)).then_inc(x_in[s], 16)

            def store(t, s):
                after(sp, xn_done, t)
                sp.dma_start(rows(k.XN2, t), xn[:, 0:C]).then_inc(stored, 16)
            two_ahead(sp, load, store)
            after_dma(sp, stored, NT - 1)

        @block.gpsimd
        def _(pool):
            def power(t, s):
                after(pool, var_ready, t)
                pool.tensor_tensor(rstd[:], ve[:], k.neghalf[:], ALU.pow).then_inc(rstd_ready, 1)
            ring(pool, power)

        @block.vector
        def _(dve):
            ln = Chain(dve, ln_step, 2)
            dve.memset(xn[:, C:CA], 1.0).then_inc(set_done, 1)
            dve.wait_ge(set_done, 1)

            def free(t):
                after_dma(dve, stored, t - 1)
                after(dve, acc_done, t - 1)

            def body(t, s):
                ln.start(t)
                loaded(dve, x_in[s], t, s)
                layernorm_dve(dve, ln, xt[:, s, :], xn[:, 0:C], st, mv, ve, rstd, var_ready, rstd_ready, xn_done, t,
                              lambda: free(t))
                ln.end()
                dve.tensor_scalar(xm[:], xn[:], k.valid[:, bass.ds(t, 1)], None, ALU.mult).then_inc(xm_done, 1)
                after(dve, xm_done, t)
            ring(dve, body)
            after(dve, acc_done, NT - 1)
            dve.tensor_copy(k.gram[:, 0, :], psG[0][:, 0:CA])
            dve.tensor_copy(k.gram[:, 1, :], psG[1][:, 0:CA])
            dve.tensor_copy(k.gramr[:], psG[2][0:1, 0:CA]).then_inc(fin, 1)
            dve.wait_ge(fin, 1)

        @block.tensor
        def _(pe):
            pe.wait_ge(set_done, 1)
            for a in range(3):
                pe.matmul(psG[a][:, 0:P], k.zero1[:], k.ones[0:1, :], start=True, stop=True)
                pe.matmul(psG[a][:, P:2 * P], k.zero1[:], k.ones[0:1, :], start=True, stop=True)
                pe.matmul(psG[a][:, 2 * P:3 * P], k.zero1[:], k.ones[0:1, :], start=True, stop=True)

            def body(t, s):
                after(pe, xm_done, t)
                for a in range(KC):
                    pe.matmul(psG[a][:, 0:CA], xm[:, a * P:(a + 1) * P], xn[:], start=False, stop=False, skip_group_check=True)
                pe.matmul(psG[2][0:1, 0:CA], xm[:, C:CA], xn[:], start=False, stop=False, skip_group_check=True)\
                    .then_inc(acc_done, 1)
            ring(pe, body)


def fold_second_layer(nc, k, w):
    CA = C + 1
    with ExitStack() as c:
        sb = lambda name, shape, dt=F32: c.enter_context(nc.sbuf_tensor("g_" + name, shape, dt))
        sem = semaphores(nc, c, before="g_")
        raw = {n: sb("raw_" + n, [P, KC, C]) for n in ("Wq", "Wk", "Wv", "Wfc")}
        T = {n: sb("T_" + n, [P, KC, C]) for n in ("Wk", "Wv", "Wfc")}
        brow = sb("brow", [1, 2, C])
        bq = sb("bq", [P, KC])
        bsum = sb("bsum", [1, 2, C])
        wl, wr = sb("wl", [P, KC, C]), sb("wr", [P, KC, C])
        GK, gkr = sb("GK", [P, KC, C]), sb("gkr", [1, C])
        PT, M2 = sb("PT", [P, KC, C]), sb("M2", [P, KC, C])
        br = sb("br", [1, C])
        wg = sb("wg", [P, KC, 16])
        att = sb("att", [P, 2, 16])
        prod = sb("prod", [P, KC, 16])
        gi, pi = sb("gi", [P, C], I32), sb("pi", [P, KC], I32)
        gf, pf = sb("gf", [P, C]), sb("pf", [P, KC])
        ps = [c.enter_context(nc.psum_tensor(f"g_ps{a}", [P, KC, C], F32)) for a in range(3)]
        psr = c.enter_context(nc.psum_tensor("g_psr", [P, 512], F32))
        w_in, iota_done, step, turned, turned_sb, mm, mm_sb = (sem(n) for n in (
            "w_in", "iota_done", "step", "turned", "turned_sb", "mm", "mm_sb"))
        block = c.enter_context(nc.Block())
        n_loads = 4 + 2 + 1 + 2 + 3 + 1 + 2

        @block.sync
        def _(sp):
            for n in raw:
                sp.dma_start(raw[n][:], w["L1_mix_" + n].rearrange("(a p) n -> p a n", p=P)).then_inc(w_in, 16)
            sp.dma_start(brow[:, 0, :], row_of(w["L1_mix_bk"])).then_inc(w_in, 16)
            sp.dma_start(brow[:, 1, :], row_of(w["L1_mix_bv"])).then_inc(w_in, 16)
            sp.dma_start(bq[:], w["L1_mix_bq"].rearrange("(a p) -> p a", p=P),
                         allow_slow_non_contiguous=True).then_inc(w_in, 16)
            sp.dma_start(bsum[:, 0, :], row_of(w["L1_mix_bfc"])).then_inc(w_in, 16)
            sp.dma_start(bsum[:, 1, :], row_of(w["L1_gnn_b_left"])).then_inc(w_in, 16)
            sp.dma_start(wl[:], w["L1_gnn_W_left"][0:C, :].rearrange("(a p) n -> p a n", p=P)).then_inc(w_in, 16)
            sp.dma_start(k.WN[:], w["L1_gnn_W_left"][C:2 * C, :].rearrange("(a p) n -> p a n", p=P)).then_inc(w_in, 16)
            sp.dma_start(wr[:], w["L1_gnn_W_right"].rearrange("(a p) n -> p a n", p=P)).then_inc(w_in, 16)
            sp.dma_start(wg[:], w["L1_ffn_W_gat"].rearrange("(a p) n -> p a n", p=P)).then_inc(w_in, 16)
            for i, n in enumerate(("L1_ffn_att_src", "L1_ffn_att_dst")):
                sp.dma_start(att[:, i, :], w[n].rearrange("h e -> (h e)").partition_broadcast(P)).then_inc(w_in, 16)

        @block.gpsimd
        def _(pool):
            pool.iota(gi[:], [[1, C]], 0, 0).then_inc(iota_done, 1)
            pool.iota(pi[:], [[P, KC]], 0, 1).then_inc(iota_done, 1)

        @block.vector
        def _(dve):
            link = Chain(dve, step, None)
            link.start_once()
            dve.wait_ge(iota_done, 2)
            link(dve.tensor_scalar(gi[:], gi[:], 5, None, ALU.logical_shift_right))
            link(dve.tensor_scalar(pi[:], pi[:], 5, None, ALU.logical_shift_right))
            link(dve.tensor_copy(gf[:], gi[:]))
            link(dve.tensor_copy(pf[:], pi[:]))
            dve.wait_ge(w_in, 16 * n_loads)
            for a in range(KC):
                link(dve.tensor_copy(k.WG[:, a, 0:16].rearrange("p (e h) -> p e h", h=4),
                                     wg[:, a, :].rearrange("p (h e) -> p e h", e=4)))
            for i in range(2):
                link(dve.tensor_tensor(prod[:], wg[:], att[:, i, :].unsqueeze(1).to_broadcast([P, KC, 16]), ALU.mult))
                link(dve.tensor_reduce(k.WG[:, :, 16 + 4 * i:20 + 4 * i], prod[:].rearrange("p a (h e) -> p a h e", e=4), AX.X, ALU.add))
            for i, n in enumerate(T):
                dve.wait_ge(turned, i + 1)
                dve.tensor_copy(T[n][:], ps[i][:]).then_inc(turned_sb, 1)
            dve.wait_ge(mm, 1)
            dve.tensor_copy(GK[:], ps[0][:])
            dve.tensor_copy(gkr[:], psr[0:1, 0:C]).then_inc(mm_sb, 1)
            dve.wait_ge(mm, 2)
            for a in range(KC):
                link(dve.tensor_scalar(PT[:, a, :], gf[:], pf[:, a:a + 1], 1.0 / N, ALU.is_equal, ALU.mult))
            dve.tensor_tensor(PT[:], PT[:], ps[1][:], ALU.mult).then_inc(mm_sb, 1)
            dve.wait_ge(mm, 3)
            dve.tensor_copy(M2[:], ps[2][:]).then_inc(mm_sb, 1)
            link(dve.tensor_tensor(wl[:], wl[:], wr[:], ALU.add))
            link(dve.tensor_tensor(br[:], bsum[:, 0, :], bsum[:, 1, :], ALU.add))
            dve.wait_ge(mm, 4)
            link(dve.tensor_tensor(k.WS[:], wl[:], ps[0][:], ALU.add))
            dve.tensor_tensor(br[:], br[:], psr[0:1, 0:C], ALU.add).then_inc(mm_sb, 1)
            dve.wait_ge(mm, 5)
            link(dve.tensor_copy(k.bias2[:], ps[1][:, 0, :]))

        @block.tensor
        def _(pe):
            pe.wait_ge(w_in, 16 * n_loads)
            for i, n in enumerate(T):
                for a in range(KC):
                    for b in range(KC):
                        last = pe.transpose(ps[i][:, a, b * P:(b + 1) * P], raw[n][:, b, a * P:(a + 1) * P], k.ident[:])
                last.then_inc(turned, 1)
            pe.wait_ge(turned_sb, 3)
            parts = [(k.gram[:, 0, :], T["Wk"][:, 0, :]), (k.gram[:, 1, :], T["Wk"][:, 1, :]), (k.gramr[:], brow[:, 0, :])]
            for o in range(3):
                dst, cols = (ps[0][:, o, :], slice(o * P, (o + 1) * P)) if o < KC else (psr[0:1, 0:C], slice(C, CA))
                for i, (g, wk) in enumerate(parts):
                    last = pe.matmul(dst, g[:, cols], wk, start=(i == 0), stop=(i == 2))
            last.then_inc(mm, 1)
            pe.wait_ge(mm_sb, 1)
            parts = [(T["Wv"][:, 0, :], GK[:, 0, :]), (T["Wv"][:, 1, :], GK[:, 1, :]), (brow[:, 1, :], gkr[:])]
            for a in range(KC):
                for i, (v, gk) in enumerate(parts):
                    last = pe.matmul(ps[1][:, a, :], v[:, a * P:(a + 1) * P], gk, start=(i == 0), stop=(i == 2))
            last.then_inc(mm, 1)
            pe.wait_ge(mm_sb, 2)
            for a in range(KC):
                for b in range(KC):
                    last = pe.matmul(ps[2][:, a, :], PT[:, b, a * P:(a + 1) * P], T["Wfc"][:, b, :], start=(b == 0), stop=(b == KC - 1))
            last.then_inc(mm, 1)
            pe.wait_ge(mm_sb, 3)
            for a in range(KC):
                for b in range(KC):
                    pe.matmul(ps[0][:, a, :], raw["Wq"][:, b, a * P:(a + 1) * P], M2[:, b, :], start=(b == 0), stop=(b == KC - 1))
            for b in range(KC):
                last = pe.matmul(psr[0:1, 0:C], bq[:, b:b + 1], M2[:, b, :], start=(b == 0), stop=(b == KC - 1))
            last.then_inc(mm, 1)
            pe.wait_ge(mm_sb, 4)
            pe.matmul(ps[1][:, 0, :], k.ones[0:1, :], br[:], start=True, stop=True).then_inc(mm, 1)


SLE = 4


def edge_sums(nc, k):
    with ExitStack() as c:
        sb = lambda name, shape, dt=F32: c.enter_context(nc.sbuf_tensor("s_" + name, shape, dt))
        sem = semaphores(nc, c, before="s_")
        idx = sb("idx", [P, SLE, BLK], I32)
        x = sb("x", [P, SLE, BLK, C])
        same = sb("same", [P, BLK])
        carry = sb("carry", [P, C])
        idx_in = [sem(f"idx_in{s}") for s in range(SLE)]
        x_in = [sem(f"x_in{s}") for s in range(SLE)]
        stored = [sem(f"stored{s}") for s in range(SLE)]
        step, sums_done, set_done, carried = sem("step"), sem("sums_done"), sem("set_done"), sem("carried")
        lanes_in = sem("lanes_in")
        block = c.enter_context(nc.Block())
        ps = k.PS.rearrange("(p i) f -> p i f", i=LA)

        @block.sync
        def _(sp):
            prime(sp, [sums_done, carried])
            sp.dma_start(k.srci[:], k.SRCL).then_inc(lanes_in, 16)
            sp.dma_start(k.same[:], k.SAMEL).then_inc(lanes_in, 16)
            sp.wait_ge(lanes_in, 32)

            def fetch(b, s):
                after(sp, carried, b - SLE)
                sp.dma_start(idx[:, s, :], k.srci[:, bass.ds(b * BLK, BLK)]).then_inc(idx_in[s], 16)
            ring(sp, fetch, n=NBA, slots=SLE)

        @block.scalar
        def _(act):
            def store(b, s):
                after(act, sums_done, b)
                act.dma_start(ps[:, bass.ds(b * BLK, BLK), :], x[:, s]).then_inc(stored[s], 16)
            ring(act, store, n=NBA, slots=SLE)
            for s in range(SLE):
                act.wait_ge(stored[s], 16 * (NBA // SLE))

        @block.gpsimd
        def _(pool):
            def gather(b, s, free=True):
                loaded(pool, idx_in[s], b, s, slots=SLE)
                if free:
                    wait_reg(pool, stored[s], (b - s) * (16 // SLE))
                for j in range(BLK):
                    pool.indirect_dma_start(x[:, s, j, :], None, k.XN2,
                                            bass.IndirectOffsetOnAxis(ap=idx[:, s, j:j + 1], axis=0)).then_inc(x_in[s], 16)
            for s in range(SLE):
                gather(s, s, free=False)
            with pool.Fori(1, NBA // SLE) as i:
                for s in range(SLE):
                    gather(SLE * i + s, s)

        @block.vector
        def _(dve):
            ch = Chain(dve, step, BLK)
            dve.memset(carry[:], 0.0).then_inc(set_done, 1)
            dve.wait_ge(set_done, 1)
            dve.wait_ge(lanes_in, 32)

            def body(b, s):
                ch.start(b)
                ch(dve.tensor_copy(same[:], k.same[:, bass.ds(b * BLK, BLK)]))
                loaded(dve, x_in[s], b, s, per=BLK, slots=SLE)
                prev = carry[:]
                for j in range(BLK):
                    ins = dve.scalar_tensor_tensor(out=x[:, s, j, :], in0=prev, scalar=same[:, j:j + 1], in1=x[:, s, j, :],
                                                   op0=ALU.mult, op1=ALU.add)
                    prev = x[:, s, j, :]
                    if j < BLK - 1:
                        ch(ins)
                ins.then_inc(sums_done, 1)
                after(dve, sums_done, b)
                dve.tensor_copy(carry[:], prev).then_inc(carried, 1)
                after(dve, carried, b)
                ch.end()
            ring(dve, body, n=NBA, slots=SLE)


def second_layer_nodes(nc, k, w):
    with ExitStack() as c:
        sb = lambda name, shape, dt=F32: c.enter_context(nc.sbuf_tensor("m_" + name, shape, dt))
        sem = semaphores(nc, c, before="m_")
        idx = sb("idx", [P, 2, 2], I32)
        r = sb("r", [P, 2, 2, C])
        xn = sb("xn", [P, 2, C])
        x2 = sb("x2", [P, 2, C])
        rc = sb("rc", [P, NT])
        rsum, hn, xb, x3, x3n = sb("rsum", [P, C]), sb("hn", [P, C]), sb("xb", [P, C]), sb("x3", [P, C]), sb("x3n", [P, C])
        hT, yT = sb("hT", [P, 4, P]), sb("yT", [P, KC, P])
        st, mv, ve, rstd = sb("st", [P, 6]), sb("mv", [P, 2]), sb("ve", [P, 1]), sb("rstd", [P, 1])
        g = sb("g", [P, 24])
        psT = c.enter_context(nc.psum_tensor("m_psT", [P, 4, P], F32))
        psO = c.enter_context(nc.psum_tensor("m_psO", [P, 512], F32))
        psU = c.enter_context(nc.psum_tensor("m_psU", [P, KC, P], F32))
        psG = c.enter_context(nc.psum_tensor("m_psG", [P, 512], F32))
        x_in = [sem("x_in0"), sem("x_in1")]
        r_in = [sem("r_in0"), sem("r_in1")]
        names = ("idx_done", "hn_done", "xb_done", "ps_T", "sb_T", "ps_O", "x3_done", "var_ready", "rstd_ready", "xn_done",
                 "ps_U", "sb_U", "ps_G", "g_done")
        (idx_done, hn_done, xb_done, ps_T, sb_T, ps_O, x3_done, var_ready, rstd_ready, xn_done,
         ps_U, sb_U, ps_G, g_done) = tiles = [sem(n) for n in names]
        stored_x, stored_g, ln_step, step = sem("stored_x"), sem("stored_g"), sem("ln_step"), sem("step")
        rc_done = sem("rc_done")
        block = c.enter_context(nc.Block())

        @block.sync
        def _(sp):
            prime(sp, tiles, [(stored_x, 1), (stored_g, 1)])

            def load(t, s):
                after(sp, ps_T, t - 2)
                after(sp, xb_done, t - 2)
                sp.dma_start(xn[:, s, :], rows(k.XN2, t)).then_inc(x_in[s], 16)
                sp.dma_start(x2[:, s, :], rows(k.X2, t)).then_inc(x_in[s], 16)

            def store(t, s):
                after(sp, x3_done, t)
                sp.dma_start(rows(k.X3, t), x3[:]).then_inc(stored_x, 16)
                after(sp, g_done, t)
                sp.dma_start(rows(k.G, t), g[:]).then_inc(stored_g, 16)
            two_ahead(sp, load, store)
            after_dma(sp, stored_x, NT - 1)
            after_dma(sp, stored_g, NT - 1)

        @block.gpsimd
        def _(pool):
            def gather(t, s):
                after(pool, idx_done, t)
                after(pool, hn_done, t - 2)
                for i, tab in enumerate((k.PS, k.INS)):
                    pool.indirect_dma_start(r[:, s, i, :], None, tab,
                                            bass.IndirectOffsetOnAxis(ap=idx[:, s, i:i + 1], axis=0)).then_inc(r_in[s], 16)

            def power(t, s):
                after(pool, var_ready, t)
                pool.tensor_tensor(rstd[:], ve[:], k.neghalf[:], ALU.pow).then_inc(rstd_ready, 1)
            skewed(pool, gather, power)

        @block.vector
        def _(dve):
            ln = Chain(dve, ln_step, 2)
            ch = Chain(dve, step, 1)
            dve.tensor_scalar(rc[:], k.cnt[:], 1.0, None, ALU.max).then_inc(rc_done, 1)
            dve.wait_ge(rc_done, 1)
            dve.reciprocal(rc[:], rc[:]).then_inc(rc_done, 1)
            dve.wait_ge(rc_done, 2)

            def index(t, s):
                if not isinstance(t, int) or t >= 2:
                    loaded(dve, r_in[s], t - 2, s, per=2)
                dve.tensor_copy(idx[:, s, 0:1], k.pos_i[:, bass.ds(t, 1)])
                dve.tensor_copy(idx[:, s, 1:2], k.inc_i[:, bass.ds(t, 1)]).then_inc(idx_done, 1)

            def body(t, s):
                ch.start(t)
                ln.start(t)
                loaded(dve, r_in[s], t, s, per=2)
                ch(dve.tensor_tensor(rsum[:], r[:, s, 0, :], r[:, s, 1, :], ALU.add))
                after(dve, ps_T, t - 1)
                dve.tensor_scalar(hn[:], rsum[:], rc[:, bass.ds(t, 1)], None, ALU.mult).then_inc(hn_done, 1)
                loaded(dve, x_in[s], t, s, per=2)
                dve.tensor_tensor(xb[:], x2[:, s, :], k.bias2[:], ALU.add).then_inc(xb_done, 1)
                after(dve, xb_done, t)
                after(dve, ps_O, t)
                after_dma(dve, stored_x, t - 1)
                dve.tensor_tensor(x3[:], xb[:], psO[:, 0:C], ALU.add).then_inc(x3_done, 1)
                after(dve, x3_done, t)
                layernorm_dve(dve, ln, x3[:], x3n[:], st, mv, ve, rstd, var_ready, rstd_ready, xn_done, t,
                              lambda: after(dve, ps_U, t - 1))
                after(dve, ps_G, t)
                after_dma(dve, stored_g, t - 1)
                dve.tensor_copy(g[:], psG[:, 0:24]).then_inc(g_done, 1)
                ln.end()
                ch.end()
            index(0, 0)
            index(1, 1)
            body(0, 0)
            index(2, 0)
            body(1, 1)
            index(3, 1)
            with dve.Fori(1, NT // 2 - 1) as j:
                body(2 * j, 0)
                index(2 * j + 2, 0)
                body(2 * j + 1, 1)
                index(2 * j + 3, 1)
            body(NT - 2, 0)
            body(NT - 1, 1)

        @block.scalar
        def _(act):
            def body(t, s):
                after(act, ps_T, t)
                after(act, ps_O, t - 1)
                act.activation(hT[:], psT[:], ACT.Copy).then_inc(sb_T, 1)
                after(act, ps_U, t)
                after(act, ps_G, t - 1)
                act.activation(yT[:], psU[:], ACT.Copy).then_inc(sb_U, 1)
            ring(act, body)

        @block.tensor
        def _(pe):
            def body(t, s):
                loaded(pe, x_in[s], t, s, per=2)
                after(pe, sb_T, t - 1)
                for a in range(KC):
                    pe.transpose(psT[:, a, :], xn[:, s, a * P:(a + 1) * P], k.ident[:])
                after(pe, hn_done, t)
                for a in range(KC):
                    last = pe.transpose(psT[:, KC + a, :], hn[:, a * P:(a + 1) * P], k.ident[:])
                last.then_inc(ps_T, 1)
                after(pe, sb_T, t)
                after(pe, x3_done, t - 1)
                for a in range(4):
                    rhs = k.WS[:, a, :] if a < KC else k.WN[:, a - KC, :]
                    last = pe.matmul(psO[:, 0:C], hT[:, a, :], rhs, start=(a == 0), stop=(a == 3))
                last.then_inc(ps_O, 1)
                after(pe, xn_done, t)
                after(pe, sb_U, t - 1)
                for a in range(KC):
                    last = pe.transpose(psU[:, a, :], x3n[:, a * P:(a + 1) * P], k.ident[:])
                last.then_inc(ps_U, 1)
                after(pe, sb_U, t)
                after(pe, g_done, t - 1)
                for a in range(KC):
                    last = pe.matmul(psG[:, 0:24], yT[:, a, :], k.WG[:, a, :], start=(a == 0), stop=(a == KC - 1))
                last.then_inc(ps_G, 1)
            ring(pe, body)


def gat_edges(nc, k):
    GB = 16
    R = 24
    with ExitStack() as c:
        sb = lambda name, shape, dt=F32: c.enter_context(nc.sbuf_tensor("t_" + name, shape, dt))
        sem = semaphores(nc, c, before="t_")
        sd = sb("sd", [P, LG, 2], I32)
        g = sb("g", [P, LG, R])
        z = sb("z", [P, LG * HE])
        e = sb("e", [P, HE, LG])
        same, bias = sb("same", [P, LG]), sb("bias", [P, LG])
        gn = sb("gn", [P, NT, R])
        gr = sb("gr", [P, 2, GB, R])
        idx = sb("idx", [P, 2, GB], I32)
        first_f, first_i, g0 = sb("first_f", [P, 1]), sb("first_i", [P, 1], I32), sb("g0", [P, R])
        sd_in, gn_in, zeroed, zero_st, placed, z_in, first_done, g0_in, moved, idx_done, step, e_done, x_done, p_done, stored = (
            sem(n) for n in ("sd_in", "gn_in", "zeroed", "zero_st", "placed", "z_in", "first_done", "g0_in", "moved",
                             "idx_done", "step", "e_done", "x_done", "p_done", "stored"))
        g_in = [sem("g_in0"), sem("g_in1")]
        block = c.enter_context(nc.Block())
        nb = LG // GB
        pz = z[:].rearrange("p (h i) -> p h i", h=HE)

        @block.sync
        def _(sp):
            prime(sp, [moved, idx_done])
            sp.dma_start(sd[:], k.SD.rearrange("(p i) f -> p i f", i=LG)).then_inc(sd_in, 16)
            sp.dma_start(gn[:], k.G.rearrange("(t p) f -> p t f", p=P)).then_inc(gn_in, 16)
            sp.wait_ge(zeroed, 1)
            sp.dma_start(k.ZD.rearrange("(p i) f -> p (i f)", i=LG), z[:]).then_inc(zero_st, 16)
            sp.wait_ge(zero_st, 16)
            sp.wait_ge(placed, 16 * NT)
            sp.dma_start(z[:], k.ZD.rearrange("(p i) f -> p (i f)", i=LG)).then_inc(z_in, 16)
            sp.wait_ge(p_done, 1)
            sp.dma_start(k.PG.rearrange("(p i) f -> p i f", i=LG), g[:]).then_inc(stored, 16)
            sp.wait_ge(stored, 16)

        @block.gpsimd
        def _(pool):
            pool.memset(z[:], 0.0).then_inc(zeroed, 1)
            pool.wait_ge(gn_in, 16)
            pool.wait_ge(zero_st, 16)
            for t in range(NT):
                pool.indirect_dma_start(k.ZD, bass.IndirectOffsetOnAxis(ap=k.start2_i[:, t:t + 1], axis=0),
                                        gn[:, t, 20:24], None).then_inc(placed, 16)
            pool.wait_ge(first_done, 1)
            pool.indirect_dma_start(g0[:], None, k.G, bass.IndirectOffsetOnAxis(ap=first_i[:], axis=0)).then_inc(g0_in, 16)

            def gather(b, s):
                after(pool, idx_done, b)
                after(pool, moved, b - 2)
                for j in range(GB):
                    pool.indirect_dma_start(gr[:, s, j, :], None, k.G,
                                            bass.IndirectOffsetOnAxis(ap=idx[:, s, j:j + 1], axis=0)).then_inc(g_in[s], 16)
            ring(pool, gather, n=nb)

        @block.vector
        def _(dve):
            link = Chain(dve, step, None)
            link.start_once()
            dve.wait_ge(sd_in, 16)
            link(dve.tensor_copy(bias[:], sd[:, :, 1]))
            link(dve.tensor_copy(k.first2[:], bias[:, 0:1]))
            link(dve.tensor_copy(k.last2[:], bias[:, LG - 1:LG]))
            link(dve.memset(same[:, 0:1], 0.0))
            link(dve.tensor_tensor(same[:, 1:LG], bias[:, 1:LG], bias[:, 0:LG - 1], ALU.is_equal))
            link(dve.tensor_scalar(bias[:], same[:], -1.0, BIG, ALU.add, ALU.mult))
            link(dve.tensor_scalar(first_f[:], k.first2[:], float(NP - 1), None, ALU.min))
            dve.tensor_copy(first_i[:], first_f[:]).then_inc(first_done, 1)

            def index(b, s):
                dve.tensor_copy(idx[:, s, :], sd[:, bass.ds(b * GB, GB), 0]).then_inc(idx_done, 1)

            def move(b, s):
                loaded(dve, g_in[s], b, s, per=GB)
                dve.tensor_copy(g[:, bass.ds(b * GB, GB), :], gr[:, s]).then_inc(moved, 1)
            index(0, 0)
            index(1, 1)
            with dve.Fori(0, nb // 2 - 1) as j:
                move(2 * j, 0)
                index(2 * j + 2, 0)
                move(2 * j + 1, 1)
                index(2 * j + 3, 1)
            move(nb - 2, 0)
            move(nb - 1, 1)
            after(dve, moved, nb - 1)
            dve.wait_ge(z_in, 16)
            dve.wait_ge(g0_in, 16)
            zi = z[:].rearrange("p (i h) -> p i h", h=HE)
            link(dve.tensor_copy(zi[:, 0, :], g0[:, 20:24]))
            for h in range(HE):
                link(dve.tensor_tensor_scan(e[:, h, :], same[:], zi[:, :, h], 0.0, ALU.mult, ALU.add))
            link(dve.tensor_tensor(e[:], e[:], g[:, :, 16:20].rearrange("p i h -> p h i"), ALU.add))
            link(dve.scalar_tensor_tensor(out=e[:], in0=e[:], scalar=0.2, in1=e[:], op0=ALU.mult, op1=ALU.max))
            for h in range(HE):
                link(dve.tensor_tensor_scan(g[:, :, 20 + h], bias[:], e[:, h, :], -BIG, ALU.add, ALU.max))
            M = g[:, :, 20:24].rearrange("p i h -> p h i")
            link(dve.tensor_tensor(pz, e[:], M, ALU.subtract))
            link(dve.memset(e[:, :, 0:1], -BIG))
            link(dve.tensor_tensor(e[:, :, 1:LG], M[:, :, 0:LG - 1], M[:, :, 1:LG], ALU.subtract))
            dve.tensor_tensor(e[:, :, 1:LG], e[:, :, 1:LG], bias[:, 1:LG].unsqueeze(1).to_broadcast([P, HE, LG - 1]), ALU.add)\
                .then_inc(e_done, 1)
            dve.wait_ge(x_done, 2)
            for x in range(HE):
                cols = g[:, :, x * HE:(x + 1) * HE].rearrange("p i h -> p h i")
                link(dve.tensor_tensor(cols, cols, pz, ALU.mult))
            for h in range(HE):
                for col in [x * HE + h for x in range(HE)]:
                    link(dve.tensor_tensor_scan(g[:, :, col], e[:, h, :], g[:, :, col], 0.0, ALU.mult, ALU.add))
                last = dve.tensor_tensor_scan(g[:, :, 16 + h], e[:, h, :], pz[:, h, :], 0.0, ALU.mult, ALU.add)
                if h < HE - 1:
                    link(last)
            last.then_inc(p_done, 1)

        @block.scalar
        def _(act):
            act.wait_ge(e_done, 1)
            act.activation(pz, pz, ACT.Exp).then_inc(x_done, 1)
            act.activation(e[:], e[:], ACT.Exp).then_inc(x_done, 1)


def gat_gates(nc, k, w):
    R = 24
    with ExitStack() as c:
        sb = lambda name, shape, dt=F32: c.enter_context(nc.sbuf_tensor("h_" + name, shape, dt))
        sem = semaphores(nc, c, before="h_")
        r = sb("r", [P, 2, NT, R])
        Mx = sb("Mx", [P, NT, HE])
        D = sb("D", [P, 2, NT, HE])
        T = sb("T", [P, 2, NT, 5 * HE])
        rz = sb("rz", [P, NT, HE])
        A, B = sb("A", [P, NT, 16]), sb("B", [P, NT, 16])
        vec, vecp = sb("vec", [P, 3, 16]), sb("vecp", [P, 3, 16])
        mean, var, rstd = sb("mean", [P, NT]), sb("var", [P, NT]), sb("rstd", [P, NT])
        s4, oh1, oh2, cand = sb("s4", [P, NT, HE]), sb("oh1", [P, NT, HE]), sb("oh2", [P, NT, HE]), sb("cand", [P, NT, HE])
        m1, m2, mn, ex, w1, w2 = (sb(n, [P, NT]) for n in ("m1", "m2", "mn", "ex", "w1", "w2"))
        im = sb("im", [P, HE])
        v_in, r_in, step, d_done, d_exp, var_done, rstd_done, x_done, x_exp = (sem(n) for n in (
            "v_in", "r_in", "step", "d_done", "d_exp", "var_done", "rstd_done", "x_done", "x_exp"))
        block = c.enter_context(nc.Block())

        @block.sync
        def _(sp):
            for i, n in enumerate(("L1_ffn_b_gat", "L1_ffn_ln_gamma", "L1_ffn_ln_beta")):
                sp.dma_start(vec[:, i, :], w[n].partition_broadcast(P)).then_inc(v_in, 16)

        @block.gpsimd
        def _(pool):
            for t in range(NT):
                for i, (tab, ix) in enumerate(((k.PG, k.pos2_i), (k.ING, k.inc2_i))):
                    pool.indirect_dma_start(r[:, i, t, :], None, tab,
                                            bass.IndirectOffsetOnAxis(ap=ix[:, t:t + 1], axis=0)).then_inc(r_in, 16)
            pool.wait_ge(var_done, 1)
            pool.tensor_tensor(rstd[:], var[:], k.neghalf[:].to_broadcast([P, NT]), ALU.pow).then_inc(rstd_done, 1)

        @block.scalar
        def _(act):
            act.wait_ge(d_done, 1)
            act.activation(D[:], D[:], ACT.Exp).then_inc(d_exp, 1)
            act.wait_ge(x_done, 1)
            act.activation(ex[:], ex[:], ACT.Exp).then_inc(x_exp, 1)

        @block.vector
        def _(dve):
            link = Chain(dve, step, None)
            link.start_once()
            dve.wait_ge(v_in, 48)
            link(dve.tensor_copy(vecp[:].rearrange("p v (e h) -> p v e h", h=HE), vec[:].rearrange("p v (h e) -> p v e h", e=HE)))
            link(dve.tensor_scalar(im[:], k.iota[:, 0:HE], float(-HE), None, ALU.add))
            dve.wait_ge(r_in, 16 * 2 * NT)
            m = r[:, :, :, 20:24]
            link(dve.tensor_tensor(Mx[:], m[:, 0], m[:, 1], ALU.max))
            link(dve.tensor_tensor(D[:, 0], m[:, 0], Mx[:], ALU.subtract))
            dve.tensor_tensor(D[:, 1], m[:, 1], Mx[:], ALU.subtract).then_inc(d_done, 1)
            dve.wait_ge(d_exp, 1)
            for i in range(2):
                link(dve.tensor_tensor(T[:, i].rearrange("p t (d h) -> p t d h", h=HE),
                                       r[:, i, :, 0:20].rearrange("p t (d h) -> p t d h", h=HE),
                                       D[:, i].unsqueeze(2).to_broadcast([P, NT, 5, HE]), ALU.mult))
            link(dve.tensor_tensor(T[:, 0], T[:, 0], T[:, 1], ALU.add))
            link(dve.tensor_scalar(rz[:], T[:, 0, :, 16:20], 1e-16, None, ALU.add))
            link(dve.reciprocal(rz[:], rz[:]))
            link(dve.tensor_tensor(A[:].rearrange("p t (e h) -> p t e h", h=HE),
                                   T[:, 0, :, 0:16].rearrange("p t (e h) -> p t e h", h=HE),
                                   rz[:].unsqueeze(2).to_broadcast([P, NT, HE, HE]), ALU.mult))

            def vector(i):
                return vecp[:, i, :].unsqueeze(1).to_broadcast([P, NT, 16])

            def over(ap, n):
                return ap.unsqueeze(2).to_broadcast([P, NT, n])
            link(dve.tensor_tensor(A[:], A[:], vector(0), ALU.add))
            link(dve.tensor_reduce(mean[:], A[:], AX.X, ALU.add))
            link(dve.tensor_scalar(mean[:], mean[:], 1.0 / 16, None, ALU.mult))
            link(dve.tensor_tensor(A[:], A[:], over(mean[:], 16), ALU.subtract))
            link(dve.tensor_tensor(B[:], A[:], A[:], ALU.mult))
            link(dve.tensor_reduce(var[:], B[:], AX.X, ALU.add))
            dve.tensor_scalar(var[:], var[:], 1.0 / 16, LN_EPS, ALU.mult, ALU.add).then_inc(var_done, 1)
            dve.wait_ge(rstd_done, 1)
            link(dve.tensor_tensor(A[:], A[:], over(rstd[:], 16), ALU.mult))
            link(dve.tensor_tensor(A[:], A[:], vector(1), ALU.mult))
            link(dve.tensor_tensor(A[:], A[:], vector(2), ALU.add))
            link(dve.tensor_reduce(s4[:], A[:].rearrange("p t (e h) -> p t e h", h=HE), AX.X, ALU.add))
            link(dve.tensor_scalar(s4[:], s4[:], 1.0 / HE, None, ALU.mult))

            def best(mx, oh):
                imb = im[:].unsqueeze(1).to_broadcast([P, NT, HE])
                link(dve.tensor_reduce(mx[:], s4[:], AX.X, ALU.max))
                link(dve.tensor_tensor(cand[:], s4[:], over(mx[:], HE), ALU.is_equal))
                link(dve.tensor_tensor(cand[:], cand[:], imb, ALU.mult))
                link(dve.tensor_reduce(mn[:], cand[:], AX.X, ALU.min))
                link(dve.tensor_tensor(oh[:], imb, over(mn[:], HE), ALU.is_equal))
            best(m1, oh1)
            link(dve.scalar_tensor_tensor(out=s4[:], in0=oh1[:], scalar=-BIG, in1=s4[:], op0=ALU.mult, op1=ALU.add))
            best(m2, oh2)
            dve.tensor_tensor(ex[:], m2[:], m1[:], ALU.subtract).then_inc(x_done, 1)
            dve.wait_ge(x_exp, 1)
            link(dve.tensor_scalar(w1[:], ex[:], 1.0, None, ALU.add))
            link(dve.reciprocal(w1[:], w1[:]))
            link(dve.tensor_tensor(w2[:], ex[:], w1[:], ALU.mult))
            link(dve.tensor_tensor(oh1[:], oh1[:], over(w1[:], HE), ALU.mult))
            link(dve.tensor_tensor(oh2[:], oh2[:], over(w2[:], HE), ALU.mult))
            link(dve.tensor_tensor(k.gate[:], oh1[:], oh2[:], ALU.add))


def program(nc, w, out, scratch):
    k = Core()
    with ExitStack() as c:
        sb = lambda name, shape, dt=F32: c.enter_context(nc.sbuf_tensor(name, shape, dt))
        k.ident, k.ones = sb("ident", [P, P]), sb("ones", [P, P])
        k.low, k.upper = sb("low", [P, P]), sb("upper", [P, P])
        k.neghalf, k.half = sb("neghalf", [P, 1]), sb("half", [P, 1])
        k.valid, k.nodef = sb("valid", [P, NT]), sb("nodef", [P, NT])
        k.iota, k.part = sb("iota", [P, P]), sb("part", [P, 1])
        k.zero1 = k.low[0:1, :]
        k.M1 = sb("M1", [P, KC, C])
        k.XP = scratch("XP", [NP, C])
        k.Q, k.KV, k.MV = scratch("Q", [NP, C]), scratch("KV", [NP, 2 * C]), scratch("MV", [NP, 2 * C])
        k.X1M, k.X1 = scratch("X1M", [NP, C]), scratch("X1", [NP, C])
        WA = (DK + 2) * HEADS
        k.PT, k.INC = scratch("PT", [P * LA, WA]), scratch("INC", [P + 1, WA])
        k.SRCL, k.SAMEL = scratch("SRCL", [P, LA], I32), scratch("SAMEL", [P, LA])
        k.first, k.last = sb("first", [P, 1]), sb("last", [P, 1])
        k.cnt, k.start = sb("cnt", [P, NT]), sb("start", [P, NT])
        k.pos_i, k.inc_i = sb("pos_i", [P, NT], I32), sb("inc_i", [P, NT], I32)
        k.X2, k.XN2, k.X3 = scratch("X2", [NP, C]), scratch("XN2", [NP, C]), scratch("X3", [NP, C])
        k.PS, k.INS = scratch("PS", [P * LA, C]), scratch("INS", [P + 1, C])
        k.G = scratch("G", [NP, 24])
        k.gram, k.gramr = sb("gram", [P, KC, C + 1]), sb("gramr", [1, C + 1])
        k.WS, k.WN, k.WG = sb("WS", [P, KC, C]), sb("WN", [P, KC, C]), sb("WG", [P, KC, 24])
        k.bias2 = sb("bias2", [P, C])
        k.cnt2, k.start2 = sb("cnt2", [P, HG]), sb("start2", [P, HG])
        k.start2_i, k.pos2_i, k.inc2_i = (sb(n, [P, HG], I32) for n in ("start2_i", "pos2_i", "inc2_i"))
        k.first2, k.last2 = sb("first2", [P, 1]), sb("last2", [P, 1])
        k.gate = sb("kgate", [P, NT, HE])
        k.SD, k.ZD = scratch("SD", [P * LG, 2], I32), scratch("ZD", [P * LG, HE])
        k.PG, k.ING = scratch("PG", [P * LG, 24]), scratch("ING", [P + 1, 24])
        constants(nc, k, w["x"])
        with ExitStack() as ca:
            lane = lambda name, dt: ca.enter_context(nc.sbuf_tensor(name, [P, LA], dt))
            k.srci, k.dsti, k.same = lane("srci", I32), lane("dsti", I32), lane("same", F32)
            project_nodes(nc, k, w)
            mix_output(nc, k, w)
            lane_lists(nc, k, w)
            rank_nodes(nc, k, k.cnt[:], NT, LA, k.start[:], k.pos_i[:], k.inc_i[:], "_a")
            edge_attention(nc, k)
            join_lanes(nc, k, k.PT, LA, k.last[:, 0:1], k.first[:, 0:1], HEADS, DK + 1, float(DK) ** -0.5, k.INC, "_a")
            attention_output(nc, k, w)
        with ExitStack() as cg:
            k.pair = cg.enter_context(nc.sbuf_tensor("pair", [P, TG, 2], I32))
            k.lo, k.hi, k.dcol = (cg.enter_context(nc.sbuf_tensor(n, [P, TG], F32)) for n in ("glo", "ghi", "dcol"))
            gat_count(nc, k, w)
            rank_nodes(nc, k, k.cnt2[:], HG, LG, k.start2[:], k.pos2_i[:], k.inc2_i[:], "_g")
            routed_ffn(nc, k, w, False, k.X1, k.X2)
        with ExitStack() as ca:
            lane = lambda name, dt: ca.enter_context(nc.sbuf_tensor(name, [P, LA], dt))
            k.srci, k.same = lane("srci2", I32), lane("same2", F32)
            normed_nodes(nc, k, w)
            fold_second_layer(nc, k, w)
            edge_sums(nc, k)
            join_lanes(nc, k, k.PS, LA, k.last[:, 0:1], k.first[:, 0:1], 0, C, 1.0, k.INS, "_s")
            second_layer_nodes(nc, k, w)
        gat_edges(nc, k)
        join_lanes(nc, k, k.PG, LG, k.last2[:, 0:1], k.first2[:, 0:1], HE, 5, 1.0, k.ING, "_g")
        gat_gates(nc, k, w)
        routed_ffn(nc, k, w, True, k.X3, out)


_OUTS = [((N, C), "float32")]


def kernel(**inputs):
    import numpy as _np
    import concourse.bacc as _bacc
    from concourse import mybir as _mybir
    from concourse.bass_utils import run_bass_kernel_spmd as _run

    nc = _bacc.Bacc("TRN2", target_bir_lowering=False, num_devices=1)
    arrays, args = {}, {}
    for name in inputs:
        a = _np.ascontiguousarray(inputs[name])
        arrays[f"in_{name}_dram"] = a
        args[name] = nc.dram_tensor(f"in_{name}_dram", a.shape, _mybir.dt.from_np(a.dtype), kind="ExternalInput").ap()
    out = nc.dram_tensor("out_0_dram", (N, C), _mybir.dt.float32, kind="ExternalOutput").ap()

    def scratch(name, shape, dt=_mybir.dt.float32):
        return nc.dram_tensor(name, shape, dt, kind="Internal").ap()

    program(nc, args, out, scratch)
    r = _run(nc, [arrays], core_ids=[0])
    return r.results[0]["out_0_dram"]
```

```python
from contextlib import ExitStack

import numpy as np
import concourse.bass as bass
from concourse import mybir

ALU = mybir.AluOpType
ACT = mybir.ActivationFunctionType
F32 = mybir.dt.float32
BF16 = mybir.dt.bfloat16
I32 = mybir.dt.int32
AX = mybir.AxisListType

P = 128
N = 6250
C = 256
NT = 50
NP = NT * P
KC = C // P
LN_EPS = 1e-5
BIG = 1e30

PRIME = 6


def wait_reg(eng, sem, value):
    eng.wait_ge(sem, value)
    if not isinstance(value, int):
        eng.nop(nofuse=True)


def after(eng, sem, t):
    wait_reg(eng, sem, t + 1 + PRIME)


def after_dma(eng, sem, t, per=1):
    wait_reg(eng, sem, (t + 1 + PRIME) * (16 * per))


def loaded(eng, sem, t, s, per=1, slots=2):
    wait_reg(eng, sem, (t - s) * (16 * per // slots) + 16 * per)


class Chain:

    def __init__(self, eng, sem, per):
        self.eng, self.sem, self.per = eng, sem, per

    def start_once(self):
        self.base, self.k = 0, 0

    def start(self, t):
        self.base, self.k = t * self.per, 0

    def __call__(self, ins):
        self.k += 1
        ins.then_inc(self.sem, 1)
        wait_reg(self.eng, self.sem, self.base + self.k)

    def end(self):
        assert self.k == self.per, (self.k, self.per)


def skewed(eng, head, tail, n=NT):
    head(0, 0)
    with eng.Fori(0, n // 2 - 1) as j:
        head(2 * j + 1, 1)
        tail(2 * j, 0)
        head(2 * j + 2, 0)
        tail(2 * j + 1, 1)
    head(n - 1, 1)
    tail(n - 2, 0)
    tail(n - 1, 1)


def two_ahead(eng, head, tail, n=NT):
    head(0, 0)
    head(1, 1)
    with eng.Fori(0, n // 2 - 1) as j:
        head(2 * j + 2, 0)
        tail(2 * j, 0)
        head(2 * j + 3, 1)
        tail(2 * j + 1, 1)
    tail(n - 2, 0)
    tail(n - 1, 1)


def ring(eng, body, n=NT, slots=2, first=0):
    with eng.Fori(first // slots, n // slots) as j:
        for s in range(slots):
            body(slots * j + s, s)


def semaphores(nc, c, before="", after=""):
    held = []

    def sem(name):
        held.append(nc.alloc_semaphore(before + name + after))
        return held[-1]

    def clear():
        nc.clear_and_free_semaphores(held)
        nc.all_engine_barrier()
    c.callback(clear)
    return sem


class Core:
    pass


def rows(ap, t):
    return ap[bass.ds(t * P, P), :] if not isinstance(t, int) else ap[t * P:(t + 1) * P, :]


def row_of(ap):
    return ap.rearrange("(a n) -> a n", a=1)


def prime(sp, sems, dma_sems=()):
    for s in sems:
        sp.sem_inc(s, PRIME)
    for s, per in dma_sems:
        sp.sem_inc(s, 16 * PRIME * per)


def constants(nc, k, x):
    with ExitStack() as c:
        zeros = c.enter_context(nc.sbuf_tensor("zeros", [P, C], F32))
        node = c.enter_context(nc.sbuf_tensor("node", [P, NT], I32))
        itmp = c.enter_context(nc.sbuf_tensor("itmp", [P, P], I32))
        ipart = c.enter_context(nc.sbuf_tensor("ipart", [P, 1], I32))
        sem = semaphores(nc, c)
        s_set, s_copied, s_iota, s_mask = (sem(n) for n in ("const_set", "x_copied", "const_iota", "const_mask"))
        block = c.enter_context(nc.Block())

        @block.gpsimd
        def _(pool):
            pool.memset(zeros[:], 0.0).then_inc(s_set, 1)
            pool.memset(k.ident[:], 0.0).then_inc(s_set, 1)
            pool.memset(k.ones[:], 1.0).then_inc(s_set, 1)
            pool.memset(k.neghalf[:], -0.5).then_inc(s_set, 1)
            pool.memset(k.half[:], 0.5).then_inc(s_set, 1)
            pool.memset(k.low[:], 1.0).then_inc(s_set, 1)
            pool.memset(k.upper[:], 1.0).then_inc(s_set, 1)
            pool.wait_ge(s_set, 7)
            pool.affine_select(out=k.ident[:], in_=k.ident[:], compare_op=ALU.not_equal, fill=1.0,
                               base=0, pattern=[[-1, P]], channel_multiplier=1).then_inc(s_set, 1)
            pool.affine_select(out=k.low[:], in_=k.low[:], compare_op=ALU.is_gt, fill=0.0,
                               base=0, pattern=[[-1, P]], channel_multiplier=1).then_inc(s_set, 1)
            pool.affine_select(out=k.upper[:], in_=k.upper[:], compare_op=ALU.is_gt, fill=0.0,
                               base=0, pattern=[[1, P]], channel_multiplier=-1).then_inc(s_set, 1)
            pool.iota(node[:], [[P, NT]], 0, 1).then_inc(s_iota, 1)
            pool.iota(itmp[:], [[1, P]], 0, 0).then_inc(s_iota, 1)
            pool.iota(ipart[:], [[1, 1]], 0, 1).then_inc(s_iota, 1)
            pool.wait_ge(s_set, 10)

        @block.vector
        def _(dve):
            dve.wait_ge(s_iota, 3)
            dve.tensor_scalar(k.valid[:], node[:], float(N), None, ALU.is_lt).then_inc(s_mask, 1)
            dve.tensor_copy(k.nodef[:], node[:]).then_inc(s_mask, 1)
            dve.tensor_copy(k.iota[:], itmp[:]).then_inc(s_mask, 1)
            dve.tensor_copy(k.part[:], ipart[:]).then_inc(s_mask, 1)
            dve.wait_ge(s_mask, 4)

        @block.sync
        def _(sp):
            sp.dma_start(k.XP[0:N, :], x).then_inc(s_copied, 16)
            sp.wait_ge(s_set, 1)
            tail = NP - N
            sp.dma_start(k.XP[N:N + P, :], zeros[:]).then_inc(s_copied, 16)
            sp.dma_start(k.XP[N + P:NP, :], zeros[0:tail - P, :]).then_inc(s_copied, 16)
            sp.wait_ge(s_copied, 48)


def layernorm_dve(dve, link, xt, xn, st, mv, ve, rstd, var_ready, rstd_ready, xn_done, t, wait_xn_free):
    link(dve.bn_stats(st[:], xt))
    link(dve.bn_aggr(mv[:], st[:]))
    dve.tensor_scalar(ve[:], mv[:, 1:2], LN_EPS, None, ALU.add).then_inc(var_ready, 1)
    wait_xn_free()
    after(dve, rstd_ready, t)
    dve.tensor_scalar(xn, xt, mv[:, 0:1], rstd[:, 0:1], ALU.subtract, ALU.mult).then_inc(xn_done, 1)
    after(dve, xn_done, t)


EA = 206250
BLK = 13
LA = 1612
NBA = LA // BLK
HEADS = 8
DK = C // HEADS


class LaneLists:

    full = EA // LA
    rest = EA - full * LA
    slots = 6

    def __init__(self, nc, k, w, c, sem):
        self.k, self.w = k, w
        sb = lambda name, shape, dt=F32: c.enter_context(nc.sbuf_tensor("l_" + name, shape, dt))
        self.lo_i, self.lo = sb("lo_i", [P, LA], I32), sb("lo", [P, LA])
        self.hi_i, self.hi = sb("hi_i", [P, LA], I32), sb("hi", [P, LA])
        self.dstf = sb("dstf", [P, LA])
        self.oh_lo = sb("oh_lo", [P, self.slots, BLK, P], BF16)
        self.oh_hi = sb("oh_hi", [P, self.slots, BLK, NT], BF16)
        self.psC = c.enter_context(nc.psum_tensor("l_psC", [P, NT], F32))
        self.set_done, self.in_done, self.dve_done = sem("l_set_done"), sem("l_in_done"), sem("l_dve_step")
        self.onehots, self.counted = sem("l_onehots"), sem("l_counted")
        self.same_done, self.kept = sem("l_same_done"), sem("l_kept")

    def primed(self):
        return [self.onehots, self.counted]

    def load(self, sp):
        k, full, rest = self.k, self.full, self.rest
        sp.wait_ge(self.set_done, 2)
        for tile, src in ((k.srci, self.w["src"]), (k.dsti, self.w["dst"])):
            sp.dma_start(tile[0:full, :], src[0:full * LA].rearrange("(p i) -> p i", i=LA)).then_inc(self.in_done, 16)
            sp.dma_start(tile[full:P, 0:rest], row_of(src[full * LA:EA])).then_inc(self.in_done, 16)

    def keep(self, sp):
        sp.wait_ge(self.in_done, 64)
        sp.wait_ge(self.same_done, 1)
        sp.dma_start(self.k.SRCL, self.k.srci[:]).then_inc(self.kept, 16)
        sp.dma_start(self.k.SAMEL, self.k.same[:]).then_inc(self.kept, 16)
        sp.wait_ge(self.kept, 32)

    def pad(self, pool):
        pool.memset(self.k.srci[:], 0).then_inc(self.set_done, 1)
        pool.memset(self.k.dsti[:], N).then_inc(self.set_done, 1)

    def dve_start(self, dve):
        k, dstf = self.k, self.dstf
        link = self.link = Chain(dve, self.dve_done, None)
        link.start_once()
        dve.wait_ge(self.in_done, 64)
        link(dve.tensor_scalar(self.lo_i[:], k.dsti[:], P - 1, None, ALU.bitwise_and))
        link(dve.tensor_scalar(self.hi_i[:], k.dsti[:], 7, None, ALU.logical_shift_right))
        link(dve.tensor_copy(self.lo[:], self.lo_i[:]))
        link(dve.tensor_copy(self.hi[:], self.hi_i[:]))
        link(dve.tensor_copy(dstf[:], k.dsti[:]))
        link(dve.memset(k.same[:, 0:1], 0.0))
        dve.tensor_tensor(k.same[:, 1:LA], dstf[:, 1:LA], dstf[:, 0:LA - 1], ALU.is_equal).then_inc(self.same_done, 1)
        link(dve.tensor_copy(k.first[:], dstf[:, 0:1]))
        link(dve.tensor_copy(k.last[:], dstf[:, LA - 1:LA]))

    def dve_step(self, dve, b, s):
        k = self.k
        after(dve, self.counted, b - self.slots)
        dve.tensor_tensor(self.oh_lo[:, s], k.iota[:].unsqueeze(1).to_broadcast([P, BLK, P]),
                          self.lo[:, bass.ds(b * BLK, BLK)].unsqueeze(2).to_broadcast([P, BLK, P]), ALU.is_equal)
        dve.tensor_tensor(self.oh_hi[:, s], k.iota[:, 0:NT].unsqueeze(1).to_broadcast([P, BLK, NT]),
                          self.hi[:, bass.ds(b * BLK, BLK)].unsqueeze(2).to_broadcast([P, BLK, NT]), ALU.is_equal)\
            .then_inc(self.onehots, 1)

    def dve_end(self, dve):
        after(dve, self.counted, NBA - 1)
        self.link(dve.tensor_copy(self.k.cnt[:], self.psC[:]))

    def pe_start(self, pe):
        pe.wait_ge(self.in_done, 64)
        pe.matmul(self.psC[:], self.k.zero1[:], self.k.ones[0:1, 0:NT], start=True, stop=True)

    def pe_step(self, pe, b, s):
        after(pe, self.onehots, b)
        for j in range(BLK):
            last = pe.matmul(self.psC[:], self.oh_lo[:, s, j, :], self.oh_hi[:, s, j, :],
                             start=False, stop=False, skip_group_check=True)
        last.then_inc(self.counted, 1)


def project_nodes(nc, k, w):
    W3 = 6 * C
    with ExitStack() as c:
        sb = lambda name, shape, dt=F32: c.enter_context(nc.sbuf_tensor(name, shape, dt))
        sem = semaphores(nc, c)
        wcat = sb("wcat", [P, KC, W3])
        bcat = sb("bcat", [P, W3])
        wout = sb("wout", [P, KC, C])
        xt = sb("xt", [P, 2, C])
        xn = sb("xn", [P, C])
        st, mv, ve, rstd = sb("st", [P, 6]), sb("mv", [P, 2]), sb("ve", [P, 1]), sb("rstd", [P, 1])
        xT = sb("xT", [P, KC, P])
        allp = sb("allp", [P, W3])
        mean = sb("mean", [P, 2])
        nmean = sb("nmean", [P, 2])
        sq = sb("sq", [P, 2, C])
        s2 = sb("s2", [P, 2])
        s2e = sb("s2e", [P, 2])
        r2 = sb("r2", [P, 2])
        q4s = sb("q4s", [P, 1])
        q4 = sb("q4", [P, 1])
        qn = sb("qn", [P, 1])
        qr = sb("qr", [P, 1])
        junk = sb("junk", [P, C])
        k2 = sb("k2", [P, C])
        k4 = sb("k4", [P, C])
        q2 = sb("q2", [P, C])
        kvT = sb("kvT", [P, KC, C])
        cn = sb("cn", [P, KC])
        cr = sb("cr", [P, KC])
        psT = c.enter_context(nc.psum_tensor("psT", [P, KC, P], F32))
        psP = c.enter_context(nc.psum_tensor("psP", [P, 3, 512], F32))
        psK = c.enter_context(nc.psum_tensor("psK", [P, KC, C], F32))
        psN = c.enter_context(nc.psum_tensor("psN", [P, 512], F32))
        psM = c.enter_context(nc.psum_tensor("psM", [P, KC, C], F32))
        w_in = sem("w_in")
        x_in = [sem("x_in0"), sem("x_in1")]
        var_ready, rstd_ready, xn_done = sem("var_ready"), sem("rstd_ready"), sem("xn_done")
        xT_ps, xT_sb, proj_done, evac_done = sem("xT_ps"), sem("xT_sb"), sem("proj_done"), sem("evac_done")
        mean_done, sq_done, q4_done, k2_done, k4_done = (sem(n) for n in
                                                         ("mean_done", "sq_done", "q4_done", "k2_done", "k4_done"))
        q2_done, acc_done = sem("q2_done"), sem("acc_done")
        stored_q, stored_kv, stored_m = sem("stored_q"), sem("stored_kv"), sem("stored_m")
        ln_step, mix_step, act_step = sem("ln_step"), sem("mix_step"), sem("act_step")
        kvT_sb, norm_sb, root_done, kvw_ps, fin = (sem(n) for n in
                                                       ("kvT_sb", "norm_sb", "root_done", "kvw_ps", "fin"))
        tiles = [var_ready, rstd_ready, xn_done, xT_ps, xT_sb, proj_done, evac_done, mean_done, sq_done,
                 q4_done, k2_done, k4_done, q2_done, acc_done]
        lists = LaneLists(nc, k, w, c, sem)
        block = c.enter_context(nc.Block())
        G = LaneLists.slots // 2
        with_blocks = NBA // (2 * G)
        assert with_blocks < NT // 2

        def beside(eng, head, tail, step):
            def pair(j, blocks):
                for g, s in ((2 * j, 0), (2 * j + 1, 1)):
                    def fill(i):
                        if blocks:
                            step(eng, g * G + i, s * G + i)
                    head(g + 1, 1 - s, fill)
                    tail(g, s, fill)

            def no_fill(i):
                pass
            head(0, 0, no_fill)
            with eng.Fori(0, with_blocks) as j:
                pair(j, True)
            with eng.Fori(with_blocks, NT // 2 - 1) as j:
                pair(j, False)
            for b in range(with_blocks * 2 * G, NBA):
                step(eng, b, b % (2 * G))
            head(NT - 1, 1, no_fill)
            tail(NT - 2, 0, no_fill)
            tail(NT - 1, 1, no_fill)

        @block.sync
        def _(sp):
            prime(sp, tiles + lists.primed(), [(stored_q, 1), (stored_kv, 1), (stored_m, 2)])
            cols = [(w["L0_gnn_Wq"], 0, C), (w["L0_gnn_Wk"], C, C), (w["L0_gnn_Wv"], 2 * C, C),
                    (w["L0_mix_W_qkv"], 3 * C, 3 * C)]
            for src, o, n in cols:
                sp.dma_start(wcat[:, :, o:o + n], src.rearrange("(a p) n -> p a n", p=P)).then_inc(w_in, 16)
            for src, o, n in [(w["L0_gnn_bq"], 0, C), (w["L0_gnn_bk"], C, C), (w["L0_gnn_bv"], 2 * C, C),
                              (w["L0_mix_b_qkv"], 3 * C, 3 * C)]:
                sp.dma_start(bcat[:, o:o + n], src.partition_broadcast(P)).then_inc(w_in, 16)
            sp.dma_start(wout[:], w["L0_mix_W_out"].rearrange("(a p) n -> p a n", p=P)).then_inc(w_in, 16)
            lists.load(sp)

            def store(t, s):
                after(sp, evac_done, t)
                sp.dma_start(rows(k.Q, t), allp[:, 0:C]).then_inc(stored_q, 16)
                sp.dma_start(rows(k.KV, t), allp[:, C:3 * C]).then_inc(stored_kv, 16)
                sp.dma_start(rows(k.MV, t)[:, C:2 * C], allp[:, 5 * C:6 * C]).then_inc(stored_m, 16)
                after(sp, q2_done, t)
                sp.dma_start(rows(k.MV, t)[:, 0:C], q2[:]).then_inc(stored_m, 16)
            ring(sp, store)
            lists.keep(sp)
            after_dma(sp, stored_q, NT - 1)
            after_dma(sp, stored_kv, NT - 1)
            after_dma(sp, stored_m, NT - 1, 2)

        @block.gpsimd
        def _(pool):
            lists.pad(pool)

            def head(t, s):
                after(pool, xn_done, t - 2)
                pool.dma_start(xt[:, s, :], rows(k.XP, t)).then_inc(x_in[s], 16)
                after(pool, var_ready, t)
                pool.tensor_tensor(rstd[:], ve[:], k.neghalf[:], ALU.pow).then_inc(rstd_ready, 1)

            def tail(t, s):
                after(pool, sq_done, t)
                pool.tensor_tensor(q4[:], q4s[:], k.half[:], ALU.pow).then_inc(q4_done, 1)
            skewed(pool, head, tail)
            pool.wait_ge(norm_sb, 1)
            pool.tensor_tensor(cr[:], cn[:], k.half[:].to_broadcast([P, KC]), ALU.pow).then_inc(root_done, 1)

        @block.vector
        def _(dve):
            ln = Chain(dve, ln_step, 2)
            mix = Chain(dve, mix_step, 6)

            def head(t, s, fill):
                def between():
                    fill(0)
                    after(dve, xT_ps, t - 1)
                ln.start(t)
                loaded(dve, x_in[s], t, s)
                layernorm_dve(dve, ln, xt[:, s, :], xn[:], st, mv, ve, rstd, var_ready, rstd_ready, xn_done, t, between)
                ln.end()

            def tail(t, s, fill):
                mix.start(t)
                after_dma(dve, stored_q, t - 1)
                after_dma(dve, stored_kv, t - 1)
                after_dma(dve, stored_m, t - 1, 2)
                after(dve, acc_done, t - 1)
                after(dve, proj_done, t)
                dve.tensor_tensor(allp[:], psP[:].rearrange("p a n -> p (a n)"), bcat[:], ALU.add).then_inc(evac_done, 1)
                after(dve, evac_done, t)
                mix(dve.tensor_reduce(mean[:], allp[:, 3 * C:5 * C].rearrange("p (a n) -> p a n", a=2), AX.X, ALU.add))
                dve.tensor_scalar(nmean[:], mean[:], -1.0 / C, None, ALU.mult).then_inc(mean_done, 1)
                fill(1)
                after(dve, sq_done, t)
                mix(dve.tensor_scalar(s2e[:], s2[:], 1e-7, None, ALU.add))
                mix(dve.reciprocal(r2[:], s2e[:]))
                dve.tensor_scalar(k2[:], sq[:, 1, :], r2[:, 1:2], k.valid[:, bass.ds(t, 1)], ALU.mult, ALU.mult)\
                    .then_inc(k2_done, 1)
                fill(2)
                after(dve, q4_done, t)
                mix(dve.tensor_scalar(qn[:], q4[:], r2[:, 0:1], 1e-12, ALU.mult, ALU.max))
                mix(dve.reciprocal(qr[:], qn[:]))
                mix(dve.tensor_scalar(qn[:], qr[:], r2[:, 0:1], None, ALU.mult))
                dve.tensor_scalar(q2[:], sq[:, 0, :], qn[:, 0:1], None, ALU.mult).then_inc(q2_done, 1)
                after(dve, k2_done, t)
                after(dve, q2_done, t)
                mix.end()
            lists.dve_start(dve)
            dve.wait_ge(w_in, 16 * 9)
            beside(dve, head, tail, lists.dve_step)
            lists.dve_end(dve)
            after(dve, acc_done, NT - 1)
            dve.tensor_copy(kvT[:], psK[:]).then_inc(kvT_sb, 1)
            dve.tensor_copy(cn[:], psN[:, 0:KC]).then_inc(norm_sb, 1)
            dve.wait_ge(kvw_ps, 1)
            dve.wait_ge(root_done, 1)
            dve.tensor_scalar(cn[:], cr[:], 1e-12, float(np.sqrt(N)), ALU.max, ALU.mult).then_inc(fin, 1)
            dve.wait_ge(fin, 1)
            dve.reciprocal(cr[:], cn[:]).then_inc(fin, 1)
            dve.wait_ge(fin, 2)
            for a in range(KC):
                dve.tensor_scalar(k.M1[:, a, :], psM[:, a, :], cr[:, a:a + 1], None, ALU.mult).then_inc(fin, 1)
            dve.wait_ge(fin, 4)

        @block.scalar
        def _(act):
            step = Chain(act, act_step, 2)

            def head(t, s):
                after(act, xT_ps, t)
                after(act, proj_done, t - 1)
                act.activation(xT[:], psT[:], ACT.Copy).then_inc(xT_sb, 1)

            def tail(t, s):
                step.start(t)
                after(act, mean_done, t)
                after(act, q2_done, t - 1)
                step(act.activation(sq[:, 0, :], allp[:, 3 * C:4 * C], ACT.Square, bias=nmean[:, 0:1], accum_out=s2[:, 0:1]))
                step(act.activation(sq[:, 1, :], allp[:, 4 * C:5 * C], ACT.Square, bias=nmean[:, 1:2], accum_out=s2[:, 1:2]))
                act.activation(junk[:], sq[:, 0, :], ACT.Square, accum_out=q4s[:, 0:1]).then_inc(sq_done, 1)
                after(act, k2_done, t)
                after(act, acc_done, t - 1)
                after(act, sq_done, t)
                act.activation(k4[:], k2[:], ACT.Square).then_inc(k4_done, 1)
                step.end()
            skewed(act, head, tail)

        @block.tensor
        def _(pe):
            pe.wait_ge(w_in, 16 * 9)

            def head(t, s, fill):
                after(pe, xn_done, t)
                after(pe, xT_sb, t - 1)
                for a in range(KC):
                    last = pe.transpose(psT[:, a, :], xn[:, a * P:(a + 1) * P], k.ident[:])
                last.then_inc(xT_ps, 1)
                after(pe, xT_sb, t)
                after(pe, evac_done, t - 1)
                for g in range(3):
                    for a in range(KC):
                        last = pe.matmul(psP[:, g, :], xT[:, a, :], wcat[:, a, g * 512:(g + 1) * 512],
                                         start=(a == 0), stop=(a == KC - 1))
                last.then_inc(proj_done, 1)

            def tail(t, s, fill):
                after(pe, k4_done, t)
                after(pe, k2_done, t)
                for a in range(KC):
                    pe.matmul(psK[:, a, :], allp[:, 5 * C + a * P:5 * C + (a + 1) * P], k2[:],
                              start=False, stop=False, skip_group_check=True)
                for a in range(KC):
                    last = pe.matmul(psN[:, a:a + 1], k4[:, a * P:(a + 1) * P], k.ones[:, 0:1],
                                     start=False, stop=False, skip_group_check=True)
                last.then_inc(acc_done, 1)
                for i in range(G):
                    fill(i)
            pe.matmul(psK[:].rearrange("p a n -> p (a n)"), k.zero1[:], bcat[0:1, 0:512], start=True, stop=True)
            pe.matmul(psN[:, 0:KC], k.zero1[:], bcat[0:1, 0:KC], start=True, stop=True)
            lists.pe_start(pe)
            beside(pe, head, tail, lists.pe_step)
            pe.wait_ge(kvT_sb, 1)
            for a in range(KC):
                for d in range(KC):
                    last = pe.matmul(psM[:, a, :], kvT[:, d, a * P:(a + 1) * P], wout[:, d, :],
                                     start=(d == 0), stop=(d == KC - 1))
            last.then_inc(kvw_ps, 1)


class MixOutput:

    def __init__(self, nc, k, w, c, sem):
        self.k, self.w = k, w
        sb = lambda name, shape, dt=F32: c.enter_context(nc.sbuf_tensor("a_" + name, shape, dt))
        self.wout = sb("wout", [P, KC, C])
        self.bias, self.bias2 = sb("bias", [P, C]), sb("bias2", [P, C])
        self.mvt, self.xt = sb("mvt", [P, 2 * C]), sb("xt", [P, C])
        self.mT = sb("mT", [P, 4, P])
        self.psT = c.enter_context(nc.psum_tensor("a_psT", [P, 4, P], F32))
        self.psO = c.enter_context(nc.psum_tensor("a_psO", [P, 512], F32))
        self.w_in, self.t_in, self.bias_done, self.stored = sem("a_w_in"), sem("a_t_in"), sem("a_bias_done"), sem("a_stored")
        self.ps_T, self.sb_T, self.ps_O = sem("a_ps_T"), sem("a_sb_T"), sem("a_ps_O")
        self.xb_done, self.out_done = sem("a_xb_done"), sem("a_out_done")

    def primed(self):
        return [self.ps_T, self.sb_T, self.ps_O, self.xb_done, self.out_done]

    def weights(self, sp):
        w = self.w
        sp.dma_start(self.wout[:], w["L0_mix_W_out"].rearrange("(a p) n -> p a n", p=P)).then_inc(self.w_in, 16)
        sp.dma_start(self.bias[:], w["L0_mix_b_out"].partition_broadcast(P)).then_inc(self.w_in, 16)
        sp.dma_start(self.bias2[:], w["L0_gnn_bo"].partition_broadcast(P)).then_inc(self.w_in, 16)

    def load(self, sp, t):
        after(sp, self.ps_T, t - 1)
        after_dma(sp, self.stored, t - 1)
        sp.dma_start(self.mvt[:], rows(self.k.MV, t)).then_inc(self.t_in, 16)
        sp.dma_start(self.xt[:], rows(self.k.XP, t)).then_inc(self.t_in, 16)

    def store(self, sp, t):
        after(sp, self.out_done, t)
        sp.dma_start(rows(self.k.X1M, t), self.xt[:]).then_inc(self.stored, 16)

    def dve_start(self, dve):
        dve.wait_ge(self.w_in, 48)
        dve.tensor_tensor(self.bias[:], self.bias[:], self.bias2[:], ALU.add).then_inc(self.bias_done, 1)
        dve.wait_ge(self.bias_done, 1)

    def dve_step(self, dve, t):
        loaded(dve, self.t_in, t, 0, per=2, slots=1)
        dve.tensor_tensor(self.xt[:], self.xt[:], self.bias[:], ALU.add).then_inc(self.xb_done, 1)
        after(dve, self.xb_done, t)
        after(dve, self.ps_O, t)
        dve.tensor_tensor(self.xt[:], self.xt[:], self.psO[:, 0:C], ALU.add).then_inc(self.out_done, 1)

    def act_step(self, act, t):
        after(act, self.ps_T, t)
        after(act, self.ps_O, t - 1)
        act.activation(self.mT[:], self.psT[:], ACT.Copy).then_inc(self.sb_T, 1)

    def pe_step(self, pe, t):
        loaded(pe, self.t_in, t, 0, per=2, slots=1)
        after(pe, self.sb_T, t - 1)
        for a in range(4):
            last = pe.transpose(self.psT[:, a, :], self.mvt[:, a * P:(a + 1) * P], self.k.ident[:])
        last.then_inc(self.ps_T, 1)
        after(pe, self.sb_T, t)
        after(pe, self.out_done, t - 1)
        for a in range(4):
            rhs = self.k.M1[:, a, :] if a < KC else self.wout[:, a - KC, :]
            last = pe.matmul(self.psO[:, 0:C], self.mT[:, a, :], rhs, start=(a == 0), stop=(a == 3))
        last.then_inc(self.ps_O, 1)


def rank_nodes(nc, k, cnt, nt, length, start, pos_i, inc_i, tag):
    with ExitStack() as c:
        sb = lambda name, shape, dt=F32: c.enter_context(nc.sbuf_tensor(name + tag, shape, dt))
        sem = semaphores(nc, c, after=tag)
        incl, tot, end, pos = sb("incl", [P, nt]), sb("tot", [P, nt]), sb("end", [P, nt]), sb("pos", [P, nt])
        lane, tmp, tmp2 = sb("lane", [P, nt]), sb("tmp", [P, nt]), sb("tmp2", [P, nt])
        starts = sb("starts", [P, P])
        onesr = sb("onesr", [P, nt])
        cmp = sb("cmp", [P, nt, P])
        psA = c.enter_context(nc.psum_tensor("psA" + tag, [P, 512], F32))
        psB = c.enter_context(nc.psum_tensor("psB" + tag, [P, 512], F32))
        summed, step = sem("summed"), sem("rank_step")
        block = c.enter_context(nc.Block())

        @block.tensor
        def _(pe):
            pe.matmul(psA[:, 0:nt], k.ones[:], cnt, start=True, stop=True)
            pe.matmul(psB[:, 0:nt], k.upper[:], cnt, start=True, stop=True).then_inc(summed, 1)

        @block.vector
        def _(dve):
            link = Chain(dve, step, None)
            link.start_once()
            link(dve.memset(onesr[:], 1.0))
            dve.wait_ge(summed, 1)
            link(dve.tensor_copy(tot[:], psA[:, 0:nt]))
            link(dve.tensor_tensor_scan(incl[:], onesr[:], tot[:], 0.0, ALU.mult, ALU.add))
            link(dve.tensor_tensor(tmp[:], incl[:], tot[:], ALU.subtract))
            link(dve.tensor_tensor(start, tmp[:], psB[:, 0:nt], ALU.add))
            link(dve.tensor_tensor(end[:], start, cnt, ALU.add))
            link(dve.tensor_scalar(pos[:], end[:], -1.0, 0.0, ALU.add, ALU.max))
            link(dve.tensor_copy(pos_i, pos[:]))
            link(dve.tensor_scalar(starts[:], k.iota[:], float(length), None, ALU.mult))
            link(dve.tensor_tensor(cmp[:], pos[:].unsqueeze(2).to_broadcast([P, nt, P]),
                                   starts[:].unsqueeze(1).to_broadcast([P, nt, P]), ALU.is_ge))
            link(dve.tensor_reduce(tmp[:], cmp[:], AX.X, ALU.add))
            link(dve.tensor_scalar(lane[:], tmp[:], -1.0, None, ALU.add))
            link(dve.tensor_scalar(tmp[:], lane[:], float(length), None, ALU.mult))
            link(dve.tensor_tensor(tmp2[:], start, tmp[:], ALU.is_lt))
            link(dve.tensor_scalar(tmp[:], lane[:], float(-P), None, ALU.add))
            link(dve.tensor_tensor(lane[:], tmp[:], tmp2[:], ALU.mult))
            link(dve.tensor_scalar(tmp[:], lane[:], float(P), None, ALU.add))
            link(dve.tensor_copy(inc_i, tmp[:]))


def edge_attention(nc, k, w):
    scale = float(DK) ** -0.5
    D1, S1 = DK + 1, BLK + 1
    with ExitStack() as c:
        sb = lambda name, shape, dt=F32: c.enter_context(nc.sbuf_tensor(name, shape, dt))
        sem = semaphores(nc, c)
        idx = sb("e_idx", [P, 2, 2, BLK], I32)
        q = sb("e_q", [P, 2, BLK, C])
        kv = sb("e_kv", [P, 2, BLK, 2 * C])
        S = sb("e_S", [P, HEADS, S1])
        bias = sb("e_bias", [P, HEADS, S1])
        bias1 = sb("e_bias1", [P, BLK])
        M = sb("e_M", [P, HEADS, S1])
        D = sb("e_D", [P, 2, HEADS, BLK])
        E = sb("e_E", [P, 2, HEADS, BLK])
        CX = sb("e_CX", [P, D1, HEADS, S1])
        PV = sb("e_PV", [P, D1, HEADS, S1])
        A = sb("e_A", [P, D1, HEADS, S1])
        O = sb("e_O", [P, BLK, (D1 + 1) * HEADS])
        idx_in = [sem("idx_in0"), sem("idx_in1")]
        q_in = [sem("q_in0"), sem("q_in1")]
        kv_in = [sem("kv_in0"), sem("kv_in1")]
        set_done, dve_step, d_done, pv_done, a_done, s_done = (sem("e_" + n) for n in (
            "set_done", "dve_step", "d_done", "pv_done", "a_done", "s_done"))
        exp_done, cx_done, o1_done, o_done, stored = (sem("e_" + n) for n in (
            "exp_done", "cx_done", "o1_done", "o_done", "stored"))
        mix = MixOutput(nc, k, w, c, sem)
        block = c.enter_context(nc.Block())
        pairs = NBA // 2

        def paired(eng, pair, n=pairs):
            with eng.Fori(0, NT) as j:
                pair(j, True)
            with eng.Fori(NT, n) as j:
                pair(j, False)

        src_l, dst_l = k.srci, k.dsti
        pt = k.PT.rearrange("(p i) f -> p i f", i=LA)

        @block.sync
        def _(sp):
            prime(sp, [d_done, pv_done, a_done, s_done, exp_done, cx_done, o_done] + mix.primed(),
                  [(stored, 1), (mix.stored, 1)])
            mix.weights(sp)

            def fetch(b, s):
                after(sp, pv_done, b - 2)
                sp.dma_start(idx[:, s, 0, :], src_l[:, bass.ds(b * BLK, BLK)]).then_inc(idx_in[s], 16)
                sp.dma_start(idx[:, s, 1, :], dst_l[:, bass.ds(b * BLK, BLK)]).then_inc(idx_in[s], 16)

            def store(b, s):
                after(sp, o_done, b)
                sp.dma_start(pt[:, bass.ds(b * BLK, BLK), :], O[:]).then_inc(stored, 16)

            def pair(j, tile):
                if tile:
                    mix.load(sp, j)
                for s in range(2):
                    fetch(2 * j + 2 + s, s)
                    store(2 * j + s, s)
                if tile:
                    mix.store(sp, j)
            fetch(0, 0)
            fetch(1, 1)
            paired(sp, pair, pairs - 1)
            store(NBA - 2, 0)
            store(NBA - 1, 1)
            after_dma(sp, stored, NBA - 1)
            after_dma(sp, mix.stored, NT - 1)

        @block.gpsimd
        def _(pool):
            def gather(b, s):
                loaded(pool, idx_in[s], b, s, per=2)
                after(pool, pv_done, b - 2)
                for j in range(BLK):
                    pool.indirect_dma_start(q[:, s, j, :], None, k.Q,
                                            bass.IndirectOffsetOnAxis(ap=idx[:, s, 1, j:j + 1], axis=0)).then_inc(q_in[s], 16)
                    pool.indirect_dma_start(kv[:, s, j, :], None, k.KV,
                                            bass.IndirectOffsetOnAxis(ap=idx[:, s, 0, j:j + 1], axis=0)).then_inc(kv_in[s], 16)
            ring(pool, gather, n=NBA)

        @block.vector
        def _(dve):
            dve.memset(bias[:], -BIG).then_inc(set_done, 1)
            dve.memset(M[:], -BIG).then_inc(set_done, 1)
            dve.memset(CX[:], 0.0).then_inc(set_done, 1)
            dve.memset(A[:], 0.0).then_inc(set_done, 1)
            dve.wait_ge(set_done, 4)
            step = Chain(dve, dve_step, 8)
            mix.dve_start(dve)

            def body(b, s):
                step.start(b)
                loaded(dve, q_in[s], b, s, per=BLK)
                loaded(dve, kv_in[s], b, s, per=BLK)
                qs = q[:, s]
                step(dve.tensor_tensor(qs, qs, kv[:, s, :, 0:C], ALU.mult))
                dve.tensor_copy(S[:, :, 0:1], M[:, :, BLK:S1])
                step(dve.tensor_scalar(bias1[:], k.same[:, bass.ds(b * BLK, BLK)], -1.0, BIG, ALU.add, ALU.mult))
                step(dve.tensor_copy(bias[:, :, 1:S1], bias1[:].unsqueeze(1).to_broadcast([P, HEADS, BLK])))
                step(dve.tensor_reduce(S[:, :, 1:S1], qs.rearrange("p j (d h) -> p h j d", h=HEADS), AX.X, ALU.add))
                after(dve, o_done, b - 1)
                step(dve.tensor_tensor_scan(M[:].rearrange("p h j -> p (h j)"), bias[:].rearrange("p h j -> p (h j)"),
                                            S[:].rearrange("p h j -> p (h j)"), -BIG, ALU.add, ALU.max))
                dve.tensor_tensor(D[:, 0], S[:, :, 1:S1], M[:, :, 1:S1], ALU.subtract)
                step(dve.tensor_tensor(D[:, 1], M[:, :, 0:BLK], M[:, :, 1:S1], ALU.subtract))
                dve.tensor_tensor(D[:, 1], D[:, 1], bias[:, :, 1:S1], ALU.add).then_inc(d_done, 1)
                step(dve.tensor_copy(PV[:, :, :, 0], A[:, :, :, BLK]))
                after(dve, exp_done, b)
                step(dve.tensor_copy(PV[:, DK, :, 1:S1], E[:, 0]))
                dve.tensor_tensor(PV[:, 0:DK, :, 1:S1], kv[:, s, :, C:2 * C].rearrange("p j (d h) -> p d h j", h=HEADS),
                                  E[:, 0].unsqueeze(1).to_broadcast([P, DK, HEADS, BLK]), ALU.mult).then_inc(pv_done, 1)
                after(dve, pv_done, b)
                after(dve, cx_done, b)
                dve.tensor_tensor_scan(A[:].rearrange("p d h j -> p (d h j)"), CX[:].rearrange("p d h j -> p (d h j)"),
                                       PV[:].rearrange("p d h j -> p (d h j)"), 0.0, ALU.mult, ALU.add).then_inc(a_done, 1)
                after(dve, a_done, b)
                step.end()

            def pair(j, tile):
                body(2 * j, 0)
                body(2 * j + 1, 1)
                if tile:
                    mix.dve_step(dve, j)
            paired(dve, pair)

        @block.scalar
        def _(act):
            act.wait_ge(set_done, 4)

            def body(b, s):
                after(act, d_done, b)
                act.activation(E[:], D[:], ACT.Exp, scale=scale).then_inc(exp_done, 1)
                after(act, exp_done, b)
                act.activation(CX[:, :, :, 1:S1], E[:, 1].unsqueeze(1).to_broadcast([P, D1, HEADS, BLK]), ACT.Copy)\
                    .then_inc(cx_done, 1)
                after(act, a_done, b)
                after_dma(act, stored, b - 1)
                act.activation(O[:, :, 0:D1 * HEADS], A[:, :, :, 1:S1].rearrange("p d h j -> p j (d h)"), ACT.Copy)\
                    .then_inc(o1_done, 1)
                act.activation(O[:, :, D1 * HEADS:], M[:, :, 1:S1].rearrange("p h j -> p j h"), ACT.Copy).then_inc(o_done, 1)

            def pair(j, tile):
                body(2 * j, 0)
                if tile:
                    mix.act_step(act, j)
                body(2 * j + 1, 1)
            paired(act, pair)

        @block.tensor
        def _(pe):
            pe.wait_ge(mix.w_in, 48)
            with pe.Fori(0, NT) as j:
                mix.pe_step(pe, j)


def join_lanes(nc, k, table, length, last_node, first_node, H, D1, scale, incoming, tag):
    W = (D1 + 1) * H if H else D1
    with ExitStack() as c:
        sb = lambda name, shape, dt=F32: c.enter_context(nc.sbuf_tensor(name + tag, shape, dt))
        sem = semaphores(nc, c, after=tag)
        ends, inc, none = sb("j_ends", [P, W]), sb("j_inc", [P, W]), sb("j_none", [1, W])
        diag, mask, mbias = sb("j_diag", [P, P]), sb("j_mask", [P, P]), sb("j_mbias", [P, P])
        X, Wt = sb("j_X", [P, P]), sb("j_Wt", [P, P])
        mx = sb("j_mx", [P, 1])
        ps = c.enter_context(nc.psum_tensor("j_ps" + tag, [P, 512], F32))
        psW = c.enter_context(nc.psum_tensor("j_psW" + tag, [P, 512], F32))
        psV = c.enter_context(nc.psum_tensor("j_psV" + tag, [P, 512], F32))
        ends_in, step, exp_done, spread, turned, joined, stored, pool_set = (sem("j_" + n) for n in (
            "ends_in", "step", "exp_done", "spread", "turned", "joined", "stored", "pool_set"))
        diag_done, wt_done, x_done, wm_done, inc_done = (sem("j_" + n) for n in ("diag_done", "wt_done", "x_done", "wm_done", "inc_done"))
        block = c.enter_context(nc.Block())
        heads = max(H, 1)

        @block.sync
        def _(sp):
            sp.dma_start(ends[:], table.rearrange("(p i) f -> p i f", i=length)[:, length - 1, :]).then_inc(ends_in, 16)
            sp.wait_ge(pool_set, 2 if H else 1)
            sp.dma_start(incoming[P:P + 1, :], none[:]).then_inc(stored, 16)
            sp.wait_ge(inc_done, heads)
            sp.dma_start(incoming[0:P, :], inc[:]).then_inc(stored, 16)
            sp.wait_ge(stored, 32)

        @block.gpsimd
        def _(pool):
            pool.memset(none[:], 0.0).then_inc(pool_set, 1)
            if H:
                pool.wait_ge(pool_set, 1)
                pool.memset(none[:, D1 * H:], -BIG).then_inc(pool_set, 1)

        @block.vector
        def _(dve):
            link = Chain(dve, step, None)
            link.start_once()
            dve.tensor_scalar(diag[:], k.ident[:], last_node, None, ALU.mult).then_inc(diag_done, 1)
            dve.wait_ge(spread, 1)
            link(dve.scalar_tensor_tensor(out=mask[:], in0=ps[:, 0:P], scalar=first_node, in1=k.low[:],
                                          op0=ALU.is_equal, op1=ALU.mult))
            link(dve.tensor_scalar(mbias[:], mask[:], -1.0, BIG, ALU.add, ALU.mult))
            dve.wait_ge(ends_in, 16)
            for h in range(heads):
                if H:
                    m = D1 * H + h
                    dve.tensor_scalar(diag[:], k.ident[:], ends[:, m:m + 1], None, ALU.mult).then_inc(diag_done, 1)
                    dve.wait_ge(spread, h + 2)
                    link(dve.tensor_tensor(X[:], ps[:, 0:P], mbias[:], ALU.add))
                    link(dve.tensor_reduce(mx[:], X[:], AX.X, ALU.max))
                    link(dve.tensor_copy(inc[:, m:m + 1], mx[:]))
                    dve.tensor_scalar(X[:], X[:], mx[:, 0:1], None, ALU.subtract).then_inc(x_done, 1)
                    dve.wait_ge(exp_done, h + 1)
                    dve.tensor_tensor(X[:], X[:], mask[:], ALU.mult).then_inc(wm_done, 1)
                else:
                    dve.tensor_copy(X[:], mask[:]).then_inc(wm_done, 1)
                dve.wait_ge(turned, h + 1)
                dve.tensor_copy(Wt[:], psW[:, 0:P]).then_inc(wt_done, 1)
                dve.wait_ge(joined, h + 1)
                if H:
                    dve.tensor_copy(inc[:, 0:D1 * H].rearrange("p (d h) -> p d h", h=H)[:, :, h], psV[:, 0:D1]).then_inc(inc_done, 1)
                else:
                    dve.tensor_copy(inc[:], psV[:, 0:D1]).then_inc(inc_done, 1)

        @block.scalar
        def _(act):
            if H:
                for h in range(H):
                    act.wait_ge(x_done, h + 1)
                    act.activation(X[:], X[:], ACT.Exp, scale=scale).then_inc(exp_done, 1)

        @block.tensor
        def _(pe):
            pe.wait_ge(diag_done, 1)
            pe.matmul(ps[:, 0:P], k.ones[:], diag[:], start=True, stop=True).then_inc(spread, 1)
            for h in range(heads):
                if H:
                    pe.wait_ge(diag_done, h + 2)
                    pe.matmul(ps[:, 0:P], k.ones[:], diag[:], start=True, stop=True).then_inc(spread, 1)
                pe.wait_ge(wm_done, h + 1)
                pe.transpose(psW[:, 0:P], X[:], k.ident[:]).then_inc(turned, 1)
                pe.wait_ge(wt_done, h + 1)
                if h == 0:
                    pe.wait_ge(ends_in, 16)
                rhs = ends[:, 0:D1 * H].rearrange("p (d h) -> p d h", h=H)[:, :, h] if H else ends[:]
                pe.matmul(psV[:, 0:D1], Wt[:], rhs, start=True, stop=True).then_inc(joined, 1)


EG = 131072
TG = EG // P
HG = 64
LG = EG // P + HG
HE = 4
SB = 8


class GatCount:

    HB = 16
    blocks = TG // HB

    def __init__(self, nc, k, w, c, sem):
        self.k, self.w = k, w
        sb = lambda name, shape, dt=F32: c.enter_context(nc.sbuf_tensor("c_" + name, shape, dt))
        self.nat_i, self.nat = sb("nat_i", [P, 2, TG], I32), sb("nat", [P, 2, TG])
        self.tmp_i = sb("tmp_i", [P, TG], I32)
        self.oh_lo, self.oh_hi = sb("oh_lo", [P, 2, self.HB, P], BF16), sb("oh_hi", [P, 2, self.HB, HG], BF16)
        self.psT = [c.enter_context(nc.psum_tensor(f"c_psT{i}", [P, TG], F32)) for i in range(2)]
        self.psC = c.enter_context(nc.psum_tensor("c_psC", [P, HG], F32))
        self.nat_in, self.setup, self.nat_done, self.turned = (
            sem(n) for n in ("c_nat_in", "c_setup", "c_nat_done", "c_turned"))
        self.onehots, self.counted = sem("c_onehots"), sem("c_counted")

    def primed(self):
        return [self.onehots, self.counted]

    def load(self, sp):
        for i in range(2):
            sp.dma_start(self.nat_i[:, i, :].rearrange("i (b p) -> i b p", p=P),
                         self.w["L1_ffn_edge_index"][i].rearrange("(b i p) -> i b p", i=P, p=P)).then_inc(self.nat_in, 16)

    def pe_start(self, pe):
        k, psT, nat = self.k, self.psT, self.nat
        pe.wait_ge(self.nat_done, 2)
        for i in range(2):
            for b in range(TG // P):
                last = pe.transpose(psT[i][:, b * P:(b + 1) * P], nat[:, i, b * P:(b + 1) * P], k.ident[:])
        last.then_inc(self.turned, 1)
        pe.matmul(self.psC[:], k.zero1[:], k.ones[0:1, 0:HG], start=True, stop=True)

    def pe_step(self, pe, b, s):
        after(pe, self.onehots, b)
        for j in range(self.HB):
            last = pe.matmul(self.psC[:], self.oh_lo[:, s, j, :], self.oh_hi[:, s, j, :], start=False, stop=False,
                             skip_group_check=True)
        last.then_inc(self.counted, 1)

    def dve_start(self, dve):
        k, nat, nat_i, tmp_i = self.k, self.nat, self.nat_i, self.tmp_i
        link = self.link = Chain(dve, self.setup, None)
        link.start_once()
        dve.wait_ge(self.nat_in, 32)
        dve.tensor_scalar(nat[:, 0, :], nat_i[:, 0, :], float(N - 1), None, ALU.min).then_inc(self.nat_done, 1)
        dve.tensor_copy(nat[:, 1, :], nat_i[:, 1, :]).then_inc(self.nat_done, 1)
        dve.wait_ge(self.turned, 1)
        for i in range(2):
            link(dve.tensor_copy(k.pair[:, :, i], self.psT[i][:]))
        link(dve.tensor_scalar(tmp_i[:], k.pair[:, :, 1], P - 1, None, ALU.bitwise_and))
        link(dve.tensor_copy(k.lo[:], tmp_i[:]))
        link(dve.tensor_scalar(tmp_i[:], k.pair[:, :, 1], 7, None, ALU.logical_shift_right))
        link(dve.tensor_copy(k.hi[:], tmp_i[:]))
        link(dve.tensor_copy(k.dcol[:], k.pair[:, :, 1]))

    def dve_step(self, dve, b, s):
        k, HB = self.k, self.HB
        after(dve, self.counted, b - 2)
        dve.tensor_tensor(self.oh_lo[:, s], k.iota[:].unsqueeze(1).to_broadcast([P, HB, P]),
                          k.lo[:, bass.ds(b * HB, HB)].unsqueeze(2).to_broadcast([P, HB, P]), ALU.is_equal)
        dve.tensor_tensor(self.oh_hi[:, s], k.iota[:, 0:HG].unsqueeze(1).to_broadcast([P, HB, HG]),
                          k.hi[:, bass.ds(b * HB, HB)].unsqueeze(2).to_broadcast([P, HB, HG]), ALU.is_equal)\
            .then_inc(self.onehots, 1)

    def dve_end(self, dve):
        after(dve, self.counted, self.blocks - 1)
        self.link(dve.tensor_scalar(self.k.cnt2[:], self.psC[:], 1.0, None, ALU.add))


def attention_output(nc, k, w):
    scale = float(DK) ** -0.5
    D1 = DK + 1
    W = (D1 + 1) * HEADS
    with ExitStack() as c:
        sb = lambda name, shape, dt=F32: c.enter_context(nc.sbuf_tensor(name, shape, dt))
        sem = semaphores(nc, c)
        wo = sb("b_wo", [P, KC, C])
        idx = sb("b_idx", [P, 2, 2], I32)
        r = sb("b_r", [P, 2, 2, W])
        xm = sb("b_xm", [P, 2, C])
        Mx = sb("b_Mx", [P, HEADS])
        D = sb("b_D", [P, 2, HEADS])
        E = sb("b_E", [P, 2, HEADS])
        T = sb("b_T", [P, 2, D1, HEADS])
        U = sb("b_U", [P, D1, HEADS])
        rz = sb("b_rz", [P, HEADS])
        att = sb("b_att", [P, C])
        aT = sb("b_aT", [P, KC, P])
        xo = sb("b_xo", [P, C])
        psT = c.enter_context(nc.psum_tensor("b_psT", [P, KC, P], F32))
        psO = c.enter_context(nc.psum_tensor("b_psO", [P, 512], F32))
        w_in = sem("b_w_in")
        x_in = [sem("b_x_in0"), sem("b_x_in1")]
        r_in = [sem("b_r_in0"), sem("b_r_in1")]
        idx_done, step, d_done, e_done, att_done, ps_T, sb_T, ps_O, out_done, stored = (
            sem("b_" + n) for n in ("idx_done", "step", "d_done", "e_done", "att_done", "ps_T", "sb_T", "ps_O",
                                    "out_done", "stored"))
        count = GatCount(nc, k, w, c, sem)
        assert count.blocks >= NT
        block = c.enter_context(nc.Block())

        @block.sync
        def _(sp):
            prime(sp, [idx_done, d_done, e_done, att_done, ps_T, sb_T, ps_O, out_done] + count.primed(),
                  [(stored, 1)])
            count.load(sp)
            sp.dma_start(wo[:], w["L0_gnn_Wo"].rearrange("(a p) n -> p a n", p=P)).then_inc(w_in, 16)

            def load(t, s):
                after(sp, out_done, t - 2)
                sp.dma_start(xm[:, s, :], rows(k.X1M, t)).then_inc(x_in[s], 16)

            def store(t, s):
                after(sp, out_done, t)
                sp.dma_start(rows(k.X1, t), xo[:]).then_inc(stored, 16)
            two_ahead(sp, load, store)
            after_dma(sp, stored, NT - 1)

        @block.gpsimd
        def _(pool):
            def gather(t, s):
                after(pool, idx_done, t)
                after(pool, att_done, t - 2)
                for g, (tab, width) in enumerate(((k.PT, W), (k.INC, W))):
                    pool.indirect_dma_start(r[:, s, g, :], None, tab,
                                            bass.IndirectOffsetOnAxis(ap=idx[:, s, g:g + 1], axis=0)).then_inc(r_in[s], 16)
            ring(pool, gather)

        @block.vector
        def _(dve):
            ch = Chain(dve, step, 5)

            def index(t, s):
                if not isinstance(t, int) or t >= 2:
                    loaded(dve, r_in[s], t - 2, s, per=2)
                dve.tensor_copy(idx[:, s, 0:1], k.pos_i[:, bass.ds(t, 1)])
                dve.tensor_copy(idx[:, s, 1:2], k.inc_i[:, bass.ds(t, 1)]).then_inc(idx_done, 1)

            def body(t, s):
                ch.start(t)
                loaded(dve, r_in[s], t, s, per=2)
                m = r[:, s, :, D1 * HEADS:]
                ch(dve.tensor_tensor(Mx[:], m[:, 0], m[:, 1], ALU.max))
                dve.tensor_tensor(D[:], m, Mx[:].unsqueeze(1).to_broadcast([P, 2, HEADS]), ALU.subtract).then_inc(d_done, 1)
                after(dve, e_done, t)
                v = r[:, s, :, 0:D1 * HEADS].rearrange("p g (d h) -> p g d h", h=HEADS)
                for g in range(2):
                    ins = dve.tensor_tensor(T[:, g], v[:, g], E[:, g].unsqueeze(1).to_broadcast([P, D1, HEADS]), ALU.mult)
                    ch(ins)
                ch(dve.tensor_tensor(U[:], T[:, 0], T[:, 1], ALU.add))
                ch(dve.reciprocal(rz[:], U[:, DK, :]))
                after(dve, ps_T, t - 1)
                dve.tensor_tensor(att[:].rearrange("p (d h) -> p d h", h=HEADS), U[:, 0:DK],
                                  rz[:].unsqueeze(1).to_broadcast([P, DK, HEADS]), ALU.mult).then_inc(att_done, 1)
                count.dve_step(dve, t, s)
                after(dve, ps_O, t)
                loaded(dve, x_in[s], t, s)
                after_dma(dve, stored, t - 1)
                dve.tensor_tensor(xo[:], xm[:, s, :], psO[:, 0:C], ALU.add).then_inc(out_done, 1)
                ch.end()
            index(0, 0)
            index(1, 1)
            count.dve_start(dve)
            body(0, 0)
            index(2, 0)
            body(1, 1)
            index(3, 1)
            with dve.Fori(1, NT // 2 - 1) as j:
                body(2 * j, 0)
                index(2 * j + 2, 0)
                body(2 * j + 1, 1)
                index(2 * j + 3, 1)
            body(NT - 2, 0)
            body(NT - 1, 1)
            for b in range(NT, count.blocks):
                count.dve_step(dve, b, b % 2)
            count.dve_end(dve)

        @block.scalar
        def _(act):
            def body(t, s):
                after(act, d_done, t)
                act.activation(E[:], D[:], ACT.Exp, scale=scale).then_inc(e_done, 1)
                after(act, ps_T, t)
                after(act, ps_O, t - 1)
                act.activation(aT[:], psT[:], ACT.Copy).then_inc(sb_T, 1)
            ring(act, body)

        @block.tensor
        def _(pe):
            pe.wait_ge(w_in, 16)

            def body(t, s):
                after(pe, att_done, t)
                after(pe, sb_T, t - 1)
                for a in range(KC):
                    last = pe.transpose(psT[:, a, :], att[:, a * P:(a + 1) * P], k.ident[:])
                last.then_inc(ps_T, 1)
                after(pe, sb_T, t)
                after(pe, out_done, t - 1)
                for a in range(KC):
                    last = pe.matmul(psO[:, 0:C], aT[:, a, :], wo[:, a, :], start=(a == 0), stop=(a == KC - 1))
                last.then_inc(ps_O, 1)
                count.pe_step(pe, t, s)
            count.pe_start(pe)
            ring(pe, body)
            for b in range(NT, count.blocks):
                count.pe_step(pe, b, b % 2)


class GatSort:

    blocks = TG // SB

    def __init__(self, nc, k, w, c, sem, psC, psR):
        self.k, self.w, self.psC, self.psR = k, w, psC, psR
        sb = lambda name, shape, dt=F32: c.enter_context(nc.sbuf_tensor("o_" + name, shape, dt))
        self.db = sb("db", [P, 2, SB * P], I32)
        self.dlo, self.dbf = sb("dlo", [P, SB * P], I32), sb("dbf", [P, 2, SB * P])
        self.ahead = sb("ahead", [P, SB * P], BF16)
        self.oht = sb("oht", [P, 2, SB, P])
        self.oh_lo, self.oh_hi = sb("oh_lo", [P, 2, SB, P], BF16), sb("oh_hi", [P, 2, SB, HG], BF16)
        self.dc = sb("dc", [P, SB])
        self.rank, self.prior = sb("rank", [P, 2, SB]), sb("prior", [P, SB])
        self.eq, self.sel = sb("eq", [P, SB - 1, SB * P // 2], BF16), sb("sel", [P, SB, HG])
        self.base = sb("base", [P, HG])
        self.loops = sb("loops", [P, HG, 2], I32)
        self.nodes_i, self.nodes_f = sb("nodes_i", [P, HG], I32), sb("nodes_f", [P, HG])
        self.C_sb = sb("C_sb", [P, HG])
        self.pos, self.pay = sb("pos", [P, 2, SB], I32), sb("pay", [P, 2, SB, 2], I32)
        self.blank = sb("blank", [P, 2, 2], I32)
        self.db_in = [sem("db_in0"), sem("db_in1")]
        self.scattered = [sem("scattered0"), sem("scattered1")]
        self.setup, self.iota_done, self.loops_done, self.placed = (
            sem(n) for n in ("setup", "iota_done", "loops_done", "placed"))
        self.base_done, self.init_done = sem("base_done"), sem("init_done")
        self.dbf_done, self.hots_done, self.r_done = sem("dbf_done"), sem("hots_done"), sem("r_done")
        self.counted, self.c_sb = sem("counted"), sem("c_sb")
        self.rank_step, self.rank_done = sem("rank_step"), sem("rank_done")
        self.sel_step, self.sel_done, self.pos_done = sem("sel_step"), sem("sel_done"), sem("pos_done")

    def primed(self):
        return [self.hots_done, self.rank_done, self.sel_done, self.pos_done, self.dbf_done, self.counted, self.c_sb,
                self.r_done]

    def pool_start(self, pool):
        k = self.k
        pool.iota(self.nodes_i[:], [[P, HG]], 0, 1).then_inc(self.iota_done, 1)
        pool.memset(self.blank[:], 0).then_inc(self.iota_done, 1)
        pool.wait_ge(self.iota_done, 2)
        for s in range(2):
            pool.dma_start(self.blank[:, s, 1:2], self.blank[:, s, 0:1]).then_inc(self.scattered[s], 16 * SB)
        pool.wait_ge(self.loops_done, 1)
        for t in range(HG):
            pool.indirect_dma_start(k.SD, bass.IndirectOffsetOnAxis(ap=k.start2_i[:, t:t + 1], axis=0),
                                    self.loops[:, t, :], None).then_inc(self.placed, 16)
        pool.wait_ge(self.placed, 16 * HG)

    def pool_step(self, pool, b, s):
        after(pool, self.pos_done, b)
        for j in range(SB):
            pool.indirect_dma_start(self.k.SD, bass.IndirectOffsetOnAxis(ap=self.pos[:, s, j:j + 1], axis=0),
                                    self.pay[:, s, j, :], None).then_inc(self.scattered[s], 16)

    def pool_end(self, pool):
        for s in range(2):
            pool.wait_ge(self.scattered[s], 16 * SB * (self.blocks // 2 + 1))

    def dve_start(self, dve):
        k = self.k
        link = Chain(dve, self.setup, None)
        link.start_once()
        dve.tensor_scalar(self.base[:], k.start2[:], 1.0, None, ALU.add).then_inc(self.base_done, 1)
        dve.wait_ge(self.iota_done, 2)
        link(dve.tensor_copy(self.loops[:, :, 1], self.nodes_i[:]))
        link(dve.tensor_scalar(self.nodes_f[:], self.nodes_i[:], float(N - 1), None, ALU.min))
        link(dve.tensor_copy(k.start2_i[:], k.start2[:]))
        dve.tensor_copy(self.loops[:, :, 0], self.nodes_f[:]).then_inc(self.loops_done, 1)
        link(dve.memset(self.ahead[:, 0:(SB - 1) * P], 1.0))
        link(dve.tensor_copy(self.ahead[:, (SB - 1) * P:], k.low[:]))
        self.rk = Chain(dve, self.rank_step, 3)
        self.sl = Chain(dve, self.sel_step, 3)
        self.prepare(dve, 0, 0)

    def prepare(self, dve, b, s):
        k, rk = self.k, self.rk
        rk.start(b)
        loaded(dve, self.db_in[s], b, s)
        after(dve, self.rank_done, b - 1)
        rk(dve.tensor_copy(self.dc[:], k.dcol[:, bass.ds(b * SB, SB)]))
        rk(dve.tensor_scalar(self.dlo[:], self.db[:, s, :], P - 1, None, ALU.bitwise_and))
        after(dve, self.sel_done, b - 2)
        after(dve, self.counted, b - 2)
        dve.tensor_scalar(self.oht[:, s].rearrange("p j e -> p (j e)"), self.dlo[:], k.part[:, 0:1], None, ALU.is_equal)
        dve.tensor_tensor(self.oh_lo[:, s], k.iota[:].unsqueeze(1).to_broadcast([P, SB, P]),
                          k.lo[:, bass.ds(b * SB, SB)].unsqueeze(2).to_broadcast([P, SB, P]), ALU.is_equal)
        dve.tensor_tensor(self.oh_hi[:, s], k.iota[:, 0:HG].unsqueeze(1).to_broadcast([P, SB, HG]),
                          k.hi[:, bass.ds(b * SB, SB)].unsqueeze(2).to_broadcast([P, SB, HG]), ALU.is_equal)\
            .then_inc(self.hots_done, 1)
        after(dve, self.dbf_done, b)
        for j in range(SB):
            n = (j + 1) * P
            last = dve.scalar_tensor_tensor(out=self.scrap(j), in0=self.dbf[:, s, 0:n], scalar=self.dc[:, j:j + 1],
                                            in1=self.ahead[:, SB * P - n:], op0=ALU.is_equal, op1=ALU.mult,
                                            accum_out=self.rank[:, s, j:j + 1])
            if j == SB - 2:
                rk(last)
        last.then_inc(self.rank_done, 1)
        rk.end()

    def scrap(self, j):
        n = (j + 1) * P
        flat = self.eq[:].rearrange("p j n -> p (j n)")
        o = P * sum(i + 1 for i in range(j)) if j < SB - 1 else 0
        return flat[:, o:o + n]

    def dve_step(self, dve, b, s):
        k, sl = self.k, self.sl
        if not isinstance(b, int) or b + 1 < self.blocks:
            self.prepare(dve, b + 1, 1 - s)
        sl.start(b)
        after(dve, self.r_done, b)
        sl(dve.tensor_tensor(self.sel[:], self.oh_hi[:, s], self.psR, ALU.mult))
        sl(dve.tensor_reduce(self.prior[:], self.sel[:], AX.X, ALU.add))
        after(dve, self.rank_done, b)
        dve.sem_inc(self.sel_done, 1)
        wait_reg(dve, self.scattered[s], (b - s) * (8 * SB) + 16 * SB)
        dve.tensor_copy(self.pay[:, s], k.pair[:, bass.ds(b * SB, SB), :])
        sl(dve.tensor_tensor(self.pos[:, s, :], self.prior[:], self.rank[:, s, :], ALU.add))
        dve.sem_inc(self.pos_done, 1)
        sl.end()

    def fetch(self, act, b, s):
        after(act, self.hots_done, b - 2)
        after(act, self.dbf_done, b - 2)
        act.dma_start(self.db[:, s, :],
                      self.w["L1_ffn_edge_index"][1, bass.ds(b * SB * P, SB * P)].partition_broadcast(P))\
            .then_inc(self.db_in[s], 16)

    def convert(self, act, b, s):
        loaded(act, self.db_in[s], b, s)
        after(act, self.rank_done, b - 2)
        act.activation(self.dbf[:, s, :], self.db[:, s, :], ACT.Copy).then_inc(self.dbf_done, 1)

    def act_start(self, act):
        self.fetch(act, 0, 0)
        self.fetch(act, 1, 1)
        self.convert(act, 0, 0)
        act.wait_ge(self.init_done, 1)

    def act_step(self, act, b, s):
        after(act, self.counted, b - 1)
        act.activation(self.C_sb[:], self.psC, ACT.Copy).then_inc(self.c_sb, 1)
        if not isinstance(b, int) or b + 1 < self.blocks:
            self.convert(act, b + 1, 1 - s)
        if not isinstance(b, int) or b + 2 < self.blocks:
            self.fetch(act, b + 2, s)

    def pe_start(self, pe):
        pe.wait_ge(self.base_done, 1)
        pe.matmul(self.psC, self.k.ident[:], self.base[:], start=True, stop=True).then_inc(self.init_done, 1)

    def pe_step(self, pe, b, s):
        after(pe, self.hots_done, b)
        after(pe, self.c_sb, b)
        after(pe, self.sel_done, b - 1)
        for j in range(SB):
            last = pe.matmul(self.psR[:, j, :], self.oht[:, s, j, :], self.C_sb[:], start=True, stop=True)
        last.then_inc(self.r_done, 1)
        pe.matmul(self.psC, self.k.ident[:], self.C_sb[:], start=True, stop=False, skip_group_check=True)
        for j in range(SB):
            last = pe.matmul(self.psC, self.oh_lo[:, s, j, :], self.oh_hi[:, s, j, :], start=False, stop=j == SB - 1,
                             skip_group_check=True)
        last.then_inc(self.counted, 1)



GT = 5
NG = NT // GT
GW = GT * P
HALF = GW // 2


def after_step(eng, sem, g, per, i):
    wait_reg(eng, sem, g * per + i + 1 + PRIME)


def routed_ffn(nc, k, w, second, x_in_dram, x_out_dram):
    EX = 4 if second else 8
    MH = 16 if second else 8
    PH = EX // 2
    tag = "_f1" if second else "_f0"
    with ExitStack() as c:
        sb = lambda name, shape, dt=F32: c.enter_context(nc.sbuf_tensor(name + tag, shape, dt))
        sem = semaphores(nc, c, after=tag)
        w1 = sb("w1", [P, KC, MH * P])
        b1 = sb("b1", [P, MH])
        w2 = sb("w2", [P, MH, C] if second else [P, MH, EX, C])
        b2 = sb("b2", [P, EX, C])
        xg = sb("xg", [P, 2, GT, C])
        xn = sb("xn", [P, GT, C])
        xT = sb("xT", [P, KC, GW])
        H = sb("H", [P, MH, GW])
        st, mv = sb("st", [P, GT, 6]), sb("mv", [P, GT, 2])
        ve, rstd = sb("ve", [P, GT]), sb("rstd", [P, GT])
        gate = sb("gate", [P, 2, GT, EX])
        if not second:
            wg, bg = sb("wg", [P, MH, EX]), sb("bg", [P, EX])
            L, X8, oh, cand = (sb(n, [P, GT, EX]) for n in ("L", "X8", "oh", "cand"))
            mx, sm, pr, mn = (sb(n, [P, GT]) for n in ("mx", "sm", "pr", "mn"))
            im = sb("im", [P, EX])
        psT = c.enter_context(nc.psum_tensor("psT" + tag, [P, 2, KC, P], F32))
        psH = c.enter_context(nc.psum_tensor("psH" + tag, [P, 2, 512], F32))
        psL = psH[:, 1, HALF:HALF + GT * EX].rearrange("p (i e) -> p i e", e=EX)
        psY = c.enter_context(nc.psum_tensor("psY" + tag, [P, 2, 2, 512], F32))
        w_in, x_in = sem("w_in"), [sem("x_in0"), sem("x_in1")]
        var_ready, rstd_ready, xn_done, ln_step = sem("var_ready"), sem("rstd_ready"), sem("xn_done"), sem("ln_step")
        tp_done, tc_done, hp_done, h_done = sem("tp_done"), sem("tc_done"), sem("hp_done"), sem("h_done")
        lg_done, lx_done, le_done, gate_done, rt_step = (sem(n) for n in ("lg_done", "lx_done", "le_done", "gate_done", "rt_step"))
        y_done, yc_done, x_done, y_step, stored = (sem(n) for n in ("y_done", "yc_done", "x_done", "y_step", "stored"))
        im_done = sem("im_done")
        sort = None
        if not second:
            psR = c.enter_context(nc.psum_tensor("psR" + tag, [P, SB, HG], F32))
            sort = GatSort(nc, k, w, c, sem, psH[:, 0, HALF:HALF + HG], psR[:])
        block = c.enter_context(nc.Block())
        rounds = [(0, 2), (2, 2), (4, 1)]
        TR, HS, YS = len(rounds), 2 * MH, 2 * GT

        def group(ap, g):
            return ap[bass.ds(g * GW, GW), :].rearrange("(i p) c -> p i c", p=P)

        @block.sync
        def _(sp):
            prime(sp, [var_ready, rstd_ready, xn_done, tp_done, tc_done, hp_done, h_done, lg_done, lx_done, le_done,
                       gate_done, y_done, yc_done, x_done] + (sort.primed() if sort else []), [(stored, GT)])
            if second:
                for e in range(EX):
                    sp.dma_start(w1[:, :, e * 2 * C:(e + 1) * 2 * C],
                                 w["L1_ffn_W1"][e].rearrange("(a p) n -> p a n", p=P)).then_inc(w_in, 16)
                    sp.dma_start(w2[:, e * 4:(e + 1) * 4, :],
                                 w["L1_ffn_W2"][e].rearrange("(m p) n -> p m n", p=P)).then_inc(w_in, 16)
                    sp.dma_start(b2[:, e, :], w["L1_ffn_b2"][e].partition_broadcast(P)).then_inc(w_in, 16)
                    sp.dma_start(b1[:, e * 4:(e + 1) * 4], w["L1_ffn_b1"][e].rearrange("(m p) -> p m", p=P),
                                 allow_slow_non_contiguous=True).then_inc(w_in, 16)
            else:
                sp.dma_start(w1[:], w["L0_ffn_W1"].rearrange("(a p) n -> p a n", p=P)).then_inc(w_in, 16)
                sp.dma_start(b1[:], w["L0_ffn_b1"].rearrange("(m p) -> p m", p=P),
                                 allow_slow_non_contiguous=True).then_inc(w_in, 16)
                sp.dma_start(wg[:], w["L0_ffn_Wg"].rearrange("(m p) e -> p m e", p=P)).then_inc(w_in, 16)
                sp.dma_start(bg[:], w["L0_ffn_bg"].partition_broadcast(P)).then_inc(w_in, 16)
                for e in range(EX):
                    sp.dma_start(w2[:, :, e, :], w["L0_ffn_Wd"][e].rearrange("(m p) n -> p m n", p=P)).then_inc(w_in, 16)
                    sp.dma_start(b2[:, e, :], w["L0_ffn_bd"][e].partition_broadcast(P)).then_inc(w_in, 16)

            def load(g, s):
                after_dma(sp, stored, g - 2, GT)
                sp.dma_start(xg[:, s], group(x_in_dram, g)).then_inc(x_in[s], 16)

            def store(g, s):
                after(sp, x_done, g)
                for i in range(GT):
                    if second and isinstance(g, int) and (g * GT + i + 1) * P > N:
                        left = N - (g * GT + i) * P
                        if left > 0:
                            sp.dma_start(x_out_dram[N - left:N, :], xg[0:left, s, i, :]).then_inc(stored, 16)
                    else:
                        sp.dma_start(x_out_dram[bass.ds(g * GW + i * P, P), :], xg[:, s, i, :]).then_inc(stored, 16)
            skewed(sp, load, store, n=NG)
            short = (NP - N) // P if second else 0
            sp.wait_ge(stored, 16 * GT * (NG + PRIME) - 16 * short)

        BG = 2 + YS if sort else 0
        breaks = (MH // 4, 3 * MH // 4)
        NEXT = 6
        rest = range(NG * BG, GatSort.blocks) if sort else ()

        def slot(g, n):
            return g * BG + n, n % 2

        def groups(body):
            def run(eng):
                with eng.Fori(0, NG // 2 - 1) as j:
                    body(2 * j, 0, True)
                    body(2 * j + 1, 1, True)
                body(NG - 2, 0, True)
                body(NG - 1, 1, False)
            return run

        @block.gpsimd
        def _(pool):
            def power(g):
                after(pool, var_ready, g)
                pool.tensor_tensor(rstd[:], ve[:], k.neghalf[:].to_broadcast([P, GT]), ALU.pow).then_inc(rstd_ready, 1)

            def body(g, s, more):
                for n in range(BG):
                    if n == 2 + NEXT and more:
                        power(g + 1)
                    sort.pool_step(pool, *slot(g, n))
                if not sort and more:
                    power(g + 1)
            if not second:
                pool.tensor_scalar(im[:], k.iota[:, 0:EX], float(-EX), None, ALU.add).then_inc(im_done, 1)
            power(0)
            if sort:
                sort.pool_start(pool)
            groups(body)(pool)
            for b in rest:
                sort.pool_step(pool, b, b % 2)
            if sort:
                sort.pool_end(pool)

        @block.vector
        def _(dve):
            ln = Chain(dve, ln_step, 2)
            rt = Chain(dve, rt_step, 9)
            yc = Chain(dve, y_step, GT * (2 * EX - 2))
            dve.wait_ge(w_in, 16 * (16 if second else 20))
            if not second:
                dve.wait_ge(im_done, 1)

            def bcast(ap):
                return ap.unsqueeze(2).to_broadcast([P, GT, EX])

            def norm(g, s):
                ln.start(g)
                loaded(dve, x_in[s], g, s)
                for i in range(GT):
                    last = dve.bn_stats(st[:, i, :], xg[:, s, i, :])
                ln(last)
                for i in range(GT):
                    last = dve.bn_aggr(mv[:, i, :], st[:, i, :])
                ln(last)
                ln.end()
                dve.tensor_scalar(ve[:], mv[:, :, 1], LN_EPS, None, ALU.add).then_inc(var_ready, 1)
                after_step(dve, tp_done, g, TR, -1)
                after(dve, rstd_ready, g)
                for i in range(GT):
                    last = dve.tensor_scalar(xn[:, i, :], xg[:, s, i, :], mv[:, i, 0:1], rstd[:, i:i + 1],
                                             ALU.subtract, ALU.mult)
                last.then_inc(xn_done, 1)
                after(dve, xn_done, g)

            def route(g, s):
                if second:
                    dve.tensor_copy(gate[:, s], k.gate[:, bass.ds(g * GT, GT), :]).then_inc(gate_done, 1)
                    after(dve, gate_done, g)
                    return
                rt.start(g)
                after(dve, lg_done, g)
                rt(dve.tensor_tensor(L[:], psL, bg[:].unsqueeze(1).to_broadcast([P, GT, EX]), ALU.add))
                rt(dve.tensor_reduce(mx[:], L[:], AX.X, ALU.max))
                dve.tensor_tensor(X8[:], L[:], bcast(mx[:]), ALU.subtract).then_inc(lx_done, 1)
                rt(dve.tensor_tensor(oh[:], L[:], bcast(mx[:]), ALU.is_equal))
                rt(dve.tensor_tensor(cand[:], oh[:], im[:].unsqueeze(1).to_broadcast([P, GT, EX]), ALU.mult))
                rt(dve.tensor_reduce(mn[:], cand[:], AX.X, ALU.min))
                rt(dve.tensor_tensor(oh[:], im[:].unsqueeze(1).to_broadcast([P, GT, EX]), bcast(mn[:]), ALU.is_equal))
                after(dve, le_done, g)
                rt(dve.tensor_reduce(sm[:], X8[:], AX.X, ALU.add))
                rt(dve.reciprocal(pr[:], sm[:]))
                rt(dve.tensor_tensor(gate[:, s], oh[:], bcast(pr[:]), ALU.mult))
                rt.end()

            def body(g, s, more):
                if sort:
                    for n in range(2):
                        sort.dve_step(dve, *slot(g, n))
                route(g, s)
                yc.start(g)
                for i in range(GT):
                    acc = xg[:, s, i, :]
                    for e in range(EX):
                        yc(dve.scalar_tensor_tensor(out=acc, in0=b2[:, e, :], scalar=gate[:, s, i, e:e + 1], in1=acc,
                                                    op0=ALU.mult, op1=ALU.add))
                    for h in range(2):
                        after_step(dve, y_done, g, YS, 2 * i + h)
                        for e in range(PH):
                            col = 512 * e if second else C * e
                            ins = dve.scalar_tensor_tensor(out=acc, in0=psY[:, h].rearrange("p b n -> p (b n)")[:, col:col + C],
                                                           scalar=gate[:, s, i, h * PH + e:h * PH + e + 1],
                                                           in1=acc, op0=ALU.mult, op1=ALU.add)
                            if e == PH - 1:
                                ins.then_inc(yc_done, 1)
                                after_step(dve, yc_done, g, YS, 2 * i + h)
                            else:
                                yc(ins)
                        if 2 * i + h == NEXT and more:
                            norm(g + 1, 1 - s)
                        if sort:
                            sort.dve_step(dve, *slot(g, 2 + 2 * i + h))
                yc.end()
                dve.engine_nop().then_inc(x_done, 1)
            norm(0, 0)
            if sort:
                sort.dve_start(dve)
            groups(body)(dve)
            for b in rest:
                sort.dve_step(dve, b, b % 2)

        @block.scalar
        def _(act):
            act.wait_ge(w_in, 16 * (16 if second else 20))

            def body(g, s, more):
                for r, (i0, n) in enumerate(rounds):
                    after_step(act, tp_done, g, TR, r)
                    if r == 0:
                        after_step(act, hp_done, g, HS, -1)
                    act.activation(xT[:, :, i0 * P:(i0 + n) * P].rearrange("p a (i n) -> p i a n", n=P), psT[:, 0:n], ACT.Copy)\
                        .then_inc(tc_done, 1)
                for m in range(MH):
                    if sort and m in breaks:
                        sort.act_step(act, *slot(g, breaks.index(m)))
                    for h in range(2):
                        after_step(act, hp_done, g, HS, 2 * m + h)
                        act.activation(H[:, m, h * HALF:(h + 1) * HALF], psH[:, h, 0:HALF], ACT.Gelu,
                                       bias=b1[:, m:m + 1]).then_inc(h_done, 1)
                if not second:
                    after(act, lx_done, g)
                    act.activation(X8[:], X8[:], ACT.Exp).then_inc(le_done, 1)
                for n in range(2, BG):
                    sort.act_step(act, *slot(g, n))
            if sort:
                sort.act_start(act)
            groups(body)(act)
            for b in rest:
                sort.act_step(act, b, b % 2)

        @block.tensor
        def _(pe):
            pe.wait_ge(w_in, 16 * (16 if second else 20))

            def body(g, s, more):
                after(pe, xn_done, g)
                for r, (i0, n) in enumerate(rounds):
                    after_step(pe, tc_done, g, TR, r - 1)
                    for i in range(n):
                        for a in range(KC):
                            last = pe.transpose(psT[:, i, a, :], xn[:, i0 + i, a * P:(a + 1) * P], k.ident[:])
                    last.then_inc(tp_done, 1)
                after_step(pe, tc_done, g, TR, TR - 1)
                for m in range(MH):
                    if sort and m in breaks:
                        sort.pe_step(pe, *slot(g, breaks.index(m)))
                    for h in range(2):
                        after_step(pe, h_done, g, HS, 2 * m + h - 2)
                        for a in range(KC):
                            last = pe.matmul(psH[:, h, 0:HALF], w1[:, a, m * P:(m + 1) * P], xT[:, a, h * HALF:(h + 1) * HALF],
                                             start=(a == 0), stop=(a == KC - 1))
                        last.then_inc(hp_done, 1)
                after_step(pe, h_done, g, HS, HS - 1)
                if not second:
                    after(pe, lx_done, g - 1)
                    for i in range(GT):
                        for m in range(MH):
                            last = pe.matmul(psL[:, i, :], H[:, m, i * P:(i + 1) * P], wg[:, m, :],
                                             start=(m == 0), stop=(m == MH - 1))
                    last.then_inc(lg_done, 1)
                for i in range(GT):
                    for h in range(2):
                        after_step(pe, yc_done, g, YS, 2 * i + h - 2)
                        for b in range(2):
                            if second:
                                e = 2 * h + b
                                for m in range(4):
                                    last = pe.matmul(psY[:, h, b, 0:C], H[:, 4 * e + m, i * P:(i + 1) * P],
                                                     w2[:, 4 * e + m, :], start=(m == 0), stop=(m == 3))
                            else:
                                e = 4 * h + 2 * b
                                for m in range(MH):
                                    last = pe.matmul(psY[:, h, b, :], H[:, m, i * P:(i + 1) * P],
                                                     w2[:, m, e:e + 2, :].rearrange("p e n -> p (e n)"),
                                                     start=(m == 0), stop=(m == MH - 1))
                        last.then_inc(y_done, 1)
                        if sort:
                            sort.pe_step(pe, *slot(g, 2 + 2 * i + h))
            if sort:
                sort.pe_start(pe)
            groups(body)(pe)
            for b in rest:
                sort.pe_step(pe, b, b % 2)


def normed_nodes(nc, k, w):
    CA = C + 1
    with ExitStack() as c:
        sb = lambda name, shape, dt=F32: c.enter_context(nc.sbuf_tensor("n_" + name, shape, dt))
        sem = semaphores(nc, c, before="n_")
        xt = sb("xt", [P, 2, GT, C])
        xn = sb("xn", [P, 2, GT, CA])
        xm = sb("xm", [P, 2, GT, CA])
        st, mv = sb("st", [P, GT, 6]), sb("mv", [P, GT, 2])
        ve, rstd = sb("ve", [P, GT]), sb("rstd", [P, GT])
        psG = [c.enter_context(nc.psum_tensor(f"n_psG{a}", [P, 512], F32)) for a in range(3)]
        x_in = [sem("x_in0"), sem("x_in1")]
        set_done, var_ready, rstd_ready, xn_done, xm_done, acc_done, stored, ln_step, fin = (sem(n) for n in (
            "set_done", "var_ready", "rstd_ready", "xn_done", "xm_done", "acc_done", "stored", "ln_step", "fin"))
        block = c.enter_context(nc.Block())

        @block.sync
        def _(sp):
            prime(sp, [var_ready, rstd_ready, xn_done, xm_done, acc_done], [(stored, 1)])

            def group(ap, g):
                return ap[bass.ds(g * GW, GW), :].rearrange("(i p) c -> p i c", p=P)

            def load(g, s):
                after(sp, xn_done, g - 2)
                sp.dma_start(xt[:, s], group(k.X2, g)).then_inc(x_in[s], 16)

            def store(g, s):
                after(sp, xn_done, g)
                after_dma(sp, stored, g - 1)
                sp.dma_start(group(k.XN2, g), xn[:, s, :, 0:C]).then_inc(stored, 16)
            two_ahead(sp, load, store, n=NG)
            after_dma(sp, stored, NG - 1)

        @block.gpsimd
        def _(pool):
            def power(g, s):
                after(pool, var_ready, g)
                pool.tensor_tensor(rstd[:], ve[:], k.neghalf[:].to_broadcast([P, GT]), ALU.pow).then_inc(rstd_ready, 1)
            ring(pool, power, n=NG)

        @block.vector
        def _(dve):
            ln = Chain(dve, ln_step, 2)
            dve.memset(xn[:, :, :, C:CA], 1.0).then_inc(set_done, 1)
            dve.wait_ge(set_done, 1)

            def body(g, s):
                ln.start(g)
                loaded(dve, x_in[s], g, s)
                for i in range(GT):
                    last = dve.bn_stats(st[:, i, :], xt[:, s, i, :])
                ln(last)
                for i in range(GT):
                    last = dve.bn_aggr(mv[:, i, :], st[:, i, :])
                ln(last)
                ln.end()
                dve.tensor_scalar(ve[:], mv[:, :, 1], LN_EPS, None, ALU.add).then_inc(var_ready, 1)
                after_dma(dve, stored, g - 2)
                after(dve, acc_done, g - 2)
                after(dve, rstd_ready, g)
                for i in range(GT):
                    last = dve.tensor_scalar(xn[:, s, i, 0:C], xt[:, s, i, :], mv[:, i, 0:1], rstd[:, i:i + 1],
                                             ALU.subtract, ALU.mult)
                last.then_inc(xn_done, 1)
                after(dve, xn_done, g)
                dve.tensor_tensor(xm[:, s], xn[:, s], k.valid[:, bass.ds(g * GT, GT)].unsqueeze(2).to_broadcast([P, GT, CA]),
                                  ALU.mult).then_inc(xm_done, 1)
            ring(dve, body, n=NG)
            after(dve, acc_done, NG - 1)
            dve.tensor_copy(k.gram[:, 0, :], psG[0][:, 0:CA])
            dve.tensor_copy(k.gram[:, 1, :], psG[1][:, 0:CA])
            dve.tensor_copy(k.gramr[:], psG[2][0:1, 0:CA]).then_inc(fin, 1)
            dve.wait_ge(fin, 1)

        @block.tensor
        def _(pe):
            pe.wait_ge(set_done, 1)
            for a in range(3):
                pe.matmul(psG[a][:, 0:P], k.zero1[:], k.ones[0:1, :], start=True, stop=True)
                pe.matmul(psG[a][:, P:2 * P], k.zero1[:], k.ones[0:1, :], start=True, stop=True)
                pe.matmul(psG[a][:, 2 * P:3 * P], k.zero1[:], k.ones[0:1, :], start=True, stop=True)

            def body(g, s):
                after(pe, xm_done, g)
                for i in range(GT):
                    for a in range(KC):
                        pe.matmul(psG[a][:, 0:CA], xm[:, s, i, a * P:(a + 1) * P], xn[:, s, i, :], start=False, stop=False,
                                  skip_group_check=True)
                    last = pe.matmul(psG[2][0:1, 0:CA], xm[:, s, i, C:CA], xn[:, s, i, :], start=False, stop=False,
                                     skip_group_check=True)
                last.then_inc(acc_done, 1)
            ring(pe, body, n=NG)


def fold_second_layer(nc, k, w):
    CA = C + 1
    with ExitStack() as c:
        sb = lambda name, shape, dt=F32: c.enter_context(nc.sbuf_tensor("g_" + name, shape, dt))
        sem = semaphores(nc, c, before="g_")
        raw = {n: sb("raw_" + n, [P, KC, C]) for n in ("Wq", "Wk", "Wv", "Wfc")}
        T = {n: sb("T_" + n, [P, KC, C]) for n in ("Wk", "Wv", "Wfc")}
        brow = sb("brow", [1, 2, C])
        bq = sb("bq", [P, KC])
        bsum = sb("bsum", [1, 2, C])
        wl, wr = sb("wl", [P, KC, C]), sb("wr", [P, KC, C])
        GK, gkr = sb("GK", [P, KC, C]), sb("gkr", [1, C])
        PT, M2 = sb("PT", [P, KC, C]), sb("M2", [P, KC, C])
        br = sb("br", [1, C])
        wg = sb("wg", [P, KC, 16])
        att = sb("att", [P, 2, 16])
        prod = sb("prod", [P, KC, 16])
        gi, pi = sb("gi", [P, C], I32), sb("pi", [P, KC], I32)
        gf, pf = sb("gf", [P, C]), sb("pf", [P, KC])
        ps = [c.enter_context(nc.psum_tensor(f"g_ps{a}", [P, KC, C], F32)) for a in range(3)]
        psr = c.enter_context(nc.psum_tensor("g_psr", [P, 512], F32))
        w_in, iota_done, step, turned, turned_sb, mm, mm_sb = (sem(n) for n in (
            "w_in", "iota_done", "step", "turned", "turned_sb", "mm", "mm_sb"))
        block = c.enter_context(nc.Block())
        n_loads = 4 + 2 + 1 + 2 + 3 + 1 + 2

        @block.sync
        def _(sp):
            for n in raw:
                sp.dma_start(raw[n][:], w["L1_mix_" + n].rearrange("(a p) n -> p a n", p=P)).then_inc(w_in, 16)
            sp.dma_start(brow[:, 0, :], row_of(w["L1_mix_bk"])).then_inc(w_in, 16)
            sp.dma_start(brow[:, 1, :], row_of(w["L1_mix_bv"])).then_inc(w_in, 16)
            sp.dma_start(bq[:], w["L1_mix_bq"].rearrange("(a p) -> p a", p=P),
                         allow_slow_non_contiguous=True).then_inc(w_in, 16)
            sp.dma_start(bsum[:, 0, :], row_of(w["L1_mix_bfc"])).then_inc(w_in, 16)
            sp.dma_start(bsum[:, 1, :], row_of(w["L1_gnn_b_left"])).then_inc(w_in, 16)
            sp.dma_start(wl[:], w["L1_gnn_W_left"][0:C, :].rearrange("(a p) n -> p a n", p=P)).then_inc(w_in, 16)
            sp.dma_start(k.WN[:], w["L1_gnn_W_left"][C:2 * C, :].rearrange("(a p) n -> p a n", p=P)).then_inc(w_in, 16)
            sp.dma_start(wr[:], w["L1_gnn_W_right"].rearrange("(a p) n -> p a n", p=P)).then_inc(w_in, 16)
            sp.dma_start(wg[:], w["L1_ffn_W_gat"].rearrange("(a p) n -> p a n", p=P)).then_inc(w_in, 16)
            for i, n in enumerate(("L1_ffn_att_src", "L1_ffn_att_dst")):
                sp.dma_start(att[:, i, :], w[n].rearrange("h e -> (h e)").partition_broadcast(P)).then_inc(w_in, 16)

        @block.gpsimd
        def _(pool):
            pool.iota(gi[:], [[1, C]], 0, 0).then_inc(iota_done, 1)
            pool.iota(pi[:], [[P, KC]], 0, 1).then_inc(iota_done, 1)

        @block.vector
        def _(dve):
            link = Chain(dve, step, None)
            link.start_once()
            dve.wait_ge(iota_done, 2)
            link(dve.tensor_scalar(gi[:], gi[:], 5, None, ALU.logical_shift_right))
            link(dve.tensor_scalar(pi[:], pi[:], 5, None, ALU.logical_shift_right))
            link(dve.tensor_copy(gf[:], gi[:]))
            link(dve.tensor_copy(pf[:], pi[:]))
            dve.wait_ge(w_in, 16 * n_loads)
            for a in range(KC):
                link(dve.tensor_copy(k.WG[:, a, 0:16].rearrange("p (e h) -> p e h", h=4),
                                     wg[:, a, :].rearrange("p (h e) -> p e h", e=4)))
            for i in range(2):
                link(dve.tensor_tensor(prod[:], wg[:], att[:, i, :].unsqueeze(1).to_broadcast([P, KC, 16]), ALU.mult))
                link(dve.tensor_reduce(k.WG[:, :, 16 + 4 * i:20 + 4 * i], prod[:].rearrange("p a (h e) -> p a h e", e=4), AX.X, ALU.add))
            for i, n in enumerate(T):
                dve.wait_ge(turned, i + 1)
                dve.tensor_copy(T[n][:], ps[i][:]).then_inc(turned_sb, 1)
            dve.wait_ge(mm, 1)
            dve.tensor_copy(GK[:], ps[0][:])
            dve.tensor_copy(gkr[:], psr[0:1, 0:C]).then_inc(mm_sb, 1)
            dve.wait_ge(mm, 2)
            for a in range(KC):
                link(dve.tensor_scalar(PT[:, a, :], gf[:], pf[:, a:a + 1], 1.0 / N, ALU.is_equal, ALU.mult))
            dve.tensor_tensor(PT[:], PT[:], ps[1][:], ALU.mult).then_inc(mm_sb, 1)
            dve.wait_ge(mm, 3)
            dve.tensor_copy(M2[:], ps[2][:]).then_inc(mm_sb, 1)
            link(dve.tensor_tensor(wl[:], wl[:], wr[:], ALU.add))
            link(dve.tensor_tensor(br[:], bsum[:, 0, :], bsum[:, 1, :], ALU.add))
            dve.wait_ge(mm, 4)
            link(dve.tensor_tensor(k.WS[:], wl[:], ps[0][:], ALU.add))
            dve.tensor_tensor(br[:], br[:], psr[0:1, 0:C], ALU.add).then_inc(mm_sb, 1)
            dve.wait_ge(mm, 5)
            link(dve.tensor_copy(k.bias2[:], ps[1][:, 0, :]))

        @block.tensor
        def _(pe):
            pe.wait_ge(w_in, 16 * n_loads)
            for i, n in enumerate(T):
                for a in range(KC):
                    for b in range(KC):
                        last = pe.transpose(ps[i][:, a, b * P:(b + 1) * P], raw[n][:, b, a * P:(a + 1) * P], k.ident[:])
                last.then_inc(turned, 1)
            pe.wait_ge(turned_sb, 3)
            parts = [(k.gram[:, 0, :], T["Wk"][:, 0, :]), (k.gram[:, 1, :], T["Wk"][:, 1, :]), (k.gramr[:], brow[:, 0, :])]
            for o in range(3):
                dst, cols = (ps[0][:, o, :], slice(o * P, (o + 1) * P)) if o < KC else (psr[0:1, 0:C], slice(C, CA))
                for i, (g, wk) in enumerate(parts):
                    last = pe.matmul(dst, g[:, cols], wk, start=(i == 0), stop=(i == 2))
            last.then_inc(mm, 1)
            pe.wait_ge(mm_sb, 1)
            parts = [(T["Wv"][:, 0, :], GK[:, 0, :]), (T["Wv"][:, 1, :], GK[:, 1, :]), (brow[:, 1, :], gkr[:])]
            for a in range(KC):
                for i, (v, gk) in enumerate(parts):
                    last = pe.matmul(ps[1][:, a, :], v[:, a * P:(a + 1) * P], gk, start=(i == 0), stop=(i == 2))
            last.then_inc(mm, 1)
            pe.wait_ge(mm_sb, 2)
            for a in range(KC):
                for b in range(KC):
                    last = pe.matmul(ps[2][:, a, :], PT[:, b, a * P:(a + 1) * P], T["Wfc"][:, b, :], start=(b == 0), stop=(b == KC - 1))
            last.then_inc(mm, 1)
            pe.wait_ge(mm_sb, 3)
            for a in range(KC):
                for b in range(KC):
                    pe.matmul(ps[0][:, a, :], raw["Wq"][:, b, a * P:(a + 1) * P], M2[:, b, :], start=(b == 0), stop=(b == KC - 1))
            for b in range(KC):
                last = pe.matmul(psr[0:1, 0:C], bq[:, b:b + 1], M2[:, b, :], start=(b == 0), stop=(b == KC - 1))
            last.then_inc(mm, 1)
            pe.wait_ge(mm_sb, 4)
            pe.matmul(ps[1][:, 0, :], k.ones[0:1, :], br[:], start=True, stop=True).then_inc(mm, 1)


SLE = 4


def edge_sums(nc, k):
    with ExitStack() as c:
        sb = lambda name, shape, dt=F32: c.enter_context(nc.sbuf_tensor("s_" + name, shape, dt))
        sem = semaphores(nc, c, before="s_")
        idx = sb("idx", [P, SLE, BLK], I32)
        x = sb("x", [P, SLE, BLK, C])
        same = sb("same", [P, BLK])
        carry = sb("carry", [P, C])
        idx_in = [sem(f"idx_in{s}") for s in range(SLE)]
        x_in = [sem(f"x_in{s}") for s in range(SLE)]
        stored = [sem(f"stored{s}") for s in range(SLE)]
        step, sums_done, set_done, carried = sem("step"), sem("sums_done"), sem("set_done"), sem("carried")
        lanes_in = sem("lanes_in")
        block = c.enter_context(nc.Block())
        ps = k.PS.rearrange("(p i) f -> p i f", i=LA)

        @block.sync
        def _(sp):
            prime(sp, [sums_done, carried])
            sp.dma_start(k.srci[:], k.SRCL).then_inc(lanes_in, 16)
            sp.dma_start(k.same[:], k.SAMEL).then_inc(lanes_in, 16)
            sp.wait_ge(lanes_in, 32)

            def fetch(b, s):
                after(sp, carried, b - SLE)
                sp.dma_start(idx[:, s, :], k.srci[:, bass.ds(b * BLK, BLK)]).then_inc(idx_in[s], 16)
            ring(sp, fetch, n=NBA, slots=SLE)

        @block.scalar
        def _(act):
            def store(b, s):
                after(act, sums_done, b)
                act.dma_start(ps[:, bass.ds(b * BLK, BLK), :], x[:, s]).then_inc(stored[s], 16)
            ring(act, store, n=NBA, slots=SLE)
            for s in range(SLE):
                act.wait_ge(stored[s], 16 * (NBA // SLE))

        @block.gpsimd
        def _(pool):
            def gather(b, s, free=True):
                loaded(pool, idx_in[s], b, s, slots=SLE)
                if free:
                    wait_reg(pool, stored[s], (b - s) * (16 // SLE))
                for j in range(BLK):
                    pool.indirect_dma_start(x[:, s, j, :], None, k.XN2,
                                            bass.IndirectOffsetOnAxis(ap=idx[:, s, j:j + 1], axis=0)).then_inc(x_in[s], 16)
            for s in range(SLE):
                gather(s, s, free=False)
            with pool.Fori(1, NBA // SLE) as i:
                for s in range(SLE):
                    gather(SLE * i + s, s)

        @block.vector
        def _(dve):
            ch = Chain(dve, step, BLK)
            dve.memset(carry[:], 0.0).then_inc(set_done, 1)
            dve.wait_ge(set_done, 1)
            dve.wait_ge(lanes_in, 32)

            def body(b, s):
                ch.start(b)
                ch(dve.tensor_copy(same[:], k.same[:, bass.ds(b * BLK, BLK)]))
                loaded(dve, x_in[s], b, s, per=BLK, slots=SLE)
                prev = carry[:]
                for j in range(BLK):
                    ins = dve.scalar_tensor_tensor(out=x[:, s, j, :], in0=prev, scalar=same[:, j:j + 1], in1=x[:, s, j, :],
                                                   op0=ALU.mult, op1=ALU.add)
                    prev = x[:, s, j, :]
                    if j < BLK - 1:
                        ch(ins)
                ins.then_inc(sums_done, 1)
                after(dve, sums_done, b)
                dve.tensor_copy(carry[:], prev).then_inc(carried, 1)
                after(dve, carried, b)
                ch.end()
            ring(dve, body, n=NBA, slots=SLE)


def second_layer_nodes(nc, k, w):
    with ExitStack() as c:
        sb = lambda name, shape, dt=F32: c.enter_context(nc.sbuf_tensor("m_" + name, shape, dt))
        sem = semaphores(nc, c, before="m_")
        idx = sb("idx", [P, 2, 2], I32)
        r = sb("r", [P, 2, 2, C])
        xn = sb("xn", [P, 2, C])
        x2 = sb("x2", [P, 2, C])
        rc = sb("rc", [P, NT])
        rsum, hn, xb, x3, x3n = sb("rsum", [P, C]), sb("hn", [P, C]), sb("xb", [P, C]), sb("x3", [P, C]), sb("x3n", [P, C])
        hT, yT = sb("hT", [P, 4, P]), sb("yT", [P, KC, P])
        st, mv, ve, rstd = sb("st", [P, 6]), sb("mv", [P, 2]), sb("ve", [P, 1]), sb("rstd", [P, 1])
        g = sb("g", [P, 24])
        psT = c.enter_context(nc.psum_tensor("m_psT", [P, 4, P], F32))
        psO = c.enter_context(nc.psum_tensor("m_psO", [P, 512], F32))
        psU = c.enter_context(nc.psum_tensor("m_psU", [P, KC, P], F32))
        psG = c.enter_context(nc.psum_tensor("m_psG", [P, 512], F32))
        x_in = [sem("x_in0"), sem("x_in1")]
        r_in = [sem("r_in0"), sem("r_in1")]
        names = ("idx_done", "hn_done", "xb_done", "ps_T", "sb_T", "ps_O", "x3_done", "var_ready", "rstd_ready", "xn_done",
                 "ps_U", "sb_U", "ps_G", "g_done")
        (idx_done, hn_done, xb_done, ps_T, sb_T, ps_O, x3_done, var_ready, rstd_ready, xn_done,
         ps_U, sb_U, ps_G, g_done) = tiles = [sem(n) for n in names]
        stored_x, stored_g, ln_step, step = sem("stored_x"), sem("stored_g"), sem("ln_step"), sem("step")
        rc_done = sem("rc_done")
        block = c.enter_context(nc.Block())

        @block.sync
        def _(sp):
            prime(sp, tiles, [(stored_x, 1), (stored_g, 1)])

            def load(t, s):
                after(sp, ps_T, t - 2)
                after(sp, xb_done, t - 2)
                sp.dma_start(xn[:, s, :], rows(k.XN2, t)).then_inc(x_in[s], 16)
                sp.dma_start(x2[:, s, :], rows(k.X2, t)).then_inc(x_in[s], 16)

            def store(t, s):
                after(sp, x3_done, t)
                sp.dma_start(rows(k.X3, t), x3[:]).then_inc(stored_x, 16)
                after(sp, g_done, t)
                sp.dma_start(rows(k.G, t), g[:]).then_inc(stored_g, 16)
            two_ahead(sp, load, store)
            after_dma(sp, stored_x, NT - 1)
            after_dma(sp, stored_g, NT - 1)

        @block.gpsimd
        def _(pool):
            def gather(t, s):
                after(pool, idx_done, t)
                after(pool, hn_done, t - 2)
                for i, tab in enumerate((k.PS, k.INS)):
                    pool.indirect_dma_start(r[:, s, i, :], None, tab,
                                            bass.IndirectOffsetOnAxis(ap=idx[:, s, i:i + 1], axis=0)).then_inc(r_in[s], 16)

            def power(t, s):
                after(pool, var_ready, t)
                pool.tensor_tensor(rstd[:], ve[:], k.neghalf[:], ALU.pow).then_inc(rstd_ready, 1)
            skewed(pool, gather, power)

        @block.vector
        def _(dve):
            ln = Chain(dve, ln_step, 2)
            ch = Chain(dve, step, 1)
            dve.tensor_scalar(rc[:], k.cnt[:], 1.0, None, ALU.max).then_inc(rc_done, 1)
            dve.wait_ge(rc_done, 1)
            dve.reciprocal(rc[:], rc[:]).then_inc(rc_done, 1)
            dve.wait_ge(rc_done, 2)

            def index(t, s):
                if not isinstance(t, int) or t >= 2:
                    loaded(dve, r_in[s], t - 2, s, per=2)
                dve.tensor_copy(idx[:, s, 0:1], k.pos_i[:, bass.ds(t, 1)])
                dve.tensor_copy(idx[:, s, 1:2], k.inc_i[:, bass.ds(t, 1)]).then_inc(idx_done, 1)

            def body(t, s):
                ch.start(t)
                ln.start(t)
                loaded(dve, r_in[s], t, s, per=2)
                ch(dve.tensor_tensor(rsum[:], r[:, s, 0, :], r[:, s, 1, :], ALU.add))
                after(dve, ps_T, t - 1)
                dve.tensor_scalar(hn[:], rsum[:], rc[:, bass.ds(t, 1)], None, ALU.mult).then_inc(hn_done, 1)
                loaded(dve, x_in[s], t, s, per=2)
                dve.tensor_tensor(xb[:], x2[:, s, :], k.bias2[:], ALU.add).then_inc(xb_done, 1)
                after(dve, xb_done, t)
                after(dve, ps_O, t)
                after_dma(dve, stored_x, t - 1)
                dve.tensor_tensor(x3[:], xb[:], psO[:, 0:C], ALU.add).then_inc(x3_done, 1)
                after(dve, x3_done, t)
                layernorm_dve(dve, ln, x3[:], x3n[:], st, mv, ve, rstd, var_ready, rstd_ready, xn_done, t,
                              lambda: after(dve, ps_U, t - 1))
                after(dve, ps_G, t)
                after_dma(dve, stored_g, t - 1)
                dve.tensor_copy(g[:], psG[:, 0:24]).then_inc(g_done, 1)
                ln.end()
                ch.end()
            index(0, 0)
            index(1, 1)
            body(0, 0)
            index(2, 0)
            body(1, 1)
            index(3, 1)
            with dve.Fori(1, NT // 2 - 1) as j:
                body(2 * j, 0)
                index(2 * j + 2, 0)
                body(2 * j + 1, 1)
                index(2 * j + 3, 1)
            body(NT - 2, 0)
            body(NT - 1, 1)

        @block.scalar
        def _(act):
            def body(t, s):
                after(act, ps_T, t)
                after(act, ps_O, t - 1)
                act.activation(hT[:], psT[:], ACT.Copy).then_inc(sb_T, 1)
                after(act, ps_U, t)
                after(act, ps_G, t - 1)
                act.activation(yT[:], psU[:], ACT.Copy).then_inc(sb_U, 1)
            ring(act, body)

        @block.tensor
        def _(pe):
            def body(t, s):
                loaded(pe, x_in[s], t, s, per=2)
                after(pe, sb_T, t - 1)
                for a in range(KC):
                    pe.transpose(psT[:, a, :], xn[:, s, a * P:(a + 1) * P], k.ident[:])
                after(pe, hn_done, t)
                for a in range(KC):
                    last = pe.transpose(psT[:, KC + a, :], hn[:, a * P:(a + 1) * P], k.ident[:])
                last.then_inc(ps_T, 1)
                after(pe, sb_T, t)
                after(pe, x3_done, t - 1)
                for a in range(4):
                    rhs = k.WS[:, a, :] if a < KC else k.WN[:, a - KC, :]
                    last = pe.matmul(psO[:, 0:C], hT[:, a, :], rhs, start=(a == 0), stop=(a == 3))
                last.then_inc(ps_O, 1)
                after(pe, xn_done, t)
                after(pe, sb_U, t - 1)
                for a in range(KC):
                    last = pe.transpose(psU[:, a, :], x3n[:, a * P:(a + 1) * P], k.ident[:])
                last.then_inc(ps_U, 1)
                after(pe, sb_U, t)
                after(pe, g_done, t - 1)
                for a in range(KC):
                    last = pe.matmul(psG[:, 0:24], yT[:, a, :], k.WG[:, a, :], start=(a == 0), stop=(a == KC - 1))
                last.then_inc(ps_G, 1)
            ring(pe, body)


def gat_edges(nc, k):
    GB = 16
    R = 24
    with ExitStack() as c:
        sb = lambda name, shape, dt=F32: c.enter_context(nc.sbuf_tensor("t_" + name, shape, dt))
        sem = semaphores(nc, c, before="t_")
        sd = sb("sd", [P, LG, 2], I32)
        g = sb("g", [P, LG, R])
        z = sb("z", [P, LG * HE])
        e = sb("e", [P, HE, LG])
        same, bias = sb("same", [P, LG]), sb("bias", [P, LG])
        gn = sb("gn", [P, NT, R])
        gr = sb("gr", [P, 2, GB, R])
        idx = sb("idx", [P, 2, GB], I32)
        first_f, first_i, g0 = sb("first_f", [P, 1]), sb("first_i", [P, 1], I32), sb("g0", [P, R])
        sd_in, gn_in, zeroed, zero_st, placed, z_in, first_done, g0_in, moved, idx_done, step, e_done, x_done, p_done, stored = (
            sem(n) for n in ("sd_in", "gn_in", "zeroed", "zero_st", "placed", "z_in", "first_done", "g0_in", "moved",
                             "idx_done", "step", "e_done", "x_done", "p_done", "stored"))
        g_in = [sem("g_in0"), sem("g_in1")]
        block = c.enter_context(nc.Block())
        nb = LG // GB
        pz = z[:].rearrange("p (h i) -> p h i", h=HE)

        @block.sync
        def _(sp):
            prime(sp, [moved, idx_done])
            sp.dma_start(sd[:], k.SD.rearrange("(p i) f -> p i f", i=LG)).then_inc(sd_in, 16)
            sp.dma_start(gn[:], k.G.rearrange("(t p) f -> p t f", p=P)).then_inc(gn_in, 16)
            sp.wait_ge(zeroed, 1)
            sp.dma_start(k.ZD.rearrange("(p i) f -> p (i f)", i=LG), z[:]).then_inc(zero_st, 16)
            sp.wait_ge(zero_st, 16)
            sp.wait_ge(placed, 16 * NT)
            sp.dma_start(z[:], k.ZD.rearrange("(p i) f -> p (i f)", i=LG)).then_inc(z_in, 16)
            sp.wait_ge(p_done, 1)
            sp.dma_start(k.PG.rearrange("(p i) f -> p i f", i=LG), g[:]).then_inc(stored, 16)
            sp.wait_ge(stored, 16)

        @block.gpsimd
        def _(pool):
            pool.memset(z[:], 0.0).then_inc(zeroed, 1)
            pool.wait_ge(gn_in, 16)
            pool.wait_ge(zero_st, 16)
            for t in range(NT):
                pool.indirect_dma_start(k.ZD, bass.IndirectOffsetOnAxis(ap=k.start2_i[:, t:t + 1], axis=0),
                                        gn[:, t, 20:24], None).then_inc(placed, 16)
            pool.wait_ge(first_done, 1)
            pool.indirect_dma_start(g0[:], None, k.G, bass.IndirectOffsetOnAxis(ap=first_i[:], axis=0)).then_inc(g0_in, 16)

            def gather(b, s):
                after(pool, idx_done, b)
                after(pool, moved, b - 2)
                for j in range(GB):
                    pool.indirect_dma_start(gr[:, s, j, :], None, k.G,
                                            bass.IndirectOffsetOnAxis(ap=idx[:, s, j:j + 1], axis=0)).then_inc(g_in[s], 16)
            ring(pool, gather, n=nb)

        @block.vector
        def _(dve):
            link = Chain(dve, step, None)
            link.start_once()
            dve.wait_ge(sd_in, 16)
            link(dve.tensor_copy(bias[:], sd[:, :, 1]))
            link(dve.tensor_copy(k.first2[:], bias[:, 0:1]))
            link(dve.tensor_copy(k.last2[:], bias[:, LG - 1:LG]))
            link(dve.memset(same[:, 0:1], 0.0))
            link(dve.tensor_tensor(same[:, 1:LG], bias[:, 1:LG], bias[:, 0:LG - 1], ALU.is_equal))
            link(dve.tensor_scalar(bias[:], same[:], -1.0, BIG, ALU.add, ALU.mult))
            link(dve.tensor_scalar(first_f[:], k.first2[:], float(NP - 1), None, ALU.min))
            dve.tensor_copy(first_i[:], first_f[:]).then_inc(first_done, 1)

            def index(b, s):
                dve.tensor_copy(idx[:, s, :], sd[:, bass.ds(b * GB, GB), 0]).then_inc(idx_done, 1)

            def move(b, s):
                loaded(dve, g_in[s], b, s, per=GB)
                dve.tensor_copy(g[:, bass.ds(b * GB, GB), :], gr[:, s]).then_inc(moved, 1)
            index(0, 0)
            index(1, 1)
            with dve.Fori(0, nb // 2 - 1) as j:
                move(2 * j, 0)
                index(2 * j + 2, 0)
                move(2 * j + 1, 1)
                index(2 * j + 3, 1)
            move(nb - 2, 0)
            move(nb - 1, 1)
            after(dve, moved, nb - 1)
            dve.wait_ge(z_in, 16)
            dve.wait_ge(g0_in, 16)
            zi = z[:].rearrange("p (i h) -> p i h", h=HE)
            link(dve.tensor_copy(zi[:, 0, :], g0[:, 20:24]))
            for h in range(HE):
                link(dve.tensor_tensor_scan(e[:, h, :], same[:], zi[:, :, h], 0.0, ALU.mult, ALU.add))
            link(dve.tensor_tensor(e[:], e[:], g[:, :, 16:20].rearrange("p i h -> p h i"), ALU.add))
            link(dve.scalar_tensor_tensor(out=e[:], in0=e[:], scalar=0.2, in1=e[:], op0=ALU.mult, op1=ALU.max))
            for h in range(HE):
                link(dve.tensor_tensor_scan(g[:, :, 20 + h], bias[:], e[:, h, :], -BIG, ALU.add, ALU.max))
            M = g[:, :, 20:24].rearrange("p i h -> p h i")
            link(dve.tensor_tensor(pz, e[:], M, ALU.subtract))
            link(dve.memset(e[:, :, 0:1], -BIG))
            link(dve.tensor_tensor(e[:, :, 1:LG], M[:, :, 0:LG - 1], M[:, :, 1:LG], ALU.subtract))
            dve.tensor_tensor(e[:, :, 1:LG], e[:, :, 1:LG], bias[:, 1:LG].unsqueeze(1).to_broadcast([P, HE, LG - 1]), ALU.add)\
                .then_inc(e_done, 1)
            dve.wait_ge(x_done, 2)
            for x in range(HE):
                cols = g[:, :, x * HE:(x + 1) * HE].rearrange("p i h -> p h i")
                link(dve.tensor_tensor(cols, cols, pz, ALU.mult))
            for h in range(HE):
                for col in [x * HE + h for x in range(HE)]:
                    link(dve.tensor_tensor_scan(g[:, :, col], e[:, h, :], g[:, :, col], 0.0, ALU.mult, ALU.add))
                last = dve.tensor_tensor_scan(g[:, :, 16 + h], e[:, h, :], pz[:, h, :], 0.0, ALU.mult, ALU.add)
                if h < HE - 1:
                    link(last)
            last.then_inc(p_done, 1)

        @block.scalar
        def _(act):
            act.wait_ge(e_done, 1)
            act.activation(pz, pz, ACT.Exp).then_inc(x_done, 1)
            act.activation(e[:], e[:], ACT.Exp).then_inc(x_done, 1)


def gat_gates(nc, k, w):
    R = 24
    with ExitStack() as c:
        sb = lambda name, shape, dt=F32: c.enter_context(nc.sbuf_tensor("h_" + name, shape, dt))
        sem = semaphores(nc, c, before="h_")
        r = sb("r", [P, 2, NT, R])
        Mx = sb("Mx", [P, NT, HE])
        D = sb("D", [P, 2, NT, HE])
        T = sb("T", [P, 2, NT, 5 * HE])
        rz = sb("rz", [P, NT, HE])
        A, B = sb("A", [P, NT, 16]), sb("B", [P, NT, 16])
        vec, vecp = sb("vec", [P, 3, 16]), sb("vecp", [P, 3, 16])
        mean, var, rstd = sb("mean", [P, NT]), sb("var", [P, NT]), sb("rstd", [P, NT])
        s4, oh1, oh2, cand = sb("s4", [P, NT, HE]), sb("oh1", [P, NT, HE]), sb("oh2", [P, NT, HE]), sb("cand", [P, NT, HE])
        m1, m2, mn, ex, w1, w2 = (sb(n, [P, NT]) for n in ("m1", "m2", "mn", "ex", "w1", "w2"))
        im = sb("im", [P, HE])
        v_in, r_in, step, d_done, d_exp, var_done, rstd_done, x_done, x_exp = (sem(n) for n in (
            "v_in", "r_in", "step", "d_done", "d_exp", "var_done", "rstd_done", "x_done", "x_exp"))
        block = c.enter_context(nc.Block())

        @block.sync
        def _(sp):
            for i, n in enumerate(("L1_ffn_b_gat", "L1_ffn_ln_gamma", "L1_ffn_ln_beta")):
                sp.dma_start(vec[:, i, :], w[n].partition_broadcast(P)).then_inc(v_in, 16)

        @block.gpsimd
        def _(pool):
            for t in range(NT):
                for i, (tab, ix) in enumerate(((k.PG, k.pos2_i), (k.ING, k.inc2_i))):
                    pool.indirect_dma_start(r[:, i, t, :], None, tab,
                                            bass.IndirectOffsetOnAxis(ap=ix[:, t:t + 1], axis=0)).then_inc(r_in, 16)
            pool.wait_ge(var_done, 1)
            pool.tensor_tensor(rstd[:], var[:], k.neghalf[:].to_broadcast([P, NT]), ALU.pow).then_inc(rstd_done, 1)

        @block.scalar
        def _(act):
            act.wait_ge(d_done, 1)
            act.activation(D[:], D[:], ACT.Exp).then_inc(d_exp, 1)
            act.wait_ge(x_done, 1)
            act.activation(ex[:], ex[:], ACT.Exp).then_inc(x_exp, 1)

        @block.vector
        def _(dve):
            link = Chain(dve, step, None)
            link.start_once()
            dve.wait_ge(v_in, 48)
            link(dve.tensor_copy(vecp[:].rearrange("p v (e h) -> p v e h", h=HE), vec[:].rearrange("p v (h e) -> p v e h", e=HE)))
            link(dve.tensor_scalar(im[:], k.iota[:, 0:HE], float(-HE), None, ALU.add))
            dve.wait_ge(r_in, 16 * 2 * NT)
            m = r[:, :, :, 20:24]
            link(dve.tensor_tensor(Mx[:], m[:, 0], m[:, 1], ALU.max))
            link(dve.tensor_tensor(D[:, 0], m[:, 0], Mx[:], ALU.subtract))
            dve.tensor_tensor(D[:, 1], m[:, 1], Mx[:], ALU.subtract).then_inc(d_done, 1)
            dve.wait_ge(d_exp, 1)
            for i in range(2):
                link(dve.tensor_tensor(T[:, i].rearrange("p t (d h) -> p t d h", h=HE),
                                       r[:, i, :, 0:20].rearrange("p t (d h) -> p t d h", h=HE),
                                       D[:, i].unsqueeze(2).to_broadcast([P, NT, 5, HE]), ALU.mult))
            link(dve.tensor_tensor(T[:, 0], T[:, 0], T[:, 1], ALU.add))
            link(dve.tensor_scalar(rz[:], T[:, 0, :, 16:20], 1e-16, None, ALU.add))
            link(dve.reciprocal(rz[:], rz[:]))
            link(dve.tensor_tensor(A[:].rearrange("p t (e h) -> p t e h", h=HE),
                                   T[:, 0, :, 0:16].rearrange("p t (e h) -> p t e h", h=HE),
                                   rz[:].unsqueeze(2).to_broadcast([P, NT, HE, HE]), ALU.mult))

            def vector(i):
                return vecp[:, i, :].unsqueeze(1).to_broadcast([P, NT, 16])

            def over(ap, n):
                return ap.unsqueeze(2).to_broadcast([P, NT, n])
            link(dve.tensor_tensor(A[:], A[:], vector(0), ALU.add))
            link(dve.tensor_reduce(mean[:], A[:], AX.X, ALU.add))
            link(dve.tensor_scalar(mean[:], mean[:], 1.0 / 16, None, ALU.mult))
            link(dve.tensor_tensor(A[:], A[:], over(mean[:], 16), ALU.subtract))
            link(dve.tensor_tensor(B[:], A[:], A[:], ALU.mult))
            link(dve.tensor_reduce(var[:], B[:], AX.X, ALU.add))
            dve.tensor_scalar(var[:], var[:], 1.0 / 16, LN_EPS, ALU.mult, ALU.add).then_inc(var_done, 1)
            dve.wait_ge(rstd_done, 1)
            link(dve.tensor_tensor(A[:], A[:], over(rstd[:], 16), ALU.mult))
            link(dve.tensor_tensor(A[:], A[:], vector(1), ALU.mult))
            link(dve.tensor_tensor(A[:], A[:], vector(2), ALU.add))
            link(dve.tensor_reduce(s4[:], A[:].rearrange("p t (e h) -> p t e h", h=HE), AX.X, ALU.add))
            link(dve.tensor_scalar(s4[:], s4[:], 1.0 / HE, None, ALU.mult))

            def best(mx, oh):
                imb = im[:].unsqueeze(1).to_broadcast([P, NT, HE])
                link(dve.tensor_reduce(mx[:], s4[:], AX.X, ALU.max))
                link(dve.tensor_tensor(cand[:], s4[:], over(mx[:], HE), ALU.is_equal))
                link(dve.tensor_tensor(cand[:], cand[:], imb, ALU.mult))
                link(dve.tensor_reduce(mn[:], cand[:], AX.X, ALU.min))
                link(dve.tensor_tensor(oh[:], imb, over(mn[:], HE), ALU.is_equal))
            best(m1, oh1)
            link(dve.scalar_tensor_tensor(out=s4[:], in0=oh1[:], scalar=-BIG, in1=s4[:], op0=ALU.mult, op1=ALU.add))
            best(m2, oh2)
            dve.tensor_tensor(ex[:], m2[:], m1[:], ALU.subtract).then_inc(x_done, 1)
            dve.wait_ge(x_exp, 1)
            link(dve.tensor_scalar(w1[:], ex[:], 1.0, None, ALU.add))
            link(dve.reciprocal(w1[:], w1[:]))
            link(dve.tensor_tensor(w2[:], ex[:], w1[:], ALU.mult))
            link(dve.tensor_tensor(oh1[:], oh1[:], over(w1[:], HE), ALU.mult))
            link(dve.tensor_tensor(oh2[:], oh2[:], over(w2[:], HE), ALU.mult))
            link(dve.tensor_tensor(k.gate[:], oh1[:], oh2[:], ALU.add))


def program(nc, w, out, scratch):
    k = Core()
    with ExitStack() as c:
        sb = lambda name, shape, dt=F32: c.enter_context(nc.sbuf_tensor(name, shape, dt))
        k.ident, k.ones = sb("ident", [P, P]), sb("ones", [P, P])
        k.low, k.upper = sb("low", [P, P]), sb("upper", [P, P])
        k.neghalf, k.half = sb("neghalf", [P, 1]), sb("half", [P, 1])
        k.valid, k.nodef = sb("valid", [P, NT]), sb("nodef", [P, NT])
        k.iota, k.part = sb("iota", [P, P]), sb("part", [P, 1])
        k.zero1 = k.low[0:1, :]
        k.M1 = sb("M1", [P, KC, C])
        k.XP = scratch("XP", [NP, C])
        k.Q, k.KV, k.MV = scratch("Q", [NP, C]), scratch("KV", [NP, 2 * C]), scratch("MV", [NP, 2 * C])
        k.X1M, k.X1 = scratch("X1M", [NP, C]), scratch("X1", [NP, C])
        WA = (DK + 2) * HEADS
        k.PT, k.INC = scratch("PT", [P * LA, WA]), scratch("INC", [P + 1, WA])
        k.SRCL, k.SAMEL = scratch("SRCL", [P, LA], I32), scratch("SAMEL", [P, LA])
        k.first, k.last = sb("first", [P, 1]), sb("last", [P, 1])
        k.cnt, k.start = sb("cnt", [P, NT]), sb("start", [P, NT])
        k.pos_i, k.inc_i = sb("pos_i", [P, NT], I32), sb("inc_i", [P, NT], I32)
        k.X2, k.XN2, k.X3 = scratch("X2", [NP, C]), scratch("XN2", [NP, C]), scratch("X3", [NP, C])
        k.PS, k.INS = scratch("PS", [P * LA, C]), scratch("INS", [P + 1, C])
        k.G = scratch("G", [NP, 24])
        k.gram, k.gramr = sb("gram", [P, KC, C + 1]), sb("gramr", [1, C + 1])
        k.WS, k.WN, k.WG = sb("WS", [P, KC, C]), sb("WN", [P, KC, C]), sb("WG", [P, KC, 24])
        k.bias2 = sb("bias2", [P, C])
        k.cnt2, k.start2 = sb("cnt2", [P, HG]), sb("start2", [P, HG])
        k.start2_i, k.pos2_i, k.inc2_i = (sb(n, [P, HG], I32) for n in ("start2_i", "pos2_i", "inc2_i"))
        k.first2, k.last2 = sb("first2", [P, 1]), sb("last2", [P, 1])
        k.gate = sb("kgate", [P, NT, HE])
        k.SD, k.ZD = scratch("SD", [P * LG, 2], I32), scratch("ZD", [P * LG, HE])
        k.PG, k.ING = scratch("PG", [P * LG, 24]), scratch("ING", [P + 1, 24])
        constants(nc, k, w["x"])
        with ExitStack() as ca:
            lane = lambda name, dt: ca.enter_context(nc.sbuf_tensor(name, [P, LA], dt))
            k.srci, k.dsti, k.same = lane("srci", I32), lane("dsti", I32), lane("same", F32)
            project_nodes(nc, k, w)
            rank_nodes(nc, k, k.cnt[:], NT, LA, k.start[:], k.pos_i[:], k.inc_i[:], "_a")
            edge_attention(nc, k, w)
            join_lanes(nc, k, k.PT, LA, k.last[:, 0:1], k.first[:, 0:1], HEADS, DK + 1, float(DK) ** -0.5, k.INC, "_a")
        with ExitStack() as cg:
            k.pair = cg.enter_context(nc.sbuf_tensor("pair", [P, TG, 2], I32))
            k.lo, k.hi, k.dcol = (cg.enter_context(nc.sbuf_tensor(n, [P, TG], F32)) for n in ("glo", "ghi", "dcol"))
            attention_output(nc, k, w)
            rank_nodes(nc, k, k.cnt2[:], HG, LG, k.start2[:], k.pos2_i[:], k.inc2_i[:], "_g")
            routed_ffn(nc, k, w, False, k.X1, k.X2)
        with ExitStack() as ca:
            lane = lambda name, dt: ca.enter_context(nc.sbuf_tensor(name, [P, LA], dt))
            k.srci, k.same = lane("srci2", I32), lane("same2", F32)
            normed_nodes(nc, k, w)
            fold_second_layer(nc, k, w)
            edge_sums(nc, k)
            join_lanes(nc, k, k.PS, LA, k.last[:, 0:1], k.first[:, 0:1], 0, C, 1.0, k.INS, "_s")
            second_layer_nodes(nc, k, w)
        gat_edges(nc, k)
        join_lanes(nc, k, k.PG, LG, k.last2[:, 0:1], k.first2[:, 0:1], HE, 5, 1.0, k.ING, "_g")
        gat_gates(nc, k, w)
        routed_ffn(nc, k, w, True, k.X3, out)


_OUTS = [((N, C), "float32")]


def kernel(**inputs):
    import numpy as _np
    import concourse.bacc as _bacc
    from concourse import mybir as _mybir
    from concourse.bass_utils import run_bass_kernel_spmd as _run

    nc = _bacc.Bacc("TRN2", target_bir_lowering=False, num_devices=1)
    arrays, args = {}, {}
    for name in inputs:
        a = _np.ascontiguousarray(inputs[name])
        arrays[f"in_{name}_dram"] = a
        args[name] = nc.dram_tensor(f"in_{name}_dram", a.shape, _mybir.dt.from_np(a.dtype), kind="ExternalInput").ap()
    out = nc.dram_tensor("out_0_dram", (N, C), _mybir.dt.float32, kind="ExternalOutput").ap()

    def scratch(name, shape, dt=_mybir.dt.float32):
        return nc.dram_tensor(name, shape, dt, kind="Internal").ap()

    program(nc, args, out, scratch)
    r = _run(nc, [arrays], core_ids=[0])
    return r.results[0]["out_0_dram"]
```
